# Optimizing a Trainium2 kernel written in Bass

```python
import numpy as np
import jax
import jax.numpy as jnp

def _softmax(x, axis=-1):
    return jax.nn.softmax(x, axis=axis)

def _gelu(x):
    return jax.nn.gelu(x, approximate=True)

def _silu(x):
    return jax.nn.silu(x)

def _sigmoid(x):
    return jax.nn.sigmoid(x)

def _layernorm(x, axis=-1, eps=1e-05):
    m = jnp.mean(x, axis=axis, keepdims=True)
    v = jnp.var(x, axis=axis, keepdims=True)
    return (x - m) / jnp.sqrt(v + eps)

def _scatter_add(tgt, idx, src, axis=0):
    return tgt.at[idx].add(src)

def _segment_sum(src, seg, n):
    return jax.ops.segment_sum(src, seg, n)
kernel_name = 'mk_decoder_preln_d4_seqx_r4_893426'

def setup_inputs(seed: int=0):
    np.random.seed(seed)
    _w = jnp.asarray

    def _rec_inputs():
        import jax
        import jax.numpy as jnp
        _rk = jax.random.key(seed)
        x = -0.0003929 + 0.9999 * jax.random.normal(jax.random.fold_in(_rk, 1), (8, 100, 256), jnp.float32)
        _lenS = 100 - jax.random.randint(jax.random.fold_in(_rk, 7), (8,), 0, max(1, 100 // 4) + 1, jnp.int32)
        _lenS2 = 361 - jax.random.randint(jax.random.fold_in(_rk, 8), (8,), 0, max(1, 361 // 4) + 1, jnp.int32)
        _ctx_512P = jax.random.normal(jax.random.fold_in(_rk, 11), (8, 16, 128), jnp.float32)
        _ctx_512c = jax.random.dirichlet(jax.random.fold_in(_rk, 511), 0.3 * jnp.ones((16,), jnp.float32), (8, 361))
        _ctx_512t = jnp.einsum('bsk,bkd->bsd', _ctx_512c, _ctx_512P)
        _ctx_512t = _ctx_512t * jax.lax.rsqrt(jnp.mean(jnp.square(_ctx_512t)) + 1e-12) * 0.953939
        ctx_512 = 4.13588e-05 + 0.999923 * (_ctx_512t + 0.3 * jax.random.normal(jax.random.fold_in(_rk, 611), (8, 361, 128), jnp.float32))
        return (x, ctx_512)
    x, ctx_512 = _rec_inputs()

    def _L0_attn_setup():
        import jax, jax.numpy as jnp
        import numpy as np
        D_MODEL = 256
        N_HEADS = 16
        D_HIDDEN = 1024
        BATCH = 2
        N_CTX = 512

        def _split_heads(t, n_heads):
            B, S, D = t.shape
            return t.reshape(B, S, n_heads, D // n_heads).transpose(0, 2, 1, 3)
        key = jax.random.key(seed)
        ks = jax.random.split(key, 4)
        scale = 0.02
        x = jax.random.normal(ks[0], (BATCH, N_CTX, D_MODEL), dtype=jnp.float32)
        Wk = jax.random.normal(ks[1], (D_MODEL, D_MODEL), dtype=jnp.float32) * scale
        bk = jnp.zeros((D_MODEL,), dtype=jnp.float32)
        Wv = jax.random.normal(ks[2], (D_MODEL, D_HIDDEN), dtype=jnp.float32) * scale
        bv = jnp.zeros((D_HIDDEN,), dtype=jnp.float32)
        Wf = jax.random.normal(ks[3], (D_HIDDEN, D_MODEL), dtype=jnp.float32) * scale
        bf = jnp.zeros((D_MODEL,), dtype=jnp.float32)
        return {'x': x, 'Wk': Wk, 'bk': bk, 'Wv': Wv, 'bv': bv, 'Wf': Wf, 'bf': bf}
    _L0_attn_all = _L0_attn_setup()
    _L0_attn_in = {k: v for k, v in _L0_attn_all.items() if k in ('Wk', 'bk', 'Wv', 'bv', 'Wf', 'bf')}
    del _L0_attn_all

    def _L0_xattn_setup():
        import jax, jax.numpy as jnp
        import numpy as np
        B, LQ, LK = (8, 512, 512)
        QD, KD, VD = (256, 128, 128)
        key = jax.random.key(seed)
        ks = jax.random.split(key, 9)
        s = 0.02
        return {'query': jax.random.normal(ks[0], (B, LQ, QD), jnp.float32), 'key': jax.random.normal(ks[1], (B, LK, KD), jnp.float32), 'value': jax.random.normal(ks[2], (B, LK, VD), jnp.float32), 'Wq': jax.random.normal(ks[3], (QD, QD), jnp.float32) * s, 'bq': jnp.zeros((QD,), jnp.float32), 'Wk': jax.random.normal(ks[4], (KD, QD), jnp.float32) * s, 'bk': jnp.zeros((QD,), jnp.float32), 'Wv': jax.random.normal(ks[5], (VD, QD), jnp.float32) * s, 'bv': jnp.zeros((QD,), jnp.float32)}
    _L0_xattn_all = _L0_xattn_setup()
    _L0_xattn_in = {k: v for k, v in _L0_xattn_all.items() if k in ('Wq', 'bq', 'Wk', 'bk', 'Wv', 'bv')}
    del _L0_xattn_all

    def _L0_ffn_setup():
        import jax, jax.numpy as jnp
        import numpy as np
        B, S, D, E, K = (4, 256, 256, 8, 2)
        key = jax.random.key(seed)
        ks = jax.random.split(key, 7)
        scale = 1.0 / np.sqrt(D)
        return {'x': jax.random.normal(ks[0], (B, S, D), dtype=jnp.float32), 'W_shared': jax.random.normal(ks[1], (D, D), dtype=jnp.float32) * scale, 'b_shared': jax.random.normal(ks[2], (D,), dtype=jnp.float32) * scale, 'W_experts': jax.random.normal(ks[3], (E, D, D), dtype=jnp.float32) * scale, 'b_experts': jax.random.normal(ks[4], (E, D), dtype=jnp.float32) * scale, 'W_router': jax.random.normal(ks[5], (E, D), dtype=jnp.float32) * scale, 'b_router': jax.random.normal(ks[6], (E,), dtype=jnp.float32) * scale}
    _L0_ffn_all = _L0_ffn_setup()
    _L0_ffn_in = {k: v for k, v in _L0_ffn_all.items() if k in ('W_shared', 'b_shared', 'W_experts', 'b_experts', 'W_router', 'b_router')}
    del _L0_ffn_all

    def _L1_attn_setup():
        import jax, jax.numpy as jnp
        import numpy as np
        N_HEAD = 16
        HEAD_SIZE = 256
        EMBED = 256
        MULTI_HEAD_SIZE = HEAD_SIZE // N_HEAD
        B, S = (4, 512)
        key = jax.random.key(seed)
        k1, k2, k3, k4 = jax.random.split(key, 4)
        x = jax.random.normal(k1, (B, S, EMBED), dtype=jnp.float32)
        w_qkv = jax.random.normal(k2, (3 * HEAD_SIZE, EMBED), dtype=jnp.float32) * 0.02
        w_proj = jax.random.normal(k3, (EMBED, HEAD_SIZE), dtype=jnp.float32) * 0.02
        b_proj = jax.random.normal(k4, (EMBED,), dtype=jnp.float32) * 0.02
        return {'x': x, 'w_qkv': w_qkv, 'w_proj': w_proj, 'b_proj': b_proj}
    _L1_attn_all = _L1_attn_setup()
    _L1_attn_in = {k: v for k, v in _L1_attn_all.items() if k in ('w_qkv', 'w_proj', 'b_proj')}
    del _L1_attn_all

    def _L1_xattn_setup():
        import jax, jax.numpy as jnp
        import numpy as np
        HEADS = 16
        D_MODEL = 256
        IMG_MODEL = 128
        D_K = D_MODEL // HEADS
        key = jax.random.key(seed)
        ks = jax.random.split(key, 12)
        B, LQ, LKV = (8, 512, 256)
        s_dm = 1.0 / np.sqrt(D_MODEL)
        s_im = 1.0 / np.sqrt(IMG_MODEL)
        return {'q': jax.random.normal(ks[0], (B, LQ, D_MODEL), jnp.float32), 'k': jax.random.normal(ks[1], (B, LKV, IMG_MODEL), jnp.float32), 'v': jax.random.normal(ks[2], (B, LKV, IMG_MODEL), jnp.float32), 'Wq': jax.random.normal(ks[3], (D_MODEL, D_MODEL), jnp.float32) * s_dm, 'bq': jnp.zeros((D_MODEL,), jnp.float32), 'Wk': jax.random.normal(ks[4], (IMG_MODEL, D_MODEL), jnp.float32) * s_im, 'bk': jnp.zeros((D_MODEL,), jnp.float32), 'Wv': jax.random.normal(ks[5], (IMG_MODEL, D_MODEL), jnp.float32) * s_im, 'bv': jnp.zeros((D_MODEL,), jnp.float32), 'Wo': jax.random.normal(ks[6], (D_MODEL, D_MODEL), jnp.float32) * s_dm, 'bo': jnp.zeros((D_MODEL,), jnp.float32)}
    _L1_xattn_all = _L1_xattn_setup()
    _L1_xattn_in = {k: v for k, v in _L1_xattn_all.items() if k in ('Wq', 'bq', 'Wk', 'bk', 'Wv', 'bv', 'Wo', 'bo')}
    del _L1_xattn_all

    def _L1_ffn_setup():
        import jax, jax.numpy as jnp
        import numpy as np
        D = 256
        F = 4 * D
        E = 8
        NS = 2
        TOP_K = 2
        B, S = (2, 256)
        key = jax.random.key(seed)
        ks = jax.random.split(key, 7)
        w = 1.0 / np.sqrt(D)
        wf = 1.0 / np.sqrt(F)
        return {'x': jax.random.normal(ks[0], (B, S, D), jnp.float32), 'centroids': jax.random.normal(ks[1], (E, D), jnp.float32) * w, 'routing_bias': jnp.zeros((E,), jnp.float32), 'Wfc_r': jax.random.normal(ks[2], (E, F, D), jnp.float32) * w, 'Wproj_r': jax.random.normal(ks[3], (E, D, F), jnp.float32) * wf, 'Wfc_sh': jax.random.normal(ks[4], (NS, F, D), jnp.float32) * w, 'Wproj_sh': jax.random.normal(ks[5], (NS, D, F), jnp.float32) * wf}
    _L1_ffn_all = _L1_ffn_setup()
    _L1_ffn_in = {k: v for k, v in _L1_ffn_all.items() if k in ('centroids', 'routing_bias', 'Wfc_r', 'Wproj_r', 'Wfc_sh', 'Wproj_sh')}
    del _L1_ffn_all

    def _L2_attn_setup():
        import jax, jax.numpy as jnp
        import numpy as np
        B, T, D, H = (4, 512, 256, 16)
        HD = D // H
        key = jax.random.key(seed)
        k1, k2, k3 = jax.random.split(key, 3)
        x = jax.random.normal(k1, (B, T, D), dtype=jnp.float32)
        w_qkv = jax.random.normal(k2, (D, 3 * D), dtype=jnp.float32) * D ** (-0.5)
        b_qkv = jnp.zeros((3 * D,), dtype=jnp.float32)
        w_proj = jax.random.normal(k3, (D, D), dtype=jnp.float32) * D ** (-0.5)
        b_proj = jnp.zeros((D,), dtype=jnp.float32)
        return {'x': x, 'w_qkv': w_qkv, 'b_qkv': b_qkv, 'w_proj': w_proj, 'b_proj': b_proj}
    _L2_attn_all = _L2_attn_setup()
    _L2_attn_in = {k: v for k, v in _L2_attn_all.items() if k in ('w_qkv', 'b_qkv', 'w_proj', 'b_proj')}
    del _L2_attn_all

    def _L2_xattn_setup():
        import jax, jax.numpy as jnp
        import numpy as np
        NUM_HEADS = 16
        HEAD_DIM = 64
        Q_DIM = 256
        KV_DIM = 128
        INNER = NUM_HEADS * HEAD_DIM
        key = jax.random.key(seed)
        ks = jax.random.split(key, 7)
        B, N, M = (32, 128, 512)
        q = jax.random.normal(ks[0], (B, N, Q_DIM), dtype=jnp.float32)
        kv = jax.random.normal(ks[1], (B, M, KV_DIM), dtype=jnp.float32)
        Wq = jax.random.normal(ks[2], (Q_DIM, INNER), dtype=jnp.float32) / np.sqrt(Q_DIM)
        Wk = jax.random.normal(ks[3], (KV_DIM, INNER), dtype=jnp.float32) / np.sqrt(KV_DIM)
        Wv = jax.random.normal(ks[4], (KV_DIM, INNER), dtype=jnp.float32) / np.sqrt(KV_DIM)
        Wo = jax.random.normal(ks[5], (INNER, Q_DIM), dtype=jnp.float32) / np.sqrt(INNER)
        bo = jax.random.normal(ks[6], (Q_DIM,), dtype=jnp.float32) * 0.01
        return {'q': q, 'kv': kv, 'Wq': Wq, 'Wk': Wk, 'Wv': Wv, 'Wo': Wo, 'bo': bo}
    _L2_xattn_all = _L2_xattn_setup()
    _L2_xattn_in = {k: v for k, v in _L2_xattn_all.items() if k in ('Wq', 'Wk', 'Wv', 'Wo', 'bo')}
    del _L2_xattn_all

    def _L2_ffn_setup():
        import jax, jax.numpy as jnp
        import numpy as np
        D_IN, D_HID = (256, 1024)

        def _ternary(key, shape):
            return jax.random.randint(key, shape, -1, 2).astype(jnp.float32)

        def _tlin(x, w, s):
            return jnp.einsum('bsi,oi->bso', x, w) * s
        key = jax.random.key(seed)
        ks = jax.random.split(key, 12)
        inv = lambda fan: 1.0 / np.sqrt(fan).astype(np.float32)
        return {'x': jax.random.normal(ks[0], (4, 512, D_IN), dtype=jnp.float32), 'w1_w': _ternary(ks[1], (D_HID, D_IN)), 'w1_s': jax.random.uniform(ks[2], (D_HID,), dtype=jnp.float32) * inv(D_IN), 'w2_w': _ternary(ks[3], (D_HID, D_IN)), 'w2_s': jax.random.uniform(ks[4], (D_HID,), dtype=jnp.float32) * inv(D_IN), 'h1_w': _ternary(ks[5], (D_HID, D_HID)), 'h1_s': jax.random.uniform(ks[6], (D_HID,), dtype=jnp.float32) * inv(D_HID), 'h2_w': _ternary(ks[7], (D_HID, D_HID)), 'h2_s': jax.random.uniform(ks[8], (D_HID,), dtype=jnp.float32) * inv(D_HID), 'w3_w': _ternary(ks[9], (D_IN, D_HID)), 'w3_s': jax.random.uniform(ks[10], (D_IN,), dtype=jnp.float32) * inv(D_HID)}
    _L2_ffn_all = _L2_ffn_setup()
    _L2_ffn_in = {k: v for k, v in _L2_ffn_all.items() if k in ('w1_w', 'w1_s', 'w2_w', 'w2_s', 'h1_w', 'h1_s', 'h2_w', 'h2_s', 'w3_w', 'w3_s')}
    del _L2_ffn_all

    def _L3_attn_setup():
        import jax, jax.numpy as jnp
        import numpy as np
        import math
        B, S, D = (2, 512, 256)
        HQ, HKV = (16, 4)
        HD = D // HQ
        N_REP = HQ // HKV
        WINDOW = 64
        ROPE_BASE = 10000.0

        def _rope(x):
            s, hd = (x.shape[1], x.shape[-1])
            inv_freq = 1.0 / ROPE_BASE ** (jnp.arange(0, hd, 2, dtype=jnp.float32) / hd)
            ang = jnp.arange(s, dtype=jnp.float32)[:, None] * inv_freq
            cos = jnp.cos(ang)[None, :, None, :].astype(x.dtype)
            sin = jnp.sin(ang)[None, :, None, :].astype(x.dtype)
            x1, x2 = (x[..., ::2], x[..., 1::2])
            out = jnp.stack([x1 * cos - x2 * sin, x1 * sin + x2 * cos], axis=-1)
            return out.reshape(x.shape)
        key = jax.random.key(seed)
        ks = jax.random.split(key, 5)
        sc = 0.02
        return {'x': jax.random.normal(ks[0], (B, S, D), dtype=jnp.float32), 'Wq': jax.random.normal(ks[1], (D, HQ * HD), dtype=jnp.float32) * sc, 'Wk': jax.random.normal(ks[2], (D, HKV * HD), dtype=jnp.float32) * sc, 'Wv': jax.random.normal(ks[3], (D, HKV * HD), dtype=jnp.float32) * sc, 'Wo': jax.random.normal(ks[4], (HQ * HD, D), dtype=jnp.float32) * sc}
    _L3_attn_all = _L3_attn_setup()
    _L3_attn_in = {k: v for k, v in _L3_attn_all.items() if k in ('Wq', 'Wk', 'Wv', 'Wo')}
    del _L3_attn_all

    def _L3_xattn_setup():
        import jax, jax.numpy as jnp
        import numpy as np
        DIM = 256
        LATENT_DIM = 128
        NUM_HEADS = 16
        HEAD_DIM = DIM // NUM_HEADS
        SCALE = HEAD_DIM ** (-0.5)
        key = jax.random.key(seed)
        k1, k2, k3, k4, k5 = jax.random.split(key, 5)
        B, xN, zN = (2, 512, 512)
        x = jax.random.normal(k1, (B, xN, DIM), dtype=jnp.float32)
        z = jax.random.normal(k2, (B, zN, LATENT_DIM), dtype=jnp.float32)
        Wq = jax.random.normal(k3, (DIM, DIM), dtype=jnp.float32) * DIM ** (-0.5)
        Wkv = jax.random.normal(k4, (2 * DIM, LATENT_DIM), dtype=jnp.float32) * LATENT_DIM ** (-0.5)
        Wo = jax.random.normal(k5, (DIM, DIM), dtype=jnp.float32) * DIM ** (-0.5)
        return {'x': x, 'z': z, 'Wq': Wq, 'Wkv': Wkv, 'Wo': Wo}
    _L3_xattn_all = _L3_xattn_setup()
    _L3_xattn_in = {k: v for k, v in _L3_xattn_all.items() if k in ('Wq', 'Wkv', 'Wo')}
    del _L3_xattn_all

    def _L3_ffn_setup():
        import jax, jax.numpy as jnp
        import numpy as np
        E, D, TOP_K = (8, 128, 2)
        EPS_NORM, EPS_COS = (1e-12, 1e-08)

        def _l2norm(v, eps):
            return v / jnp.maximum(jnp.linalg.norm(v, axis=-1, keepdims=True), eps)

        def _mlp(x, gw, uw, dw):
            return jax.nn.silu(x @ gw.T) * (x @ uw.T) @ dw.T
        key = jax.random.key(seed)
        ks = jax.random.split(key, 12)
        B, S, H, F_ = (2, 512, 256, 512)
        G = E * D
        w = lambda k, shp: jax.random.normal(k, shp, dtype=jnp.float32) * 0.02
        return {'hidden_states': jax.random.normal(ks[0], (B, S, H), dtype=jnp.float32), 'gru_w_ih': w(ks[1], (3 * G, H)), 'gru_w_hh': w(ks[2], (3 * G, G)), 'expr_w': w(ks[3], (G, H)), 'ctx_w': w(ks[4], (G, H)), 'ctx_b': jnp.zeros((G,), dtype=jnp.float32), 'gate_w': w(ks[5], (E, F_, H)), 'up_w': w(ks[6], (E, F_, H)), 'down_w': w(ks[7], (E, H, F_)), 'shared_gate_w': w(ks[8], (F_, H)), 'shared_up_w': w(ks[9], (F_, H)), 'shared_down_w': w(ks[10], (H, F_))}
    _L3_ffn_all = _L3_ffn_setup()
    _L3_ffn_in = {k: v for k, v in _L3_ffn_all.items() if k in ('gru_w_ih', 'gru_w_hh', 'expr_w', 'ctx_w', 'ctx_b', 'gate_w', 'up_w', 'down_w', 'shared_gate_w', 'shared_up_w', 'shared_down_w')}
    del _L3_ffn_all
    return {'x': x, 'ctx_512': ctx_512, 'L0_attn_Wk': _L0_attn_in['Wk'], 'L0_attn_bk': _L0_attn_in['bk'], 'L0_attn_Wv': _L0_attn_in['Wv'], 'L0_attn_bv': _L0_attn_in['bv'], 'L0_attn_Wf': _L0_attn_in['Wf'], 'L0_attn_bf': _L0_attn_in['bf'], 'L0_xattn_Wq': _L0_xattn_in['Wq'], 'L0_xattn_bq': _L0_xattn_in['bq'], 'L0_xattn_Wk': _L0_xattn_in['Wk'], 'L0_xattn_bk': _L0_xattn_in['bk'], 'L0_xattn_Wv': _L0_xattn_in['Wv'], 'L0_xattn_bv': _L0_xattn_in['bv'], 'L0_ffn_W_shared': _L0_ffn_in['W_shared'], 'L0_ffn_b_shared': _L0_ffn_in['b_shared'], 'L0_ffn_W_experts': _L0_ffn_in['W_experts'], 'L0_ffn_b_experts': _L0_ffn_in['b_experts'], 'L0_ffn_W_router': _L0_ffn_in['W_router'], 'L0_ffn_b_router': _L0_ffn_in['b_router'], 'L1_attn_w_qkv': _L1_attn_in['w_qkv'], 'L1_attn_w_proj': _L1_attn_in['w_proj'], 'L1_attn_b_proj': _L1_attn_in['b_proj'], 'L1_xattn_Wq': _L1_xattn_in['Wq'], 'L1_xattn_bq': _L1_xattn_in['bq'], 'L1_xattn_Wk': _L1_xattn_in['Wk'], 'L1_xattn_bk': _L1_xattn_in['bk'], 'L1_xattn_Wv': _L1_xattn_in['Wv'], 'L1_xattn_bv': _L1_xattn_in['bv'], 'L1_xattn_Wo': _L1_xattn_in['Wo'], 'L1_xattn_bo': _L1_xattn_in['bo'], 'L1_ffn_centroids': _L1_ffn_in['centroids'], 'L1_ffn_routing_bias': _L1_ffn_in['routing_bias'], 'L1_ffn_Wfc_r': _L1_ffn_in['Wfc_r'], 'L1_ffn_Wproj_r': _L1_ffn_in['Wproj_r'], 'L1_ffn_Wfc_sh': _L1_ffn_in['Wfc_sh'], 'L1_ffn_Wproj_sh': _L1_ffn_in['Wproj_sh'], 'L2_attn_w_qkv': _L2_attn_in['w_qkv'], 'L2_attn_b_qkv': _L2_attn_in['b_qkv'], 'L2_attn_w_proj': _L2_attn_in['w_proj'], 'L2_attn_b_proj': _L2_attn_in['b_proj'], 'L2_xattn_Wq': _L2_xattn_in['Wq'], 'L2_xattn_Wk': _L2_xattn_in['Wk'], 'L2_xattn_Wv': _L2_xattn_in['Wv'], 'L2_xattn_Wo': _L2_xattn_in['Wo'], 'L2_xattn_bo': _L2_xattn_in['bo'], 'L2_ffn_w1_w': _L2_ffn_in['w1_w'], 'L2_ffn_w1_s': _L2_ffn_in['w1_s'], 'L2_ffn_w2_w': _L2_ffn_in['w2_w'], 'L2_ffn_w2_s': _L2_ffn_in['w2_s'], 'L2_ffn_h1_w': _L2_ffn_in['h1_w'], 'L2_ffn_h1_s': _L2_ffn_in['h1_s'], 'L2_ffn_h2_w': _L2_ffn_in['h2_w'], 'L2_ffn_h2_s': _L2_ffn_in['h2_s'], 'L2_ffn_w3_w': _L2_ffn_in['w3_w'], 'L2_ffn_w3_s': _L2_ffn_in['w3_s'], 'L3_attn_Wq': _L3_attn_in['Wq'], 'L3_attn_Wk': _L3_attn_in['Wk'], 'L3_attn_Wv': _L3_attn_in['Wv'], 'L3_attn_Wo': _L3_attn_in['Wo'], 'L3_xattn_Wq': _L3_xattn_in['Wq'], 'L3_xattn_Wkv': _L3_xattn_in['Wkv'], 'L3_xattn_Wo': _L3_xattn_in['Wo'], 'L3_ffn_gru_w_ih': _L3_ffn_in['gru_w_ih'], 'L3_ffn_gru_w_hh': _L3_ffn_in['gru_w_hh'], 'L3_ffn_expr_w': _L3_ffn_in['expr_w'], 'L3_ffn_ctx_w': _L3_ffn_in['ctx_w'], 'L3_ffn_ctx_b': _L3_ffn_in['ctx_b'], 'L3_ffn_gate_w': _L3_ffn_in['gate_w'], 'L3_ffn_up_w': _L3_ffn_in['up_w'], 'L3_ffn_down_w': _L3_ffn_in['down_w'], 'L3_ffn_shared_gate_w': _L3_ffn_in['shared_gate_w'], 'L3_ffn_shared_up_w': _L3_ffn_in['shared_up_w'], 'L3_ffn_shared_down_w': _L3_ffn_in['shared_down_w']}

def reference(x, ctx_512, L0_attn_Wk, L0_attn_bk, L0_attn_Wv, L0_attn_bv, L0_attn_Wf, L0_attn_bf, L0_xattn_Wq, L0_xattn_bq, L0_xattn_Wk, L0_xattn_bk, L0_xattn_Wv, L0_xattn_bv, L0_ffn_W_shared, L0_ffn_b_shared, L0_ffn_W_experts, L0_ffn_b_experts, L0_ffn_W_router, L0_ffn_b_router, L1_attn_w_qkv, L1_attn_w_proj, L1_attn_b_proj, L1_xattn_Wq, L1_xattn_bq, L1_xattn_Wk, L1_xattn_bk, L1_xattn_Wv, L1_xattn_bv, L1_xattn_Wo, L1_xattn_bo, L1_ffn_centroids, L1_ffn_routing_bias, L1_ffn_Wfc_r, L1_ffn_Wproj_r, L1_ffn_Wfc_sh, L1_ffn_Wproj_sh, L2_attn_w_qkv, L2_attn_b_qkv, L2_attn_w_proj, L2_attn_b_proj, L2_xattn_Wq, L2_xattn_Wk, L2_xattn_Wv, L2_xattn_Wo, L2_xattn_bo, L2_ffn_w1_w, L2_ffn_w1_s, L2_ffn_w2_w, L2_ffn_w2_s, L2_ffn_h1_w, L2_ffn_h1_s, L2_ffn_h2_w, L2_ffn_h2_s, L2_ffn_w3_w, L2_ffn_w3_s, L3_attn_Wq, L3_attn_Wk, L3_attn_Wv, L3_attn_Wo, L3_xattn_Wq, L3_xattn_Wkv, L3_xattn_Wo, L3_ffn_gru_w_ih, L3_ffn_gru_w_hh, L3_ffn_expr_w, L3_ffn_ctx_w, L3_ffn_ctx_b, L3_ffn_gate_w, L3_ffn_up_w, L3_ffn_down_w, L3_ffn_shared_gate_w, L3_ffn_shared_up_w, L3_ffn_shared_down_w):
    import jax
    import jax.numpy as jnp

    def _L0_attn_ref(x, Wk, bk, Wv, bv, Wf, bf):
        import jax, jax.numpy as jnp
        import numpy as np
        D_MODEL = 256
        N_HEADS = 16
        D_HIDDEN = 1024
        BATCH = 2
        N_CTX = 512

        def _split_heads(t, n_heads):
            B, S, D = t.shape
            return t.reshape(B, S, n_heads, D // n_heads).transpose(0, 2, 1, 3)
        B, S, D = x.shape
        H = N_HEADS
        Q = _split_heads(x, H)
        K = _split_heads(x @ Wk + bk, H)
        V = _split_heads(x @ Wv + bv, H)
        causal = jnp.tril(jnp.ones((S, S), dtype=bool))
        mask = jnp.where(causal, 0.0, -jnp.inf).astype(x.dtype)
        scores = jnp.einsum('bhqd,bhkd->bhqk', Q, K) + mask
        attn = jax.nn.softmax(scores, axis=-1)
        o = jnp.einsum('bhqk,bhkd->bhqd', attn, V)
        o = o.transpose(0, 2, 1, 3).reshape(B, S, -1)
        return x + jax.nn.gelu(o, approximate=False) @ Wf + bf

    def _L0_xattn_ref(query, key, value, Wq, bq, Wk, bk, Wv, bv):
        import jax, jax.numpy as jnp
        import numpy as np
        B, LQ, LK = (8, 512, 512)
        QD, KD, VD = (256, 128, 128)
        q = jnp.einsum('bld,de->ble', query, Wq) + bq
        k = jnp.einsum('bld,de->ble', key, Wk) + bk
        v = jnp.einsum('bld,de->ble', value, Wv) + bv
        scores = jnp.einsum('bqe,bke->bqk', q, k)
        attn = jax.nn.softmax(scores, axis=-1)
        out = jnp.einsum('bqk,bke->bqe', attn, v)
        return out

    def _L0_ffn_ref(x, W_shared, b_shared, W_experts, b_experts, W_router, b_router):
        import jax, jax.numpy as jnp
        import numpy as np
        B, S, D, E, K = (4, 256, 256, 8, 2)
        shared = jnp.einsum('bsd,hd->bsh', x, W_shared) + b_shared
        scores = jnp.einsum('bsd,ed->bse', x, W_router) + b_router
        top_w, top_i = jax.lax.top_k(scores, K)
        top_w = jax.nn.softmax(top_w, axis=-1)
        gates = jnp.sum(top_w[..., None] * jax.nn.one_hot(top_i, E, dtype=x.dtype), axis=-2)
        y = jnp.einsum('bsd,ehd->bseh', x, W_experts) + b_experts
        routed = jnp.einsum('bse,bseh->bsh', gates, y)
        return shared + routed

    def _L1_attn_ref(x, w_qkv, w_proj, b_proj):
        import jax, jax.numpy as jnp
        import numpy as np
        N_HEAD = 16
        HEAD_SIZE = 256
        EMBED = 256
        MULTI_HEAD_SIZE = HEAD_SIZE // N_HEAD
        B, S = (4, 512)
        qkv = jnp.einsum('bse,he->bsh', x, w_qkv)
        q, k, v = jnp.split(qkv, 3, axis=-1)
        scale = 1.0 / np.sqrt(MULTI_HEAD_SIZE).astype(np.float32)
        scores = jnp.einsum('bqh,bkh->bqk', q, k) * scale
        probs = jax.nn.softmax(scores, axis=-1)
        out = jnp.einsum('bqk,bkh->bqh', probs, v)
        Bn, Sn, H = out.shape
        out = jnp.swapaxes(out, 1, 2).reshape(Bn, Sn, H)
        out = jnp.einsum('bsh,eh->bse', out, w_proj) + b_proj
        return out

    def _L1_xattn_ref(q, k, v, Wq, bq, Wk, bk, Wv, bv, Wo, bo):
        import jax, jax.numpy as jnp
        import numpy as np
        HEADS = 16
        D_MODEL = 256
        IMG_MODEL = 128
        D_K = D_MODEL // HEADS
        B, LQ, _ = q.shape
        LKV = k.shape[1]
        qh = (q @ Wq + bq).reshape(B, LQ, HEADS, D_K).transpose(0, 2, 1, 3)
        kh = (k @ Wk + bk).reshape(B, LKV, HEADS, D_K).transpose(0, 2, 1, 3)
        vh = (v @ Wv + bv).reshape(B, LKV, HEADS, D_K).transpose(0, 2, 1, 3)
        scale = 1.0 / np.sqrt(D_K)
        scores = jnp.einsum('bhqd,bhkd->bhqk', qh, kh) * scale
        attn = jax.nn.softmax(scores, axis=-1)
        out = jnp.einsum('bhqk,bhkd->bhqd', attn, vh)
        concat = out.transpose(0, 2, 1, 3).reshape(B, LQ, D_MODEL)
        return concat @ Wo + bo

    def _L1_ffn_ref(x, centroids, routing_bias, Wfc_r, Wproj_r, Wfc_sh, Wproj_sh):
        import jax, jax.numpy as jnp
        import numpy as np
        D = 256
        F = 4 * D
        E = 8
        NS = 2
        TOP_K = 2
        B, S = (2, 256)
        raw = jnp.einsum('bsd,ed->bse', x, centroids)
        routing_scores = jax.nn.sigmoid(raw)
        balanced = jax.nn.sigmoid(raw + routing_bias)
        _, top_idx = jax.lax.top_k(balanced, TOP_K)
        gathered = jnp.take_along_axis(routing_scores, top_idx, axis=-1)
        top_w = jax.nn.softmax(gathered, axis=-1)
        combine = jnp.sum(jax.nn.one_hot(top_idx, E, dtype=x.dtype) * top_w[..., None], axis=-2)
        h_sh = jax.nn.gelu(jnp.einsum('bsd,nfd->bsnf', x, Wfc_sh), approximate=False)
        shared_out = jnp.einsum('bsnf,ndf->bsd', h_sh, Wproj_sh)
        h_r = jax.nn.gelu(jnp.einsum('bsd,efd->bsef', x, Wfc_r), approximate=False)
        expert_out = jnp.einsum('bsef,edf->bsed', h_r, Wproj_r)
        routed_out = jnp.einsum('bsed,bse->bsd', expert_out, combine)
        return x + shared_out + routed_out

    def _L2_attn_ref(x, w_qkv, b_qkv, w_proj, b_proj):
        import jax, jax.numpy as jnp
        import numpy as np
        B, T, D, H = (4, 512, 256, 16)
        HD = D // H
        b, t, d = x.shape
        scale = HD ** (-0.5)
        qkv = x @ w_qkv + b_qkv
        qkv = qkv.reshape(b, t, 3, H, HD)
        qkv = jnp.transpose(qkv, (2, 0, 3, 1, 4))
        q, k, v = (qkv[0], qkv[1], qkv[2])
        att = jnp.einsum('bhqd,bhkd->bhqk', q, k) * scale
        mask = jnp.tril(jnp.ones((t, t), dtype=att.dtype))[None, None]
        att = att * mask + (1.0 - mask) * -1000000000.0
        att = jax.nn.softmax(att, axis=-1)
        y = jnp.einsum('bhqk,bhkd->bhqd', att, v)
        y = jnp.transpose(y, (0, 2, 1, 3)).reshape(b, t, d)
        return y @ w_proj + b_proj

    def _L2_xattn_ref(q, kv, Wq, Wk, Wv, Wo, bo):
        import jax, jax.numpy as jnp
        import numpy as np
        NUM_HEADS = 16
        HEAD_DIM = 64
        Q_DIM = 256
        KV_DIM = 128
        INNER = NUM_HEADS * HEAD_DIM
        B, N, _ = q.shape
        M = kv.shape[1]
        scale = HEAD_DIM ** (-0.5)
        qh = (q @ Wq).reshape(B, N, NUM_HEADS, HEAD_DIM).transpose(0, 2, 1, 3)
        kh = (kv @ Wk).reshape(B, M, NUM_HEADS, HEAD_DIM).transpose(0, 2, 1, 3)
        vh = (kv @ Wv).reshape(B, M, NUM_HEADS, HEAD_DIM).transpose(0, 2, 1, 3)
        scores = jnp.einsum('bhnd,bhmd->bhnm', qh, kh) * scale
        attn = jax.nn.softmax(scores, axis=-1)
        out = jnp.einsum('bhnm,bhmd->bhnd', attn, vh)
        out = out.transpose(0, 2, 1, 3).reshape(B, N, INNER)
        return out @ Wo + bo

    def _L2_ffn_ref(x, w1_w, w1_s, w2_w, w2_s, h1_w, h1_s, h2_w, h2_s, w3_w, w3_s):
        import jax, jax.numpy as jnp
        import numpy as np
        D_IN, D_HID = (256, 1024)

        def _ternary(key, shape):
            return jax.random.randint(key, shape, -1, 2).astype(jnp.float32)

        def _tlin(x, w, s):
            return jnp.einsum('bsi,oi->bso', x, w) * s
        h = jax.nn.silu(_tlin(x, w1_w, w1_s)) * _tlin(x, w2_w, w2_s)
        h = jax.nn.gelu(_tlin(h, h1_w, h1_s), approximate=False)
        h = jax.nn.gelu(_tlin(h, h2_w, h2_s), approximate=False)
        return _tlin(h, w3_w, w3_s)

    def _L3_attn_ref(x, Wq, Wk, Wv, Wo):
        import jax, jax.numpy as jnp
        import numpy as np
        import math
        B, S, D = (2, 512, 256)
        HQ, HKV = (16, 4)
        HD = D // HQ
        N_REP = HQ // HKV
        WINDOW = 64
        ROPE_BASE = 10000.0

        def _rope(x):
            s, hd = (x.shape[1], x.shape[-1])
            inv_freq = 1.0 / ROPE_BASE ** (jnp.arange(0, hd, 2, dtype=jnp.float32) / hd)
            ang = jnp.arange(s, dtype=jnp.float32)[:, None] * inv_freq
            cos = jnp.cos(ang)[None, :, None, :].astype(x.dtype)
            sin = jnp.sin(ang)[None, :, None, :].astype(x.dtype)
            x1, x2 = (x[..., ::2], x[..., 1::2])
            out = jnp.stack([x1 * cos - x2 * sin, x1 * sin + x2 * cos], axis=-1)
            return out.reshape(x.shape)
        b, s, _ = x.shape
        xq = (x @ Wq).reshape(b, s, HQ, HD)
        xk = (x @ Wk).reshape(b, s, HKV, HD)
        xv = (x @ Wv).reshape(b, s, HKV, HD)
        xq = _rope(xq)
        xk = _rope(xk)
        keys = jnp.repeat(xk, N_REP, axis=2)
        values = jnp.repeat(xv, N_REP, axis=2)
        scores = jnp.einsum('bqhd,bkhd->bhqk', xq, keys) / math.sqrt(HD)
        idx = jnp.arange(s)
        mask = jnp.abs(idx[:, None] - idx[None, :]) <= WINDOW // 2
        scores = jnp.where(mask[None, None], scores, -jnp.inf)
        attn = jax.nn.softmax(scores.astype(jnp.float32), axis=-1).astype(xq.dtype)
        ctx = jnp.einsum('bhqk,bkhd->bqhd', attn, values).reshape(b, s, HQ * HD)
        return ctx @ Wo

    def _L3_xattn_ref(x, z, Wq, Wkv, Wo):
        import jax, jax.numpy as jnp
        import numpy as np
        DIM = 256
        LATENT_DIM = 128
        NUM_HEADS = 16
        HEAD_DIM = DIM // NUM_HEADS
        SCALE = HEAD_DIM ** (-0.5)
        B, xN, _ = x.shape
        _, zN, _ = z.shape
        Q = (x @ Wq.T).reshape(B, xN, NUM_HEADS, HEAD_DIM)
        KV = (z @ Wkv.T).reshape(B, zN, 2, NUM_HEADS, HEAD_DIM)
        K = KV[:, :, 0]
        V = KV[:, :, 1]
        attn = jnp.einsum('bqhd,bkhd->bhqk', Q, K) * SCALE
        attn = jax.nn.softmax(attn, axis=-1)
        O = jnp.einsum('bhqk,bkhd->bqhd', attn, V).reshape(B, xN, DIM)
        return O @ Wo.T

    def _L3_ffn_ref(hidden_states, gru_w_ih, gru_w_hh, expr_w, ctx_w, ctx_b, gate_w, up_w, down_w, shared_gate_w, shared_up_w, shared_down_w):
        import jax, jax.numpy as jnp
        import numpy as np
        E, D, TOP_K = (8, 128, 2)
        EPS_NORM, EPS_COS = (1e-12, 1e-08)

        def _l2norm(v, eps):
            return v / jnp.maximum(jnp.linalg.norm(v, axis=-1, keepdims=True), eps)

        def _mlp(x, gw, uw, dw):
            return jax.nn.silu(x @ gw.T) * (x @ uw.T) @ dw.T
        B, S, H = hidden_states.shape
        h0 = hidden_states.mean(axis=1) @ ctx_w.T + ctx_b
        xw = hidden_states @ gru_w_ih.T

        def step(h, xw_t):
            hw = h @ gru_w_hh.T
            xr, xz, xn = jnp.split(xw_t, 3, axis=-1)
            hr, hz, hnn = jnp.split(hw, 3, axis=-1)
            r = jax.nn.sigmoid(xr + hr)
            z = jax.nn.sigmoid(xz + hz)
            n = jnp.tanh(xn + r * hnn)
            h_new = (1.0 - z) * n + z * h
            return (h_new, h_new)
        _, hs = jax.lax.scan(step, h0, jnp.swapaxes(xw, 0, 1))
        routing = jnp.swapaxes(hs, 0, 1).reshape(B, S, E, D)
        routing = _l2norm(routing, EPS_NORM)
        expr = (hidden_states @ expr_w.T).reshape(B, S, E, D)
        gram = jnp.einsum('bsed,bsfd->bsef', routing, routing)
        diff = gram - jnp.eye(E, dtype=routing.dtype)
        diff_n = _l2norm(diff, EPS_NORM)
        penalty = jnp.mean(jnp.sum(diff_n ** 2, axis=(-2, -1)))
        num = jnp.sum(expr * routing, axis=-1)
        den = jnp.maximum(jnp.linalg.norm(expr, axis=-1), EPS_COS) * jnp.maximum(jnp.linalg.norm(routing, axis=-1), EPS_COS)
        cos_dist = 1.0 - num / den
        scores = (cos_dist * (1.0 + penalty)).reshape(B * S, E)
        top_v, top_i = jax.lax.top_k(scores, TOP_K)
        mult = jax.nn.softmax(top_v, axis=-1)
        onehot = jax.nn.one_hot(top_i, E, dtype=mult.dtype)
        cw = jnp.einsum('tk,tke->te', mult, onehot)
        xf = hidden_states.reshape(B * S, H)
        out = jnp.zeros_like(xf)
        for e in range(E):
            out = out + cw[:, e:e + 1] * _mlp(xf, gate_w[e], up_w[e], down_w[e])
        moe = out.reshape(B, S, H)
        shared = jax.lax.stop_gradient(_mlp(hidden_states, shared_gate_w, shared_up_w, shared_down_w))
        return moe + shared
    x = x + _L0_attn_ref(_layernorm(x, axis=-1), L0_attn_Wk, L0_attn_bk, L0_attn_Wv, L0_attn_bv, L0_attn_Wf, L0_attn_bf)
    x = x + _L0_xattn_ref(_layernorm(x, axis=-1), ctx_512, ctx_512, L0_xattn_Wq, L0_xattn_bq, L0_xattn_Wk, L0_xattn_bk, L0_xattn_Wv, L0_xattn_bv)
    x = x + _L0_ffn_ref(_layernorm(x, axis=-1), L0_ffn_W_shared, L0_ffn_b_shared, L0_ffn_W_experts, L0_ffn_b_experts, L0_ffn_W_router, L0_ffn_b_router)
    x = x + _L1_attn_ref(_layernorm(x, axis=-1), L1_attn_w_qkv, L1_attn_w_proj, L1_attn_b_proj)
    x = x + _L1_xattn_ref(_layernorm(x, axis=-1), ctx_512, ctx_512, L1_xattn_Wq, L1_xattn_bq, L1_xattn_Wk, L1_xattn_bk, L1_xattn_Wv, L1_xattn_bv, L1_xattn_Wo, L1_xattn_bo)
    x = x + _L1_ffn_ref(_layernorm(x, axis=-1), L1_ffn_centroids, L1_ffn_routing_bias, L1_ffn_Wfc_r, L1_ffn_Wproj_r, L1_ffn_Wfc_sh, L1_ffn_Wproj_sh)
    x = x + _L2_attn_ref(_layernorm(x, axis=-1), L2_attn_w_qkv, L2_attn_b_qkv, L2_attn_w_proj, L2_attn_b_proj)
    x = x + _L2_xattn_ref(_layernorm(x, axis=-1), ctx_512, L2_xattn_Wq, L2_xattn_Wk, L2_xattn_Wv, L2_xattn_Wo, L2_xattn_bo)
    x = x + _L2_ffn_ref(_layernorm(x, axis=-1), L2_ffn_w1_w, L2_ffn_w1_s, L2_ffn_w2_w, L2_ffn_w2_s, L2_ffn_h1_w, L2_ffn_h1_s, L2_ffn_h2_w, L2_ffn_h2_s, L2_ffn_w3_w, L2_ffn_w3_s)
    x = x + _L3_attn_ref(_layernorm(x, axis=-1), L3_attn_Wq, L3_attn_Wk, L3_attn_Wv, L3_attn_Wo)
    x = x + _L3_xattn_ref(_layernorm(x, axis=-1), ctx_512, L3_xattn_Wq, L3_xattn_Wkv, L3_xattn_Wo)
    x = x + _L3_ffn_ref(_layernorm(x, axis=-1), L3_ffn_gru_w_ih, L3_ffn_gru_w_hh, L3_ffn_expr_w, L3_ffn_ctx_w, L3_ffn_ctx_b, L3_ffn_gate_w, L3_ffn_up_w, L3_ffn_down_w, L3_ffn_shared_gate_w, L3_ffn_shared_up_w, L3_ffn_shared_down_w)
    return x

_drawn_inputs = setup_inputs


def setup_inputs(seed=0):
    import zlib

    import numpy as np

    out = dict(_drawn_inputs(seed))
    spreads = {'L0_attn_bk': (0.0, 0.1),
     'L0_attn_bv': (0.0, 0.1),
     'L0_attn_bf': (0.0, 0.1),
     'L0_xattn_bq': (0.0, 0.1),
     'L0_xattn_bk': (0.0, 0.1),
     'L0_xattn_bv': (0.0, 0.1),
     'L1_xattn_bq': (0.0, 0.1),
     'L1_xattn_bk': (0.0, 0.1),
     'L1_xattn_bv': (0.0, 0.1),
     'L1_xattn_bo': (0.0, 0.1),
     'L1_ffn_routing_bias': (0.0, 0.1),
     'L2_attn_b_qkv': (0.0, 0.1),
     'L2_attn_b_proj': (0.0, 0.1),
     'L3_ffn_ctx_b': (0.0, 0.1)}
    factors = {}
    for name, (base, spread) in spreads.items():
        noise = np.random.default_rng([zlib.crc32(name.encode()), seed]).standard_normal(out[name].shape)
        drawn = base * np.exp(spread * noise) if base else spread * noise
        out[name] = jnp.asarray(drawn.astype(out[name].dtype))
    for name, factor in factors.items():
        out[name] = (out[name] * factor).astype(out[name].dtype)
    return out
```

```python
from contextlib import ExitStack, contextmanager

import numpy as np

import concourse.bass as bass
from concourse import mybir

F32 = mybir.dt.float32
I32 = mybir.dt.int32
ACT = mybir.ActivationFunctionType
ALU = mybir.AluOpType
AX = mybir.AxisListType.X

B, S, D, E = 8, 100, 256, 8
T = B * S
P = 128
C = D // P
NK, KR, KC = 361, 121, 3
NKP = KR * KC
CTX = 128
H = 16
HD = D // H
F1, E1 = 1024, 10
F2 = 1024
F3, E3 = 512, 9
G, ED = 1024, 128
HALF = T // 2
EPS = 1e-5
MASKED = -1e30



def packing(*items):
    at, where = 0, {}
    for name, n in items:
        where[name] = (at, n)
        at += n
    return where, at


CONST, CONST_N = packing(("ident", P), ("rank", E), ("causal", S), ("window", S), ("cos", S), ("sin", S), ("cos4", S), ("sin4", S), ("ones", P),
                          ("ones8", 32))
WA, WA_N = packing(
    ("a_pick", C * 512), ("a_wk", C * 512), ("a_wv", C * 1024), ("a_wf", 8 * D), ("a_bk", 4),
    ("x_wq", C * D), ("x_wk", D), ("x_wv", D), ("x_bq", C), ("x_bk", C),
    ("f_w", C * 9 * D), ("f_router", C * E), ("f_b", D),
    ("s_wqkv", C * 768), ("s_wo", C * D),
    ("y_wq", C * 512), ("y_wk", 512), ("y_wv", D), ("y_wo", C * D), ("y_bq", 4), ("y_bk", 4),
    ("r_a_bv", 1024), ("r_a_bf", D), ("r_x_bv", D), ("r_router", E), ("r_s_bo", D), ("r_y_bv", D), ("r_y_bo", D))
WB, WB_N = packing(
    ("wq", C * 512), ("wk", C * 512), ("wv", C * D), ("wo", C * D), ("bq", 4), ("bk", 4),
    ("x_wq", C * 1024), ("x_wk", 1024), ("x_wv", 1024), ("x_wo", 8 * D),
    ("r_bv", D), ("r_bo", D), ("r_x_bo", D))
WC, WC_N = packing(
    ("wq", C * 512), ("wqs", C * 512), ("wk", C * 512), ("wks", C * 512), ("wv", C * D), ("wo", C * D),
    ("x_wq", C * 512), ("x_wk", 512), ("x_wv", D), ("x_wo", C * D))

AT_WA = 0
AT_WB = 0
AT_WC = WB_N
AT_WORK = 21500
AT_FW = 34300
AT_WORK2 = 38396
ARENA = 42750
assert WA_N <= AT_WORK and WB_N + WC_N <= AT_WORK

LAP_A = dict(d_evac=38, a_evac=34, s_exp=12, xn=6, gate_d=2, gate_e=1, turn=1)
LAP_B = dict(d_evac=32, a_evac=24, s_exp=10, xn=2)
LAP_C = dict(d_evac=28, a_evac=20, s_exp=10, xn=2, rotated=2)
LAP_F1 = dict(d_evac=8, a_evac=16)
LAP_F3 = dict(d_evac=16, a_evac=8)
for per in (LAP_A, LAP_B, LAP_C, LAP_F1, LAP_F3):
    per.update(d_full=per["d_evac"], a_full=per["a_evac"])
    if "s_exp" in per:
        per.update(s_full=per["s_exp"], s_max=per["s_exp"])


class Count:

    def __init__(self, eng, sems):
        self.eng, self.sems = eng, sems
        self.before, self.now = dict(d_evac=2, a_evac=2, s_exp=2), {}
        self.lap, self.per, self.parity = None, {}, {"d": 0, "a": 0, "s": 0}

    def add(self, key, n=1):
        self.now[key] = self.now.get(key, 0) + n
        return self.now[key]

    def got(self, key):
        return self.now.get(key, 0)

    def value(self, key, n):
        value = self.before.get(key, 0) + n
        assert value > 0, (key, value)
        if self.lap is not None and self.per.get(key, 0):
            return self.lap * self.per[key] + value
        return value

    def wait(self, key, n):
        self.eng.wait_ge(self.sems[key], self.value(key, n))

    def next(self, key, n=1):
        self.wait(key, self.add(key, n))

    @contextmanager
    def laps(self, laps, per):
        for key, n in self.now.items():
            self.before[key] = self.before.get(key, 0) + n
        self.now, self.per = {}, per
        with self.eng.Fori(0, laps) as lap:
            self.lap = lap
            yield lap
        wrong = {key: n for key, n in self.now.items() if per.get(key) != n}
        assert not wrong, (wrong, per)
        for key, n in per.items():
            self.before[key] = self.before.get(key, 0) + laps * n
        self.now, self.lap, self.per = {}, None, {}


def build(nc, dram, out):
    with ExitStack() as ctx:
        def sb(name, shape):
            return ctx.enter_context(nc.sbuf_tensor(name, shape, F32))

        def scratch(name, shape):
            return nc.dram_tensor(name, shape, F32, kind="Internal").ap()

        X = sb("X", [S, B * D])
        XN = sb("XN", [S, B * D])
        XNT = sb("XNT", [P, C, T])
        ctx_now = sb("ctx_now", [CTX, NKP])
        const = sb("const_sb", [P, CONST_N])
        arena = sb("arena", [P, ARENA])
        stats = sb("stats", [S, B, 8])
        rstd = sb("rstd", [S, 2 * B])
        gates = sb("gates", [S, E1, B])
        gate_now = sb("gate_now", [S, B])
        idle = sb("idle", [S, 32])
        small = sb("small", [S, 16, B, E])
        gate_row = sb("gate_row", [S, E + 1])
        cent = sb("cent", [P, C * E])
        bq4 = sb("bq4", [P, 8])
        rbias = sb("rbias", [S, E])
        sums = sb("sums", [S, H])
        rsum = sb("rsum", [S, H])
        ntop = sb("ntop", [S, 16])
        banks = ctx.enter_context(nc.psum_tensor("banks", [P, 8, 512], F32))

        turned = scratch("turned", (B, D * S))
        history = scratch("history", (B, S, G))

        def cut(pack, base, name, *dims):
            at, n = pack[name]
            a = arena[:, base + at:base + at + n]
            if len(dims) == 1:
                a = a.rearrange("p (k n) -> p k n", k=dims[0])
            return a

        def cst(name):
            at, n = CONST[name]
            return const[:, at:at + n]

        ident, ones, ones8 = cst("ident"), cst("ones"), cst("ones8")[0:1, :]

        at = AT_WORK

        def work(n):
            nonlocal at
            a = arena[:, at:at + n]
            at += n
            return a

        xb = work(D)[0:S]
        xn = work(D)[0:S]
        xnT = work(C * S).rearrange("p (k s) -> p k s", k=C)
        qT = work(8 * S).rearrange("p (k s) -> p k s", k=8)
        kT = work(8 * NK).rearrange("p (k s) -> p k s", k=8)
        v = work(KC * 1024).rearrange("p (c n) -> p c n", c=KC)
        o = work(1024)[0:S]
        oT = work(8 * S).rearrange("p (k s) -> p k s", k=8)
        gT = work(S)
        rope_t = work(4 * S).rearrange("p (k s) -> p k s", k=4)
        rope_u = work(4 * S).rearrange("p (k s) -> p k s", k=4)
        assert at <= AT_FW, at
        at = AT_WORK2
        probs_x = work(2 * 2 * NKP)[0:S].rearrange("p (u i k) -> p u i k", u=2, i=2)
        probs_s = work(2 * 2 * 4 * S)[0:S].rearrange("p (u i k) -> p u i k", u=2, i=2)
        pT = work(2 * 4 * S).rearrange("p (i m s) -> p i m s", i=2, m=4)
        assert at <= ARENA, at

        h0T = arena[:, AT_WORK:AT_WORK + 6400].rearrange("p (f t) -> p f t", f=8)
        h1T = arena[:, AT_WORK + 6400:AT_WORK + 12800].rearrange("p (f t) -> p f t", f=8)
        fc = arena[:, AT_FW:AT_FW + 2048].rearrange("p (k f) -> p k f", k=2)
        pj = arena[:, AT_FW + 2048:AT_FW + 4096].rearrange("p (f d) -> p f d", f=8)
        w2 = arena[:, AT_FW + 2048:AT_FW + 4096].rearrange("p (k f) -> p k f", k=2)
        slots = [arena[:, 1024 * i:1024 * (i + 1)].rearrange("p (k o) -> p k o", k=8) for i in range(4)]
        w3 = arena[:, 4096:6144].rearrange("p (f d) -> p f d", f=8)
        w3s = arena[:, 6144:6400]
        s2 = arena[:, 6400:6432].rearrange("p (m f) -> p m f", m=4)
        y2 = arena[:, 6656:6656 + 2 * D].rearrange("p (i d) -> p i d", i=2)
        silu2 = arena[:, AT_WORK2:AT_WORK2 + 800].rearrange("p (r t) -> p r t", r=2)
        gu3 = arena[:, AT_FW:AT_FW + 2048].rearrange("p (u k f) -> p u k f", u=2, k=2)
        dn3 = arena[:, AT_FW + 2048:AT_FW + 3072].rearrange("p (f d) -> p f d", f=4)
        whh = arena[:, 0:24576].rearrange("p (k j n) -> p k j n", k=8, j=4)
        wih = arena[:, 24576:30720].rearrange("p (k j n) -> p k j n", k=2, j=4)
        g0 = 30720

        def gru(n):
            nonlocal g0
            a = arena[:, g0:g0 + n]
            g0 += n
            return a

        h = gru(512).rearrange("p (i n) -> p i n", i=2)
        hT = gru(256).rearrange("p (c q) -> p c q", c=2)
        xt = gru(128).rearrange("p (i k q) -> p i k q", i=2, k=2)
        rz = gru(512)
        omz = gru(256)
        zh = gru(256)
        cand = gru(256)
        t1 = gru(256)
        mean = gru(64).rearrange("p (k q) -> p k q", k=2)
        cb = gru(1024)
        assert g0 <= AT_FW, g0
        cw = arena[:, AT_WORK2:AT_WORK2 + 2048].rearrange("p (k g) -> p k g", k=2)
        ew = arena[:, 0:2048].rearrange("p (k g) -> p k g", k=2)
        R = arena[0:S, 2048:2048 + 2 * G].rearrange("p (i g) -> p i g", i=2)
        ex = arena[0:S, 4096:4096 + G]
        prod = arena[0:S, 5120:5120 + G]
        dots = arena[0:S, 6144:6144 + 3 * B * E].rearrange("p (q b e) -> p q b e", q=3, b=B)
        gram = arena[0:S, 6400:6400 + 512].rearrange("p (b q) -> p b q", b=B)
        gsq = arena[0:S, 6912:6912 + 512].rearrange("p (b q) -> p b q", b=B)
        pen = arena[0:S, 7424:7424 + 16]
        h3 = arena[:, 8192:8192 + 3200].rearrange("p (f t) -> p f t", f=4)
        silu3 = arena[:, 12288:12288 + 800].rearrange("p (r t) -> p r t", r=2)

        names = (
            "d_full", "d_evac", "a_full", "a_evac", "s_full", "s_max", "s_exp",
            "xn", "rotated", "root_in", "root_out", "gate_d", "gate_e", "turn", "v_step", "a_step", "silu", "xt_zero", "phase", "raw",
            "rz_full", "n_full", "x_used", "x_slice", "rz_done", "n_in", "n_done", "h_new", "h_turned", "h_back",
            "pen_in", "R_used", "zeroed",
            "l_const", "l_x", "l_ctx", "l_wa", "l_wb", "l_wc", "l_fc", "l_pj", "l_rb", "l_w2", "l_s0", "l_s1",
            "l_s2", "l_s3", "l_w3", "l_gru", "l_cw", "l_h0", "l_h1", "l_gu", "l_dn", "l_ew", "l_R0", "l_R1",
            "o_turn", "l_out")
        sem = {name: ctx.enter_context(nc.semaphore(name)) for name in names}
        block = ctx.enter_context(nc.Block())

        RING = {"d": 4, "a": 6}
        MARK = {}

        SELF = [[[(4 * c + j, [(32 * j, HD, c)]) for c in range(4)] for j in (2 * u, 2 * u + 1)] for u in range(2)]
        CROSS = [[[(hh, [(32 * (hh % 4), HD, hh // 4)])] for hh in (2 * u, 2 * u + 1)] for u in range(8)]
        WIDE = [[[(hh, [(64 * (hh % 2), 64, hh // 2)])] for hh in (2 * u, 2 * u + 1)] for u in range(8)]
        WHOLE = [[[(0, [(0, P, 0), (0, P, 1)])]]]

        def probs_of(unit_slot, bank, keys):
            return (probs_s if keys == S else probs_x)[:, unit_slot, bank]

        def wa(name, *k):
            return cut(WA, AT_WA, name, *k)

        def wb(name, *k):
            return cut(WB, AT_WB, name, *k)

        def wc(name, *k):
            return cut(WC, AT_WC, name, *k)

        def like(dst, src):
            return src if len(dst.shape) == 2 else src.rearrange("p (a b) -> p a b", a=dst.shape[1])

        def per_column(bias, n, width):
            return bias[:, 0:n].unsqueeze(2).to_broadcast([P, n, width])

        @block.tensor
        def _(pe):
            n = Count(pe, sem)

            def open_unit(ring):
                n.wait(ring + "_evac", n.got(ring + "_evac") - 1)
                bank = RING[ring] + n.parity[ring]
                n.parity[ring] ^= 1
                return banks[:, bank, :], n.add(ring + "_evac")

            def evacuated(ring, unit=None):
                n.wait(ring + "_evac", n.got(ring + "_evac") if unit is None else unit)

            def full(ring, last):
                last.then_inc(sem[ring + "_full"], 1)

            def turn_rows(ring, src, chunks):
                u, k = open_unit(ring)
                for c in range(chunks):
                    last = nc.tensor.transpose(u[:, c * S:(c + 1) * S], src[:, c * P:(c + 1) * P], ident[0:S, 0:S])
                full(ring, last)
                return k

            def features(ring, w, lo, hi):
                u, k = open_unit(ring)
                for i, c in enumerate(range(lo, hi)):
                    for kk in range(C):
                        last = nc.tensor.matmul(u[:, i * S:(i + 1) * S], w[:, kk, c * P:(c + 1) * P], xnT[:, kk, :],
                                                start=kk == 0, stop=kk == C - 1)
                full(ring, last)
                return k

            def tokens(ring, parts, cols, bias=None):
                u, k = open_unit(ring)
                for i, (a, b) in enumerate(parts):
                    last = nc.tensor.matmul(u[0:S, 0:cols], a, b, start=i == 0, stop=bias is None and i == len(parts) - 1)
                if bias is not None:
                    last = nc.tensor.matmul(u[0:S, 0:cols], ones[0:1, 0:S], bias, start=False, stop=True)
                full(ring, last)
                return k

            def project(ring, w, lo, cols, bias=None):
                return tokens(ring, [(xnT[:, kk, :], w[:, kk, lo:lo + cols]) for kk in range(C)], cols, bias)

            def context_keys(w, chunks, rings):
                for c in range(chunks):
                    ring = rings[c % len(rings)]
                    u, _ = open_unit(ring)
                    full(ring, nc.tensor.matmul(u[:, 0:NK], w[:, c * P:(c + 1) * P], ctx_now[:, 0:NK], start=True, stop=True))

            def context_values(w, width, bias, rings):
                cols = min(width, 512)
                pieces = [(c, j) for c in range(KC) for j in range(0, width, cols)]
                per = 512 // cols
                for i in range(0, len(pieces), per):
                    ring = rings[i // per % len(rings)]
                    u, _ = open_unit(ring)
                    for m, (c, j) in enumerate(pieces[i:i + per]):
                        last = nc.tensor.matmul(u[0:KR, m * cols:(m + 1) * cols], ctx_now[:, c * KR:(c + 1) * KR],
                                                w[:, j:j + cols], start=True, stop=bias is None)
                        if bias is not None:
                            last = nc.tensor.matmul(u[0:KR, m * cols:(m + 1) * cols], ones[0:1, 0:KR],
                                                    bias[0:1, j:j + cols], start=False, stop=True)
                    full(ring, last)

            def scores(unit, keys):
                n.wait("s_exp", n.got("s_exp") - 1)
                slot = n.parity["s"]
                n.parity["s"] ^= 1
                for m in range(len(unit[0])):
                    for i, bank in enumerate(unit):
                        parts = bank[m][1]
                        for q, (r, w, c) in enumerate(parts):
                            last = nc.tensor.matmul(banks[0:S, 2 * slot + i, m * keys:(m + 1) * keys], qT[r:r + w, c, :],
                                                    kT[r:r + w, c, 0:keys], start=q == 0, stop=q == len(parts) - 1)
                last.then_inc(sem["s_full"], 1)
                return slot, n.add("s_exp")

            def attention(units, keys, dv):
                evacuated("a")
                evacuated("d")
                open_ = [scores(unit, keys) for unit in units[:2]]
                chunks, step = (1, S) if keys == S else (KC, KR)
                for g, unit in enumerate(units):
                    slot, done = open_.pop(0)
                    n.wait("s_exp", done)
                    used = []
                    for i, bank in enumerate(unit):
                        u, k = open_unit("da"[i])
                        for m in range(len(bank) * chunks):
                            last = nc.tensor.transpose(u[0:step, m * S:(m + 1) * S],
                                                       probs_of(slot, i, keys)[:, m * step:(m + 1) * step], ident[0:S, 0:S])
                        full("da"[i], last)
                        used.append(("da"[i], k))
                    if g + 2 < len(units):
                        open_.append(scores(units[g + 2], keys))
                    for ring, k in used:
                        evacuated(ring, k)
                    u, k = open_unit("d")
                    at = 0
                    for i, bank in enumerate(unit):
                        for m, (hh, _) in enumerate(bank):
                            for c in range(chunks):
                                last = nc.tensor.matmul(u[0:S, at:at + dv], pT[0:step, i, m * chunks + c, :],
                                                        v[0:step, c, hh * dv:(hh + 1) * dv], start=c == 0, stop=c == chunks - 1)
                            at += dv
                    full("d", last)
                evacuated("d")

            def out_rows(chunks, w, bias, ring="a"):
                for c in range(0, chunks, 4):
                    turn_rows(ring, o[:, c * P:], min(4, chunks - c))
                evacuated(ring)
                tokens("d", [(oT[:, c, :], w[:, c, :]) for c in range(chunks)], D, bias)

            def normed():
                n.next("xn")
                evacuated("a", turn_rows("a", xn, C))

            pe.wait_ge(sem["l_const"], 16)
            pe.wait_ge(sem["l_wa"], 16)
            with n.laps(B, LAP_A) as lap:
                normed()
                features("a", wa("a_pick", C), 0, 4)
                features("d", wa("a_wk", C), 0, 4)
                for j in (0, 512):
                    project("a", wa("a_wv", C), j, 512, wa("r_a_bv")[0:1, j:j + 512])
                attention(SELF, S, 64)
                out_rows(8, wa("a_wf", 8), wa("r_a_bf")[0:1, :])
                normed()
                features("d", wa("x_wq", C), 0, 2)
                pe.wait_ge(sem["l_ctx"], 16 * lap + 16)
                context_keys(wa("x_wk"), C, "a")
                context_values(wa("x_wv"), D, wa("r_x_bv"), "a")
                attention(WHOLE, NK, D)
                normed()
                project("d", wa("f_router", C), 0, E, wa("r_router")[0:1, :])
                for j in range(0, 9, 2):
                    project("d", wa("f_w", C), j * D, min(2, 9 - j) * D)
                n.next("gate_d", 2)
                u, k = open_unit("a")
                full("a", nc.tensor.transpose(u[0:9, 0:S], gate_row[:, :], ident[0:S, 0:S]))
                evacuated("a", k)
                tokens("d", [(gT[0:9, :], wa("f_b")[0:9, :])], D)
                normed()
                features("a", wa("s_wqkv", C), 0, 4)
                project("a", wa("s_wqkv", C), 512, D)
                evacuated("a")
                slot, _ = scores(WHOLE[0], S)
                n.next("xn")
                u, k = open_unit("d")
                full("d", nc.tensor.transpose(u[0:S, 0:S], probs_s[:, slot, 0, 0:S], ident[0:S, 0:S]))
                evacuated("d", k)
                u, k = open_unit("a")
                for c in range(C):
                    last = nc.tensor.matmul(u[:, c * S:(c + 1) * S], v[0:S, 0, c * P:(c + 1) * P], pT[0:S, 0, 0, :],
                                            start=True, stop=True)
                full("a", last)
                MARK["turn"] = k
                pe.wait_ge(sem["turn"], 16 * lap + 16)
                turn_rows("a", o, C)
                evacuated("a")
                tokens("d", [(oT[:, 4 + c, :], wa("s_wo", C)[:, c, :]) for c in range(C)], D, wa("r_s_bo")[0:1, :])
                normed()
                features("d", wa("y_wq", C), 0, 4)
                context_keys(wa("y_wk"), 4, "da")
                context_values(wa("y_wv"), D, wa("r_y_bv"), "a")
                attention(CROSS, NK, HD)
                out_rows(C, wa("y_wo", C), wa("r_y_bo")[0:1, :])

            def turn_all():
                n.next("xn")
                for b in range(B):
                    turn_rows("a", XN[:, b * D:], C)
                evacuated("a")

            def all_features(ring, parts, half):
                u, k = open_unit(ring)
                for i, (w, x) in enumerate(parts):
                    last = nc.tensor.matmul(u[:, 0:HALF], w, x[:, half * HALF:(half + 1) * HALF],
                                            start=i == 0, stop=i == len(parts) - 1)
                full(ring, last)
                return k

            def down(hid, w, chunks):
                for b in range(B):
                    tokens("d", [(hid[:, f, b * S:(b + 1) * S], w[:, f, :]) for f in range(chunks)], D)

            def router_rows(w):
                u, _ = open_unit("d")
                for b in range(B):
                    for kk in range(C):
                        last = nc.tensor.matmul(u[0:S, b * E:(b + 1) * E], XNT[:, kk, b * S:(b + 1) * S], w[:, kk, :],
                                                start=kk == 0, stop=kk == C - 1)
                full("d", last)

            turn_all()
            pe.wait_ge(sem["l_rb"], 32)
            router_rows(cent[:, :].rearrange("p (k e) -> p k e", k=C))
            MARK["F1"] = {key: n.value(key, n.got(key)) for key in ("d_evac", "a_evac")}
            with n.laps(E1, LAP_F1) as e:
                pe.wait_ge(sem["l_fc"], 16 * e + 16)
                for f in range(8):
                    for half in range(2):
                        all_features("a", [(fc[:, kk, f * P:(f + 1) * P], XNT[:, kk, :]) for kk in range(C)], half)
                evacuated("a")
                pe.wait_ge(sem["l_pj"], 16 * e + 16)
                down(h0T, pj, 8)

            pe.wait_ge(sem["l_wb"], 16)
            pe.wait_ge(sem["l_wc"], 16)
            with n.laps(B, LAP_B) as lap:
                normed()
                features("d", wb("wq", C), 0, 4)
                features("d", wb("wk", C), 0, 4)
                project("a", wb("wv", C), 0, D, wb("r_bv")[0:1, :])
                attention(SELF, S, HD)
                out_rows(C, wb("wo", C), wb("r_bo")[0:1, :])
                normed()
                features("a", wb("x_wq", C), 0, 4)
                features("d", wb("x_wq", C), 4, 8)
                pe.wait_ge(sem["l_ctx"], 16 * lap + 16 * (B + 1))
                context_keys(wb("x_wk"), 8, "da")
                context_values(wb("x_wv"), 1024, None, "ad")
                attention(WIDE, NK, 64)
                out_rows(8, wb("x_wo", 8), wb("r_x_bo")[0:1, :])

            turn_all()
            pe.wait_ge(sem["l_w2"], 48)
            for f in range(8):
                for half in range(2):
                    all_features("a", [(fc[:, kk, f * P:(f + 1) * P], XNT[:, kk, :]) for kk in range(C)], half)
                    all_features("d", [(w2[:, kk, f * P:(f + 1) * P], XNT[:, kk, :]) for kk in range(C)], half)
            evacuated("d")
            MARK["slots"] = []
            for i in range(16):
                source = h0T if i < 8 else h1T
                if i == 8:
                    evacuated("a")
                pe.wait_ge(sem["l_s%d" % (i % 4)], 16 * (i // 4 + 1))
                for half in range(2):
                    k = all_features("a", [(slots[i % 4][:, kk, :], source[:, kk, :]) for kk in range(8)], half)
                MARK["slots"].append(n.value("a_evac", k))
            evacuated("a")
            pe.wait_ge(sem["l_w3"], 32)
            down(h0T, w3, 8)

            with n.laps(B, LAP_C) as lap:
                normed()
                for name in ("wq", "wqs", "wk", "wks"):
                    features("d", wc(name, C), 0, 4)
                project("a", wc("wv", C), 0, D)
                n.next("rotated", 2)
                attention(SELF, S, HD)
                out_rows(C, wc("wo", C), None)
                normed()
                features("a", wc("x_wq", C), 0, 4)
                pe.wait_ge(sem["l_ctx"], 16 * lap + 16 * (2 * B + 1))
                context_keys(wc("x_wk"), 4, "da")
                context_values(wc("x_wv"), D, None, "a")
                attention(CROSS, NK, HD)
                out_rows(C, wc("x_wo", C), None)

            turn_all()
            pe.wait_ge(sem["l_cw"], 32)
            pe.wait_ge(sem["zeroed"], 1)
            u, k = open_unit("d")
            for j in range(4):
                for kk in range(C):
                    nc.tensor.matmul(u[32 * j:32 * j + 32, 0:256], mean[:, kk, :], cw[:, kk, 256 * j:256 * j + 256],
                                     start=kk == 0, stop=False, skip_group_check=True)
                last = nc.tensor.matmul(u[32 * j:32 * j + 32, 0:256], ones8, cb[0:1, 256 * j:256 * j + 256],
                                        start=False, stop=True, skip_group_check=True)
            full("d", last)

            def turn_state(i):
                pt = banks[:, 4, :]
                for c in range(2):
                    last = nc.tensor.transpose(pt[:, c * P:(c + 1) * P], h[:, i, c * P:(c + 1) * P], ident[:, :])
                last.then_inc(sem["h_back"], 1)

            def x_part(i):
                for kk in range(C):
                    for j in range(4):
                        nc.tensor.matmul(banks[32 * j:32 * j + 32, i, :], xt[:, i, kk, :], wih[:, kk, j, 0:512],
                                         start=kk == 0, stop=False, skip_group_check=True)
                for kk in range(C):
                    for j in range(4):
                        last = nc.tensor.matmul(banks[32 * j:32 * j + 32, 2 + i, 256:512], xt[:, i, kk, :], wih[:, kk, j, 512:768],
                                                start=kk == 0, stop=False, skip_group_check=True)
                last.then_inc(sem["x_used"], 1)

            pe.wait_ge(sem["l_gru"], 32)
            pe.wait_ge(sem["x_slice"], 1)
            x_part(0)
            pe.wait_ge(sem["h_new"], 1)
            turn_state(1)
            with pe.Fori(0, S // 2) as t:
                for i in range(2):
                    pe.wait_ge(sem["h_turned"], 2 * t + i + 1)
                    for kk in range(8):
                        for j in range(4):
                            last = nc.tensor.matmul(banks[32 * j:32 * j + 32, i, :], hT[:, kk % 2, 32 * (kk // 2):32 * (kk // 2) + 32],
                                                    whh[:, kk, j, 0:512], start=False, stop=kk == 7, skip_group_check=True)
                    last.then_inc(sem["rz_full"], 1)
                    for kk in range(8):
                        for j in range(4):
                            last = nc.tensor.matmul(banks[32 * j:32 * j + 32, 2 + i, 0:256], hT[:, kk % 2, 32 * (kk // 2):32 * (kk // 2) + 32],
                                                    whh[:, kk, j, 512:768], start=False, stop=kk == 7, skip_group_check=True)
                    last.then_inc(sem["n_full"], 1)
                    pe.wait_ge(sem["x_slice"], 2 * t + i + 2)
                    x_part(1 - i)
                    pe.wait_ge(sem["h_new"], 2 * t + i + 2)
                    turn_state(i)

            pe.wait_ge(sem["l_ew"], 16)
            pe.wait_ge(sem["h_turned"], S + 1)
            for b in range(B):
                for j in range(2):
                    tokens("a", [(XNT[:, kk, b * S:(b + 1) * S], ew[:, kk, 512 * j:512 * j + 512]) for kk in range(C)], 512)
            pe.wait_ge(sem["pen_in"], 1)
            u, k = open_unit("d")
            full("d", nc.tensor.matmul(u[0:S, 0:1], ones[0:S, 0:S], pen[:, 8:9], start=True, stop=True))

            MARK["F3"] = {key: n.value(key, n.got(key)) for key in ("d_evac", "a_evac")}
            with n.laps(E3, LAP_F3) as e:
                pe.wait_ge(sem["l_gu"], 16 * e + 16)
                for f in range(4):
                    for half in range(2):
                        all_features("a", [(gu3[:, 0, kk, f * P:(f + 1) * P], XNT[:, kk, :]) for kk in range(C)], half)
                        all_features("d", [(gu3[:, 1, kk, f * P:(f + 1) * P], XNT[:, kk, :]) for kk in range(C)], half)
                evacuated("d")
                pe.wait_ge(sem["l_dn"], 16 * e + 16)
                down(h3, dn3, 4)

        @block.scalar
        def _(act):
            n = Count(act, sem)

            def take():
                n.next("a_full")
                bank = RING["a"] + n.parity["a"]
                n.parity["a"] ^= 1
                n.add("a_evac")
                return banks[:, bank, :]

            def evac(dst, rows, cols, func=ACT.Copy, scale=1.0):
                nc.scalar.activation(dst, like(dst, take()[0:rows, 0:cols]), func, scale=scale).then_inc(sem["a_evac"], 1)

            def flat(t, lo, hi):
                return t[:, lo:hi, :].rearrange("p k s -> p (k s)")

            def exps(unit, keys, at):
                n.next("s_max")
                slot = n.parity["s"]
                n.parity["s"] ^= 1
                for i, bank in enumerate(unit):
                    for m in range(len(bank)):
                        col = len(bank) * i + m
                        last = nc.scalar.activation(probs_of(slot, i, keys)[:, m * keys:(m + 1) * keys],
                                                    banks[0:S, 2 * slot + i, m * keys:(m + 1) * keys], ACT.Exp,
                                                    bias=ntop[:, 8 * slot + col:8 * slot + col + 1],
                                                    accum_out=sums[:, at + col:at + col + 1])
                last.then_inc(sem["s_exp"], 1)
                n.add("s_exp")

            def attention(units, keys):
                size = sum(len(bank) for bank in units[0])
                for g, unit in enumerate(units[:2]):
                    exps(unit, keys, size * g)
                for g, unit in enumerate(units):
                    if len(unit) > 1:
                        if keys == S:
                            evac(pT[0:S, 1, 0:4, :], S, 4 * S)
                        else:
                            evac(pT[0:KR, 1, 0:KC, :], KR, KC * S)
                    if g + 2 < len(units):
                        exps(units[g + 2], keys, size * (g + 2))

            def values(width, rings="a"):
                cols = min(width, 512)
                pieces = [(c, j) for c in range(KC) for j in range(0, width, cols)]
                per = 512 // cols
                for i in range(0, len(pieces), per):
                    if rings[i // per % len(rings)] == "a":
                        c, j = pieces[i]
                        m = len(pieces[i:i + per])
                        evac(v[0:KR, c:c + m, j:j + cols], KR, m * cols)

            act.wait_ge(sem["l_wa"], 16)
            with n.laps(B, LAP_A) as lap:
                evac(flat(xnT, 0, 2), P, 2 * S)
                evac(flat(qT, 0, 4), P, 4 * S)
                for j in (0, 512):
                    evac(v[0:S, 0, j:j + 512], S, 512)
                attention(SELF, S)
                for c in (0, 4):
                    evac(flat(oT, c, c + 4), P, 4 * S, ACT.Gelu)
                evac(flat(xnT, 0, 2), P, 2 * S)
                for c in range(C):
                    u = take()
                    nc.scalar.activation(kT[:, c, :], u[:, 0:NK], ACT.Identity, bias=wa("x_bk")[:, c:c + 1]
                                         ).then_inc(sem["a_evac"], 1)
                values(D)
                attention(WHOLE, NK)
                evac(flat(xnT, 0, 2), P, 2 * S)
                n.wait("gate_d", n.add("gate_d"))
                nc.scalar.activation(small[:, 12, 0:1, 0], small[:, 11, 0:1, 0], ACT.Exp).then_inc(sem["gate_e"], 1)
                n.add("gate_d")
                n.add("gate_e")
                evac(gT[0:9, :], 9, S)
                evac(flat(xnT, 0, 2), P, 2 * S)
                u = take()
                nc.scalar.activation(flat(qT, 0, 2), u[:, 0:2 * S], ACT.Copy, scale=0.25)
                nc.scalar.activation(kT[:, 0:2, 0:S], u[:, 2 * S:4 * S].rearrange("p (k s) -> p k s", k=2), ACT.Copy
                                     ).then_inc(sem["a_evac"], 1)
                evac(v[0:S, 0, 0:D], S, D)
                exps(WHOLE[0], S, 0)
                evac(flat(oT, 0, 2), P, 2 * S)
                evac(flat(oT, 4, 6), P, 2 * S)
                evac(flat(xnT, 0, 2), P, 2 * S)
                for c in (1, 3):
                    u = take()
                    nc.scalar.activation(kT[:, c, :], u[:, 0:NK], ACT.Identity, bias=wa("y_bk")[:, c:c + 1]
                                         ).then_inc(sem["a_evac"], 1)
                values(D)
                attention(CROSS, NK)
                evac(flat(oT, 0, 2), P, 2 * S)

            def turned_all():
                for b in range(B):
                    evac(XNT[:, :, b * S:(b + 1) * S], P, 2 * S)

            turned_all()
            act.wait_ge(sem["raw"], 1)
            nc.scalar.activation(small[:, 0:2], small[:, 14:16], ACT.Sigmoid).then_inc(sem["raw"], 1)
            n.wait("gate_d", n.add("gate_d"))
            nc.scalar.activation(small[:, 12, :, 0], small[:, 11, :, 0], ACT.Exp).then_inc(sem["gate_e"], 1)
            n.add("gate_e")
            n.add("d_evac")
            with n.laps(E1, LAP_F1):
                for f in range(8):
                    for half in range(2):
                        evac(h0T[:, f, half * HALF:(half + 1) * HALF], P, HALF, ACT.Gelu)

            with n.laps(B, LAP_B):
                evac(flat(xnT, 0, 2), P, 2 * S)
                evac(v[0:S, 0, 0:D], S, D)
                attention(SELF, S)
                evac(flat(oT, 0, 2), P, 2 * S)
                evac(flat(xnT, 0, 2), P, 2 * S)
                evac(flat(qT, 0, 4), P, 4 * S, scale=0.125)
                for c in (1, 3, 5, 7):
                    evac(kT[:, c, :], P, NK)
                values(1024, "ad")
                attention(CROSS, NK)
                for c in (0, 4):
                    evac(flat(oT, c, c + 4), P, 4 * S)

            turned_all()
            act.wait_ge(sem["l_w2"], 48)
            for f in range(8):
                for half in range(2):
                    if 2 * f + half >= 2:
                        n.wait("d_evac", 2 * f + half - 1)
                    u = take()
                    nc.scalar.activation(silu2[:, half, :], u[:, 0:HALF], ACT.Silu, scale=s2[:, 0, f:f + 1]
                                         ).then_inc(sem["a_evac"], 1)
            for i in range(16):
                dst = h1T if i < 8 else h0T
                for half in range(2):
                    u = take()
                    nc.scalar.activation(dst[:, i % 8, half * HALF:(half + 1) * HALF], u[:, 0:HALF], ACT.Gelu,
                                         scale=s2[:, 2 + i // 8, i % 8:i % 8 + 1]).then_inc(sem["a_evac"], 1)
            n.add("d_evac", 16 + 8)

            with n.laps(B, LAP_C):
                evac(flat(xnT, 0, 2), P, 2 * S)
                evac(v[0:S, 0, 0:D], S, D)
                attention(SELF, S)
                evac(flat(oT, 0, 2), P, 2 * S)
                evac(flat(xnT, 0, 2), P, 2 * S)
                evac(flat(qT, 0, 4), P, 4 * S, scale=0.25)
                for c in (1, 3):
                    evac(kT[:, c, :], P, NK)
                values(D)
                attention(CROSS, NK)
                evac(flat(oT, 0, 2), P, 2 * S)

            turned_all()
            n.add("d_evac")
            with act.Fori(0, S // 2) as t:
                for i in range(2):
                    act.wait_ge(sem["rz_full"], 2 * t + i + 1)
                    act.wait_ge(sem["h_new"], 2 * t + i + 1)
                    nc.scalar.activation(rz[:, :], banks[:, i, :], ACT.Sigmoid).then_inc(sem["rz_done"], 1)
                    act.wait_ge(sem["n_in"], 2 * t + i + 1)
                    nc.scalar.activation(cand[:, :], t1[:, :], ACT.Tanh).then_inc(sem["n_done"], 1)
            for b in range(B):
                if b:
                    act.wait_ge(sem["R_used"], b)
                for j in range(2):
                    evac(ex[:, 512 * j:512 * j + 512], S, 512)
            for i, norms in enumerate((dots[:, 0:2], small[:, 7])):
                act.wait_ge(sem["root_in"], i + 1)
                nc.scalar.activation(norms, norms, ACT.Sqrt).then_inc(sem["root_out"], 1)
            n.wait("gate_d", n.add("gate_d"))
            nc.scalar.activation(small[:, 12, :, 0], small[:, 11, :, 0], ACT.Exp).then_inc(sem["gate_e"], 1)
            n.add("gate_e")
            n.add("d_evac")
            with n.laps(E3, LAP_F3):
                for i in range(8):
                    n.wait("d_evac", i - 1)
                    u = take()
                    nc.scalar.activation(silu3[:, i % 2, :], u[:, 0:HALF], ACT.Silu).then_inc(sem["a_evac"], 1)

        @block.vector
        def _(dve):
            n = Count(dve, sem)
            steps = [0]

            def step(ins):
                steps[0] += 1
                ins.then_inc(sem["v_step"], 1)
                dve.wait_ge(sem["v_step"], steps[0])

            def settle():
                step(nc.vector.memset(idle[:, 0:1], 0.0))

            signals = [0]

            def signal(key, by=1):
                signals[0] += 1
                nc.vector.memset(idle[:, signals[0]:signals[0] + 1], 0.0).then_inc(sem[key], by)

            @contextmanager
            def laps(count, per):
                dve.sem_clear(sem["v_step"])
                steps[0] = 0
                with n.laps(count, per) as lap:
                    yield lap
                    settle()
                    dve.sem_clear(sem["v_step"])
                    steps[0] = 0

            def take():
                n.next("d_full")
                bank = RING["d"] + n.parity["d"]
                n.parity["d"] ^= 1
                n.add("d_evac")
                return banks[:, bank, :]

            def emptied(last):
                last.then_inc(sem["d_evac"], 1)

            def own():
                n.wait("d_evac", n.got("d_evac"))

            def kernel_rows(u, chunks, width=S):
                return u[:, 0:chunks * width].rearrange("p (k s) -> p k s", k=chunks)

            def evac(dst, rows, cols):
                emptied(nc.vector.tensor_copy(dst, like(dst, take()[0:rows, 0:cols])))

            def biased(dst, chunks, bias, scale=1.0):
                u = take()
                emptied(nc.vector.scalar_tensor_tensor(dst, kernel_rows(u, chunks), scale, per_column(bias, chunks, S),
                                                       ALU.mult, ALU.add))

            def inverse_root(y, x, t):
                step(nc.vector.tensor_scalar(x, x, EPS, None, ALU.add))
                step(nc.vector.tensor_scalar(y.bitcast(I32), x.bitcast(I32), 1, None, ALU.arith_shift_right))
                step(nc.vector.tensor_scalar(y.bitcast(I32), y.bitcast(I32), -1.0, float(0x5F3759DF), ALU.mult, ALU.add))
                for _ in range(3):
                    if x.shape[1] == 1:
                        step(nc.vector.scalar_tensor_tensor(t, y, x, y, ALU.mult, ALU.mult))
                    else:
                        step(nc.vector.tensor_tensor(t, y, y, ALU.mult))
                        step(nc.vector.tensor_tensor(t, t, x, ALU.mult))
                    step(nc.vector.tensor_scalar(t, t, -0.5, 1.5, ALU.mult, ALU.add))
                    step(nc.vector.tensor_tensor(y, y, t, ALU.mult))

            def norm():
                step(nc.vector.bn_stats(stats[:, 0, 0:6], xb))
                step(nc.vector.bn_aggr(stats[:, 0, 6:8], stats[:, 0, 0:6]))
                inverse_root(rstd[:, 0:1], stats[:, 0, 7:8], rstd[:, 1:2])
                nc.vector.tensor_scalar(xn, xb, stats[:, 0, 6:7], rstd[:, 0:1], ALU.subtract, ALU.mult
                                        ).then_inc(sem["xn"], 1)
                n.add("xn")

            def maxima(unit, keys, mask=None):
                n.next("s_full")
                slot = n.parity["s"]
                n.parity["s"] ^= 1
                i, m = len(unit), len(unit[0])
                sc = banks[0:S, 2 * slot:2 * slot + i, 0:m * keys]
                if m > 1:
                    sc = sc.rearrange("p i (m k) -> p i m k", m=m)
                if mask is not None:
                    over = mask[0:S, :].unsqueeze(1).unsqueeze(1).to_broadcast([S, i, m, keys])
                    step(nc.vector.tensor_tensor(sc, sc, over, ALU.add))
                top = ntop[:, 8 * slot:8 * slot + i * m]
                nc.vector.tensor_reduce(top if m == 1 else top.rearrange("p (i m) -> p i m", i=i), sc, AX, ALU.max, negate=True
                                        ).then_inc(sem["s_max"], 1)
                return slot

            def heads_out(g, unit, dv):
                u = take()
                size = sum(len(bank) for bank in unit)
                if size == 8:
                    dst = o[:, 0:H * dv].rearrange("p (m j d) -> p j m d", m=4, j=4)[:, 2 * g:2 * g + 2]
                    src = u[0:S, 0:8 * dv].rearrange("p (i m d) -> p i m d", i=2, m=4)
                    over = rsum[:, 8 * g:8 * g + 8].rearrange("p (i m) -> p i m", i=2).unsqueeze(3).to_broadcast([S, 2, 4, dv])
                else:
                    dst = o[:, 2 * g * dv:(2 * g + 2) * dv].rearrange("p (i d) -> p i d", i=2)
                    src = u[0:S, 0:2 * dv].rearrange("p (i d) -> p i d", i=2)
                    over = rsum[:, 2 * g:2 * g + 2].unsqueeze(2).to_broadcast([S, 2, dv])
                emptied(nc.vector.tensor_tensor(dst, src, over, ALU.mult))

            def attention(units, keys, dv, mask=None, out=heads_out):
                size = sum(len(bank) for bank in units[0])
                for unit in units[:2]:
                    maxima(unit, keys, mask)
                for g, unit in enumerate(units):
                    n.add("s_exp")
                    n.wait("s_exp", n.got("s_exp"))
                    step(nc.vector.reciprocal(rsum[:, size * g:size * (g + 1)], sums[:, size * g:size * (g + 1)]))
                    if keys == S:
                        evac(pT[0:S, 0, 0:4, :], S, 4 * S)
                    else:
                        evac(pT[0:KR, 0, 0:KC, :], KR, KC * S)
                    if g + 2 < len(units):
                        maxima(units[g + 2], keys, mask)
                    out(g, unit, dv)

            def add_unit():
                u = take()
                emptied(nc.vector.tensor_tensor(xb, xb, u[0:S, 0:D], ALU.add))
                own()

            def top_two(nb, value, score, gate, ready):
                t = lambda i: small[:, i, 0:nb, :]
                col = lambda i: small[:, i, 0:nb, 0:1]
                wide_ = lambda a: a.to_broadcast([S, nb, E])
                rank = cst("rank")[0:S, :].unsqueeze(1).to_broadcast([S, nb, E])
                hot = (8, 9)
                for r in range(2):
                    step(nc.vector.tensor_reduce(col(2), score, AX, ALU.max))
                    step(nc.vector.tensor_tensor(t(3), score, wide_(col(2)), ALU.is_equal))
                    step(nc.vector.tensor_tensor(t(4), t(3), rank, ALU.mult))
                    step(nc.vector.tensor_reduce(col(5), t(4), AX, ALU.max))
                    step(nc.vector.tensor_tensor(t(hot[r]), t(4), wide_(col(5)), ALU.is_equal))
                    step(nc.vector.tensor_tensor(t(6), t(hot[r]), value, ALU.mult))
                    step(nc.vector.tensor_reduce(col(7 if r == 0 else 10), t(6), AX, ALU.add))
                    if r == 0:
                        step(nc.vector.scalar_tensor_tensor(score, t(hot[0]), MASKED, score, ALU.mult, ALU.add))
                nc.vector.tensor_tensor(col(11), col(10), col(7), ALU.subtract).then_inc(sem["gate_d"], 1)
                n.add("gate_d")
                n.next("gate_e")
                step(nc.vector.tensor_scalar(col(2), col(12), 1.0, None, ALU.add))
                step(nc.vector.reciprocal(col(5), col(2)))
                step(nc.vector.tensor_tensor(col(7), col(12), col(5), ALU.mult))
                step(nc.vector.tensor_tensor(t(3), t(8), wide_(col(5)), ALU.mult))
                step(nc.vector.tensor_tensor(t(4), t(9), wide_(col(7)), ALU.mult))
                ready(nc.vector.tensor_tensor(gate, t(3), t(4), ALU.add))

            nc.vector.memset(gate_row[:, :], 1.0).then_inc(sem["d_evac"], 2)
            step(nc.vector.memset(probs_x[:, :, :, :], 0.0))
            nc.vector.memset(small[:, :, :, :], 0.0).then_inc(sem["a_evac"], 2)
            dve.wait_ge(sem["l_x"], 16)
            dve.wait_ge(sem["l_wa"], 16)
            dve.wait_ge(sem["l_const"], 16)
            step(nc.vector.tensor_scalar(bq4[:, 0:4], wa("y_bq")[:, 0:4], 0.25, None, ALU.mult))
            nc.vector.memset(stats[:, :, :], 0.0).then_inc(sem["s_exp"], 2)
            with laps(B, LAP_A) as lap:
                step(nc.vector.tensor_copy(xb, X[:, bass.ds(lap * D, D)]))
                norm()
                biased(kT[:, 0:4, 0:S], 4, wa("a_bk"))
                attention(SELF, S, 64, cst("causal"))
                n.wait("xn", n.got("xn"))
                step(nc.vector.tensor_tensor(xb, xb, xn, ALU.add))
                add_unit()
                norm()
                biased(qT[:, 0:2, :], 2, wa("x_bq"))

                def onto_x(g, unit, dv):
                    emptied(nc.vector.scalar_tensor_tensor(xb, take()[0:S, 0:D], rsum[:, 0:1], xb, ALU.mult, ALU.add))
                attention(WHOLE, NK, D, None, onto_x)
                own()
                norm()
                u = take()
                emptied(nc.vector.tensor_copy(small[:, 0, 0, :], u[0:S, 0:E]))
                own()
                step(nc.vector.tensor_copy(small[:, 1, 0, :], small[:, 0, 0, :]))

                def ready(last):
                    last.then_inc(sem["gate_d"], 1)
                    n.next("gate_d")
                top_two(1, small[:, 0, 0:1, :], small[:, 1, 0:1, :], gate_row[:, 0:E].unsqueeze(1), ready)
                for j in range(0, 9, 2):
                    u = take()
                    m = min(2, 9 - j)
                    for i in range(m):
                        last = nc.vector.scalar_tensor_tensor(xb, u[0:S, i * D:(i + 1) * D], gate_row[:, j + i:j + i + 1], xb,
                                                              ALU.mult, ALU.add)
                        if i + 1 < m:
                            step(last)
                    emptied(last)
                    own()
                add_unit()
                norm()
                slot = maxima(WHOLE[0], S)
                n.next("s_exp")
                step(nc.vector.reciprocal(rsum[:, 0:1], sums[:, 0:1]))
                nc.vector.tensor_scalar(probs_s[:, slot, 0, 0:S], probs_s[:, slot, 0, 0:S], rsum[:, 0:1], None, ALU.mult
                                        ).then_inc(sem["xn"], 1)
                n.add("xn")
                evac(pT[0:S, 0, 0, :], S, S)
                add_unit()
                norm()
                biased(qT[:, 0:4, :], 4, bq4, 0.25)
                for c in (0, 2):
                    emptied(nc.vector.tensor_scalar(kT[:, c, :], take()[:, 0:NK], wa("y_bk")[:, c:c + 1], None, ALU.add))
                attention(CROSS, NK, HD)
                add_unit()
                settle()
                step(nc.vector.tensor_copy(X[:, bass.ds(lap * D, D)], xb))

            def norm_all():
                for b in range(B):
                    last = nc.vector.bn_stats(stats[:, b, 0:6], X[:, b * D:(b + 1) * D])
                step(last)
                for b in range(B):
                    last = nc.vector.bn_aggr(stats[:, b, 6:8], stats[:, b, 0:6])
                step(last)
                inverse_root(rstd[:, 0:B], stats[:, :, 7], rstd[:, B:])
                for b in range(B):
                    last = nc.vector.tensor_scalar(XN[:, b * D:(b + 1) * D], X[:, b * D:(b + 1) * D], stats[:, b, 6:7],
                                                   rstd[:, b:b + 1], ALU.subtract, ALU.mult)
                last.then_inc(sem["xn"], 1)
                n.next("xn")
                n.add("a_evac", B)

            def phase_over():
                signal("phase")

            phase_over()
            norm_all()
            step(nc.vector.tensor_tensor(X[:, :], X[:, :], XN[:, :], ALU.add))
            dve.wait_ge(sem["l_rb"], 32)
            u = take()
            raw = u[0:S, 0:B * E].rearrange("p (b e) -> p b e", b=B)
            step(nc.vector.tensor_copy(small[:, 14], raw))
            emptied(nc.vector.tensor_tensor(small[:, 15], raw, rbias[:, :].unsqueeze(1).to_broadcast([S, B, E]), ALU.add))
            n.wait("d_evac", n.got("d_evac"))
            nc.vector.memset(gates[:, E:E1, :], 1.0).then_inc(sem["raw"], 1)
            dve.wait_ge(sem["raw"], 2)
            top_two(B, small[:, 0], small[:, 1], gates[:, 0:E, :].rearrange("p e b -> p b e"), step)

            def experts(lap_gate):
                step(nc.vector.tensor_copy(gate_now[:, :].unsqueeze(1), gates[:, bass.ds(lap_gate, 1), :]))

            def weighted():
                for b in range(B):
                    xs = X[:, b * D:(b + 1) * D]
                    emptied(nc.vector.scalar_tensor_tensor(xs, take()[0:S, 0:D], gate_now[:, b:b + 1], xs, ALU.mult, ALU.add))

            with laps(E1, LAP_F1) as e:
                experts(e)
                weighted()
                own()

            phase_over()
            dve.wait_ge(sem["l_wb"], 16)
            step(nc.vector.tensor_scalar(bq4[:, 4:8], wb("bq"), 0.25, None, ALU.mult))
            with laps(B, LAP_B) as lap:
                step(nc.vector.tensor_copy(xb, X[:, bass.ds(lap * D, D)]))
                norm()
                biased(qT[:, 0:4, :], 4, bq4[:, 4:8], 0.25)
                biased(kT[:, 0:4, 0:S], 4, wb("bk"))
                attention(SELF, S, HD, cst("causal"))
                add_unit()
                norm()
                emptied(nc.vector.tensor_scalar(qT[:, 4:8, :], kernel_rows(take(), 4), 0.125, None, ALU.mult))
                for c in (0, 2, 4, 6):
                    evac(kT[:, c, :], P, NK)
                for i in (1, 3, 5):
                    evac(v[0:KR, i // 2, 512:1024], KR, 512)
                attention(WIDE, NK, 64)
                add_unit()
                settle()
                step(nc.vector.tensor_copy(X[:, bass.ds(lap * D, D)], xb))

            phase_over()
            norm_all()
            dve.wait_ge(sem["l_w2"], 48)
            for f in range(8):
                for half in range(2):
                    n.next("a_evac")
                    emptied(nc.vector.scalar_tensor_tensor(h0T[:, f, half * HALF:(half + 1) * HALF], take()[:, 0:HALF],
                                                           s2[:, 1, f:f + 1], silu2[:, half, :], ALU.mult, ALU.mult))
            n.add("a_evac", 32)
            dve.wait_ge(sem["l_w3"], 32)
            for b in range(B):
                xs = X[:, b * D:(b + 1) * D]
                emptied(nc.vector.tensor_tensor(y2[0:S, b % 2, :], take()[0:S, 0:D], w3s[0:S, :], ALU.mult))
                own()
                step(nc.vector.tensor_tensor(xs, xs, y2[0:S, b % 2, :], ALU.add))

            def rotated(dst, cos, sin):
                for name, t in ((cos, rope_t), (sin, rope_u)):
                    emptied(nc.vector.tensor_tensor(t, kernel_rows(take(), 4), cst(name).unsqueeze(1).to_broadcast([P, 4, S]),
                                                    ALU.mult))
                own()
                nc.vector.tensor_tensor(dst, rope_t, rope_u, ALU.add).then_inc(sem["rotated"], 1)
                n.next("rotated")

            with laps(B, LAP_C) as lap:
                step(nc.vector.tensor_copy(xb, X[:, bass.ds(lap * D, D)]))
                norm()
                rotated(qT[:, 0:4, :], "cos", "sin")
                rotated(kT[:, 0:4, 0:S], "cos4", "sin4")
                attention(SELF, S, HD, cst("window"))
                add_unit()
                norm()
                for c in (0, 2):
                    evac(kT[:, c, :], P, NK)
                attention(CROSS, NK, HD)
                add_unit()
                settle()
                step(nc.vector.tensor_copy(X[:, bass.ds(lap * D, D)], xb))

            phase_over()
            norm_all()
            step(nc.vector.memset(mean[:, :, :], 0.0))
            n.wait("a_evac", n.got("a_evac"))
            for kk in range(C):
                last = nc.vector.tensor_reduce(mean[:, kk, 0:B], XNT[:, kk, :].rearrange("p (b s) -> p b s", b=B), AX, ALU.add)
            step(last)
            nc.vector.tensor_scalar(mean[:, :, :], mean[:, :, :], 1.0 / S, None, ALU.mult).then_inc(sem["zeroed"], 1)
            emptied(nc.vector.tensor_copy(h[:, 1, :], take()[:, 0:256]))
            own()
            signal("h_new")
            for i in range(2):
                signal("l_h%d" % i, 64)
            dve.wait_ge(sem["h_back"], 1)
            nc.vector.tensor_copy(hT[:, :, :].rearrange("p c q -> p (c q)"), banks[:, 4, 0:256]).then_inc(sem["h_turned"], 1)
            dve.sem_clear(sem["v_step"])
            steps[0] = 0
            with dve.Fori(0, S // 2) as t:
                for i in range(2):
                    dve.wait_ge(sem["rz_done"], 2 * t + i + 1)
                    step(nc.vector.tensor_tensor(zh[:, :], rz[:, 256:512], h[:, 1 - i, :], ALU.mult))
                    step(nc.vector.tensor_scalar(omz[:, :], rz[:, 256:512], -1.0, 1.0, ALU.mult, ALU.add))
                    dve.wait_ge(sem["n_full"], 2 * t + i + 1)
                    step(nc.vector.tensor_tensor(t1[:, :], rz[:, 0:256], banks[:, 2 + i, 0:256], ALU.mult))
                    nc.vector.tensor_tensor(t1[:, :], t1[:, :], banks[:, 2 + i, 256:512], ALU.add).then_inc(sem["n_in"], 1)
                    dve.wait_ge(sem["n_done"], 2 * t + i + 1)
                    step(nc.vector.tensor_tensor(cand[:, :], cand[:, :], omz[:, :], ALU.mult))
                    dve.wait_ge(sem["l_h%d" % i], 64 * t + 64)
                    nc.vector.tensor_tensor(h[:, i, :], cand[:, :], zh[:, :], ALU.add).then_inc(sem["h_new"], 1)
                    dve.wait_ge(sem["h_back"], 2 * t + i + 2)
                    nc.vector.tensor_copy(hT[:, :, :].rearrange("p c q -> p (c q)"), banks[:, 4, 0:256]).then_inc(sem["h_turned"], 1)
                settle()
                dve.sem_clear(sem["v_step"])
                steps[0] = 0

            eight = lambda a: a.rearrange("p (e d) -> p e d", d=ED)
            dve.wait_ge(sem["h_turned"], S + 1)
            for b in range(B):
                dve.wait_ge(sem["l_R%d" % (b % 2)], 16 * (b // 2 + 1))
                rb = R[:, b % 2, :]
                step(nc.vector.tensor_tensor(prod, rb, rb, ALU.mult))
                step(nc.vector.tensor_reduce(dots[:, 0, b, :], eight(prod), AX, ALU.add))
                for s_ in range(1, E):
                    m = E - s_
                    step(nc.vector.tensor_tensor(prod[:, 0:m * ED], rb[:, 0:m * ED], rb[:, s_ * ED:], ALU.mult))
                    step(nc.vector.tensor_reduce(gram[:, b, s_:s_ + (m - 1) * (E + 1) + 1:E + 1], eight(prod[:, 0:m * ED]), AX, ALU.add))
                    step(nc.vector.tensor_copy(gram[:, b, E * s_:E * s_ + (m - 1) * (E + 1) + 1:E + 1], gram[:, b, s_:s_ + (m - 1) * (E + 1) + 1:E + 1]))
                n.wait("a_evac", n.add("a_evac", 2))
                step(nc.vector.tensor_tensor(prod, ex, ex, ALU.mult))
                step(nc.vector.tensor_reduce(dots[:, 1, b, :], eight(prod), AX, ALU.add))
                nc.vector.tensor_tensor(prod, ex, rb, ALU.mult).then_inc(sem["R_used"], 1)
                dve.wait_ge(sem["R_used"], b + 1)
                step(nc.vector.tensor_reduce(dots[:, 2, b, :], eight(prod), AX, ALU.add))
            t = lambda i: small[:, i]
            step(nc.vector.tensor_copy(gram[:, :, 0:E * E:E + 1], dots[:, 0]))
            signal("root_in")
            dve.wait_ge(sem["root_out"], 1)
            step(nc.vector.tensor_scalar(t(2), dots[:, 0], 1e-12, None, ALU.max))
            step(nc.vector.reciprocal(t(3), t(2)))
            step(nc.vector.tensor_tensor(t(4), dots[:, 0], t(3), ALU.mult))
            step(nc.vector.tensor_scalar(t(4), t(4), 1e-8, None, ALU.max))
            step(nc.vector.tensor_scalar(t(5), dots[:, 1], 1e-8, None, ALU.max))
            step(nc.vector.tensor_tensor(t(4), t(4), t(5), ALU.mult))
            step(nc.vector.reciprocal(t(5), t(4)))
            step(nc.vector.tensor_tensor(t(6), dots[:, 2], t(3), ALU.mult))
            step(nc.vector.tensor_tensor(t(6), t(6), t(5), ALU.mult))
            step(nc.vector.tensor_scalar(t(6), t(6), -1.0, 1.0, ALU.mult, ALU.add))
            for b in range(B):
                gb = gram[:, b, :].rearrange("p (e f) -> p e f", e=E)
                step(nc.vector.tensor_tensor(gb, gb, t(3)[:, b, :].unsqueeze(2).to_broadcast([S, E, E]), ALU.mult))
                step(nc.vector.tensor_tensor(gb, gb, t(3)[:, b, :].unsqueeze(1).to_broadcast([S, E, E]), ALU.mult))
            step(nc.vector.tensor_scalar(gram[:, :, 0:E * E:E + 1], gram[:, :, 0:E * E:E + 1], -1.0, None, ALU.add))
            step(nc.vector.tensor_tensor(gsq, gram, gram, ALU.mult))
            g3 = gsq.rearrange("p b (e f) -> p (b e) f", e=E)
            t7 = t(7).rearrange("p b e -> p (b e)")
            nc.vector.tensor_reduce(t7, g3, AX, ALU.add).then_inc(sem["root_in"], 1)
            dve.wait_ge(sem["root_out"], 2)
            step(nc.vector.tensor_scalar(t(7), t(7), 1e-12, None, ALU.max))
            step(nc.vector.reciprocal(t(7), t(7)))
            gr = gram.rearrange("p b (e f) -> p (b e) f", e=E)
            step(nc.vector.tensor_tensor(gr, gr, t7.unsqueeze(2).to_broadcast([S, B * E, E]), ALU.mult))
            step(nc.vector.tensor_tensor(gsq, gram, gram, ALU.mult))
            nc.vector.tensor_reduce(pen[:, 8:9], gsq.rearrange("p b q -> p (b q)"), AX, ALU.add).then_inc(sem["pen_in"], 1)
            emptied(nc.vector.tensor_scalar(pen[:, 9:10], take()[0:S, 0:1], 1.0 / T, 1.0, ALU.mult, ALU.add))
            own()
            step(nc.vector.tensor_scalar(t(0), t(6), pen[:, 9:10], None, ALU.mult))
            step(nc.vector.tensor_copy(t(1), t(0)))
            top_two(B, small[:, 0], small[:, 1], gates[:, 0:E, :].rearrange("p e b -> p b e"), step)
            phase_over()
            with laps(E3, LAP_F3) as e:
                experts(e)
                for f in range(4):
                    for half in range(2):
                        n.next("a_evac")
                        emptied(nc.vector.tensor_tensor(h3[:, f, half * HALF:(half + 1) * HALF], take()[:, 0:HALF],
                                                        silu3[:, half, :], ALU.mult))
                weighted()
                own()
            phase_over()

        @block.gpsimd
        def _(pool):
            pool.wait_ge(sem["zeroed"], 1)
            nc.gpsimd.memset(xt[:, :, :, :], 0.0).then_inc(sem["xt_zero"], 1)
            pool.wait_ge(sem["xt_zero"], 1)
            by_s = XNT[:, :, :].rearrange("p k (b s) -> p k b s", b=B)
            nc.gpsimd.tensor_copy(xt[:, 0, :, 0:B], by_s[:, :, :, 0]).then_inc(sem["x_slice"], 1)
            nc.gpsimd.tensor_copy(xt[:, 1, :, 0:B], by_s[:, :, :, 1]).then_inc(sem["x_slice"], 1)
            with pool.Fori(0, S // 2 - 1) as t:
                for i in range(2):
                    pool.wait_ge(sem["x_used"], 2 * t + i + 1)
                    nc.gpsimd.tensor_copy(xt[:, i, :, 0:B], by_s[:, :, :, bass.ds(2 * t + i + 2, 1)].rearrange("p k b s -> p k (b s)")
                                          ).then_inc(sem["x_slice"], 1)
            pool.wait_ge(sem["x_used"], S - 1)
            nc.gpsimd.tensor_copy(xt[:, 0, :, 0:B], by_s[:, :, :, S - 1]).then_inc(sem["x_slice"], 1)

        @block.sync
        def _(sp):
            def load(dst, name, s, n=16):
                sp.dma_start(dst, dram[name]).then_inc(sem[s], n)

            load(const[:, :], "const", "l_const")
            sp.dma_start(X[:, :].rearrange("s (b d) -> s b d", b=B), dram["x"].rearrange("b s d -> s b d")).then_inc(sem["l_x"], 16)
            load(arena[:, AT_WA:AT_WA + WA_N], "WA", "l_wa")
            ctxs = dram["ctxT"].rearrange("(b p) k -> b p k", b=B)
            n = Count(sp, sem)

            def context(lap, first):
                sp.dma_start(ctx_now[:, :], ctxs[bass.ds(lap, 1)].rearrange("o p k -> (o p) k")).then_inc(sem["l_ctx"], 16)

            sp.dma_start(cent[:, :], dram["centroids"]).then_inc(sem["l_rb"], 16)
            sp.dma_start(rbias[:, :], dram["routing_bias"].partition_broadcast(S)).then_inc(sem["l_rb"], 16)
            turned_rows = turned.rearrange("b (c p s) -> b p c s", c=C, p=P)
            turned_back = turned.rearrange("b (s d) -> b s d", s=S)
            with n.laps(B, LAP_A) as lap:
                n.wait("s_exp", 0)
                context(lap, 0)
                n.wait("a_evac", MARK["turn"])
                sp.dma_start(turned_rows[bass.ds(lap, 1)].rearrange("o p c s -> (o p) c s"), oT[:, 0:2, :]).then_inc(sem["o_turn"], 16)
                sp.wait_ge(sem["o_turn"], 16 * lap + 16)
                sp.dma_start(o[:, 0:D], turned_back[bass.ds(lap, 1)].rearrange("o s d -> (o s) d")).then_inc(sem["turn"], 16)
            sp.wait_ge(sem["phase"], 1)
            load(arena[:, AT_WB:AT_WB + WB_N], "WB", "l_wb")
            load(arena[:, AT_WC:AT_WC + WC_N], "WC", "l_wc")
            fcs = dram["fc"].rearrange("(e p) n -> e p n", e=E1)
            pjs = dram["pj"].rearrange("(e p) n -> e p n", e=E1)
            with sp.Fori(0, E1) as e:
                sp.wait_ge(sem["a_evac"], e * LAP_F1["a_evac"] + MARK["F1"]["a_evac"])
                sp.dma_start(arena[:, AT_FW:AT_FW + 2048], fcs[bass.ds(e, 1)].rearrange("o p n -> (o p) n")).then_inc(sem["l_fc"], 16)
                sp.wait_ge(sem["d_evac"], e * LAP_F1["d_evac"] + MARK["F1"]["d_evac"])
                sp.dma_start(arena[:, AT_FW + 2048:AT_FW + 4096], pjs[bass.ds(e, 1)].rearrange("o p n -> (o p) n")).then_inc(sem["l_pj"], 16)
            sp.wait_ge(sem["phase"], 2)
            load(arena[:, AT_FW:AT_FW + 2048], "w1", "l_w2")
            load(arena[:, AT_FW + 2048:AT_FW + 4096], "w2", "l_w2")
            with sp.Fori(0, B) as lap:
                sp.wait_ge(sem["s_exp"], lap * LAP_B["s_exp"] + n.before["s_exp"])
                context(lap, B)
            sp.wait_ge(sem["phase"], 3)
            load(arena[:, 6400:6432], "s2", "l_w2")
            load(arena[:, 4096:6144], "w3", "l_w3")
            sp.dma_start(w3s[0:S, :], dram["w3s"].partition_broadcast(S)).then_inc(sem["l_w3"], 16)
            hh_ = dram["hh"].rearrange("(i p) n -> i p n", i=16)
            for i in range(16):
                if i >= 4:
                    sp.wait_ge(sem["a_evac"], MARK["slots"][i - 4])
                sp.dma_start(arena[:, 1024 * (i % 4):1024 * (i % 4) + 1024], hh_[i]).then_inc(sem["l_s%d" % (i % 4)], 16)
            with sp.Fori(0, B) as lap:
                sp.wait_ge(sem["s_exp"], lap * LAP_C["s_exp"] + n.before["s_exp"] + B * LAP_B["s_exp"])
                context(lap, 2 * B)
            sp.wait_ge(sem["phase"], 4)
            load(arena[:, 0:24576], "whh", "l_gru")
            load(arena[:, 24576:30720], "wih", "l_gru")
            load(arena[:, AT_WORK2:AT_WORK2 + 2048], "ctx_w", "l_cw")
            load(cb[0:1, :], "ctx_b", "l_cw")
            by_group = history.rearrange("b s (j u) -> s j b u", j=4)
            with sp.Fori(0, S // 2) as t:
                for i in range(2):
                    sp.wait_ge(sem["h_new"], 2 * t + i + 2)
                    for j in range(4):
                        sp.dma_start(by_group[bass.ds(2 * t + i, 1), j].rearrange("o b u -> (o b) u"), h[32 * j:32 * j + B, i, :]
                                     ).then_inc(sem["l_h%d" % i], 16)
            sp.wait_ge(sem["h_turned"], S + 1)
            load(arena[:, 0:2048], "ew", "l_ew")
            sp.wait_ge(sem["l_h0"], 64 * (S // 2 + 1))
            sp.wait_ge(sem["l_h1"], 64 * (S // 2 + 1))
            for b in range(B):
                if b >= 2:
                    sp.wait_ge(sem["R_used"], b - 1)
                sp.dma_start(R[:, b % 2, :], history[b]).then_inc(sem["l_R%d" % (b % 2)], 16)
            gus = dram["gu"].rearrange("(e p) n -> e p n", e=E3)
            dns = dram["dn"].rearrange("(e p) n -> e p n", e=E3)
            with sp.Fori(0, E3) as e:
                sp.wait_ge(sem["a_evac"], e * LAP_F3["a_evac"] + MARK["F3"]["a_evac"])
                sp.wait_ge(sem["d_evac"], e * LAP_F3["d_evac"] + MARK["F3"]["d_evac"] - 8)
                sp.dma_start(arena[:, AT_FW:AT_FW + 2048], gus[bass.ds(e, 1)].rearrange("o p n -> (o p) n")).then_inc(sem["l_gu"], 16)
                sp.wait_ge(sem["d_evac"], e * LAP_F3["d_evac"] + MARK["F3"]["d_evac"])
                sp.dma_start(arena[:, AT_FW + 2048:AT_FW + 3072], dns[bass.ds(e, 1)].rearrange("o p n -> (o p) n")).then_inc(sem["l_dn"], 16)
            sp.wait_ge(sem["phase"], 6)
            sp.dma_start(out.rearrange("b s d -> s b d"), X[:, :].rearrange("s (b d) -> s b d", b=B)).then_inc(sem["l_out"], 16)
            sp.wait_ge(sem["l_out"], 16)


def rows_first(w):
    k, m = w.shape
    return np.ascontiguousarray(w.reshape(k // P, P, m).transpose(1, 0, 2).reshape(P, -1))


def pad_heads(w):
    w = w.reshape(-1, H, HD)
    out = np.zeros((w.shape[0], H, 32), w.dtype)
    out[:, :, :HD] = w
    return out.reshape(w.shape[0], H * 32)


def columns(bias):
    return np.ascontiguousarray(bias.reshape(-1, P).T)


def pack(where, total, parts):
    out = np.zeros((P, total), np.float32)
    for name, (at, m) in where.items():
        a = parts[name]
        a = a.reshape(1, -1) if a.ndim == 1 else a
        assert a.shape[1] == m, (name, a.shape, m)
        out[:a.shape[0], at:at + m] = a
    return out


def constants():
    i = np.arange(S)
    inv = (1.0 / np.float32(10000.0) ** (np.arange(0, HD, 2, dtype=np.float32) / HD)).astype(np.float32)
    ang = np.arange(S, dtype=np.float32)[:, None] * inv
    cos, sin = np.cos(ang), np.sin(ang)
    rot_c, rot_s = np.zeros((P, S), np.float32), np.zeros((P, S), np.float32)
    for q in range(4):
        for d in range(HD):
            rot_c[32 * q + d] = cos[:, d // 2]
            rot_s[32 * q + d] = (1 if d % 2 else -1) * sin[:, d // 2]
    return dict(
        ident=np.eye(P, dtype=np.float32), rank=np.tile(E - np.arange(E, dtype=np.float32), (P, 1)),
        causal=np.where(i[None] <= i[:, None], 0, MASKED).astype(np.float32),
        window=np.where(abs(i[None] - i[:, None]) <= 32, 0, MASKED).astype(np.float32),
        cos=rot_c, sin=rot_s, cos4=rot_c / 4, sin4=rot_s / 4, ones=np.ones((P, P), np.float32),
        ones8=np.tile((np.arange(32) < B).astype(np.float32), (P, 1)))


def layouts(a):
    L0a, L0x, L0f = (lambda s: a["L0_attn_" + s]), (lambda s: a["L0_xattn_" + s]), (lambda s: a["L0_ffn_" + s])
    y = lambda s: a["L1_xattn_" + s]
    qkv1 = a["L1_attn_w_qkv"].T
    pick = np.eye(D, dtype=np.float32)
    experts0 = np.concatenate([w.T for w in L0f("W_experts")] + [L0f("W_shared").T], 1)
    wa = dict(
        a_pick=rows_first(pad_heads(pick)), a_wk=rows_first(pad_heads(L0a("Wk"))), a_wv=rows_first(L0a("Wv")),
        a_wf=rows_first(L0a("Wf")), a_bk=columns(pad_heads(L0a("bk")[None])[0]),
        x_wq=rows_first(L0x("Wq")), x_wk=L0x("Wk"), x_wv=L0x("Wv"), x_bq=columns(L0x("bq")), x_bk=columns(L0x("bk")),
        f_w=rows_first(experts0), f_router=rows_first(L0f("W_router").T),
        f_b=np.concatenate([L0f("b_experts"), L0f("b_shared")[None]], 0),
        s_wqkv=rows_first(qkv1), s_wo=rows_first(a["L1_attn_w_proj"].T),
        y_wq=rows_first(pad_heads(y("Wq"))), y_wk=pad_heads(y("Wk")), y_wv=y("Wv"), y_wo=rows_first(y("Wo")),
        y_bq=columns(pad_heads(y("bq")[None])[0]), y_bk=columns(pad_heads(y("bk")[None])[0]),
        r_a_bv=L0a("bv"), r_a_bf=L0a("bf"), r_x_bv=L0x("bv"), r_router=L0f("b_router"),
        r_s_bo=a["L1_attn_b_proj"], r_y_bv=y("bv"), r_y_bo=y("bo"))
    w, bb = a["L2_attn_w_qkv"], a["L2_attn_b_qkv"]
    z = lambda s: a["L2_xattn_" + s]
    wb = dict(
        wq=rows_first(pad_heads(w[:, :D])), wk=rows_first(pad_heads(w[:, D:2 * D])), wv=rows_first(w[:, 2 * D:]),
        wo=rows_first(a["L2_attn_w_proj"]), bq=columns(pad_heads(bb[None, :D])[0]), bk=columns(pad_heads(bb[None, D:2 * D])[0]),
        x_wq=rows_first(z("Wq")), x_wk=z("Wk"), x_wv=z("Wv"), x_wo=rows_first(z("Wo")),
        r_bv=bb[2 * D:], r_bo=a["L2_attn_b_proj"], r_x_bo=z("bo"))
    swap = np.arange(D).reshape(-1, 2)[:, ::-1].reshape(-1)
    q3 = a["L3_attn_Wq"]
    each = lambda m: np.repeat(m.reshape(D, 4, HD), 4, axis=1).reshape(D, D)
    k3, v3 = each(a["L3_attn_Wk"]), each(a["L3_attn_Wv"])
    kv = a["L3_xattn_Wkv"].T
    wc = dict(
        wq=rows_first(pad_heads(q3)), wqs=rows_first(pad_heads(q3[:, swap])), wk=rows_first(pad_heads(k3)),
        wks=rows_first(pad_heads(k3[:, swap])), wv=rows_first(v3), wo=rows_first(a["L3_attn_Wo"]),
        x_wq=rows_first(pad_heads(a["L3_xattn_Wq"].T)), x_wk=pad_heads(kv[:, :D]), x_wv=kv[:, D:],
        x_wo=rows_first(a["L3_xattn_Wo"].T))
    context = np.zeros((B, CTX, NKP), np.float32)
    context[:, :, :NK] = a["ctx_512"].transpose(0, 2, 1)
    stack = lambda ws: np.concatenate([rows_first(m.T) for m in ws], 0)
    g = lambda m: np.ascontiguousarray(
        m.T.reshape(-1, P, 3, 4, 256).transpose(1, 0, 3, 2, 4).reshape(P, -1))
    f = lambda s: a["L2_ffn_" + s]
    hidden = lambda m: np.concatenate([rows_first(m.T[:, o * P:(o + 1) * P]) for o in range(8)], 0)
    t = lambda s: a["L3_ffn_" + s]
    gate_up = [np.concatenate([rows_first(gw.T), rows_first(uw.T)], 1)
               for gw, uw in list(zip(t("gate_w"), t("up_w"))) + [(t("shared_gate_w"), t("shared_up_w"))]]
    return dict(
        const=pack(CONST, CONST_N, constants()), x=a["x"], ctxT=context.reshape(B * CTX, NKP),
        WA=pack(WA, WA_N, wa), WB=pack(WB, WB_N, wb), WC=pack(WC, WC_N, wc),
        centroids=rows_first(a["L1_ffn_centroids"].T), routing_bias=a["L1_ffn_routing_bias"],
        fc=stack(list(a["L1_ffn_Wfc_r"]) + list(a["L1_ffn_Wfc_sh"])),
        pj=stack(list(a["L1_ffn_Wproj_r"]) + list(a["L1_ffn_Wproj_sh"])),
        w1=rows_first(f("w1_w").T), w2=rows_first(f("w2_w").T), w3=rows_first(f("w3_w").T), w3s=f("w3_s"),
        s2=np.concatenate([columns(f(s)) for s in ("w1_s", "w2_s", "h1_s", "h2_s")], 1),
        hh=np.concatenate([hidden(f("h1_w")), hidden(f("h2_w"))], 0),
        whh=g(t("gru_w_hh")), wih=g(t("gru_w_ih")), ctx_w=rows_first(t("ctx_w").T), ctx_b=t("ctx_b")[None],
        ew=rows_first(t("expr_w").T), gu=np.concatenate(gate_up, 0),
        dn=stack(list(t("down_w")) + [t("shared_down_w")]))


def kernel(**inputs):
    import concourse.bacc as _bacc
    from concourse.bass_utils import run_bass_kernel_spmd as _run

    nc = _bacc.Bacc("TRN2", target_bir_lowering=False, num_devices=1)
    arrays = {name: np.ascontiguousarray(m) for name, m in layouts({k: np.asarray(m) for k, m in inputs.items()}).items()}
    dram = {name: nc.dram_tensor(name, m.shape, F32, kind="ExternalInput").ap() for name, m in arrays.items()}
    out = nc.dram_tensor("out", (B, S, D), F32, kind="ExternalOutput").ap()
    build(nc, dram, out)
    return _run(nc, [arrays], core_ids=[0]).results[0]["out"]
```

```python
from contextlib import ExitStack, contextmanager

import numpy as np

import concourse.bass as bass
from concourse import mybir

F32 = mybir.dt.float32
I32 = mybir.dt.int32
ACT = mybir.ActivationFunctionType
ALU = mybir.AluOpType
AX = mybir.AxisListType.X

B, S, D, E = 8, 100, 256, 8
T = B * S
P = 128
C = D // P
NK, KR, KC = 361, 121, 3
NKP = KR * KC
CTX = 128
H = 16
HD = D // H
F1, E1 = 1024, 10
F2 = 1024
F3, E3 = 512, 9
G, ED = 1024, 128
HALF = T // 2
EPS = 1e-5
MASKED = -1e30



def packing(*items):
    at, where = 0, {}
    for name, n in items:
        where[name] = (at, n)
        at += n
    return where, at


CONST, CONST_N = packing(("ident", P), ("rank", E), ("causal", S), ("window", S), ("cos", S), ("sin", S), ("m1", 4), ("m4", 4), ("ones", P),
                          ("ones8", 32))
WA, WA_N = packing(
    ("a_pick", C * 512), ("a_wk", C * 512), ("a_wv", C * 1024), ("a_wf", 8 * D), ("a_bk", 4),
    ("x_wq", C * D), ("x_wk", D), ("x_wv", D), ("x_bq", C), ("x_bk", C),
    ("f_w", C * 9 * D), ("f_router", C * E), ("f_b", D),
    ("s_wqkv", C * 768), ("s_wo", C * D),
    ("y_wq", C * 512), ("y_wk", 512), ("y_wv", 512), ("y_wo", 4 * D), ("y_bq", 4), ("y_bk", 4),
    ("r_a_bv", 1024), ("r_a_bf", D), ("r_x_bv", D), ("r_router", E), ("r_s_bo", D), ("r_y_bv", 512), ("r_y_bo", D))
WB, WB_N = packing(
    ("wq", C * 512), ("wk", C * 512), ("wv", C * 512), ("wo", 4 * D), ("bq", 4), ("bk", 4),
    ("x_wq", C * 1024), ("x_wk", 1024), ("x_wv", 1024), ("x_wo", 8 * D),
    ("r_bv", 512), ("r_bo", D), ("r_x_bo", D))
WC, WC_N = packing(
    ("wq", C * 512), ("wqs", C * 512), ("wk", C * 512), ("wks", C * 512), ("wv", C * 512), ("wo", 4 * D),
    ("x_wq", C * 512), ("x_wk", 512), ("x_wv", 512), ("x_wo", 4 * D))

AT_WA = 0
AT_WB = 0
AT_WC = WB_N
AT_WORK = 21500
AT_FW = 34300
AT_WORK2 = 38396
ARENA = 42750
assert WA_N <= AT_WORK and WB_N + WC_N <= AT_WORK

LAP_A = dict(d_evac=20, a_evac=44, s_exp=12, xn=6, gate_d=2, gate_e=1, turn=1, p_ready=10, gelu=1, o_ready=1)
LAP_B = dict(d_evac=14, a_evac=32, s_exp=10, xn=2, p_ready=10)
LAP_C = dict(d_evac=10, a_evac=30, s_exp=10, xn=2, p_ready=10, rotated=2)
LAP_F1 = dict(d_evac=8, a_evac=16)
LAP_F3 = dict(d_evac=16, a_evac=8)
for per in (LAP_A, LAP_B, LAP_C, LAP_F1, LAP_F3):
    per.update(d_full=per["d_evac"], a_full=per["a_evac"])
    if "s_exp" in per:
        per.update(s_full=per["s_exp"], s_max=per["s_exp"])


class Count:

    def __init__(self, eng, sems):
        self.eng, self.sems = eng, sems
        self.before, self.now = dict(d_evac=2, a_evac=2, s_exp=2), {}
        self.lap, self.per, self.parity = None, {}, {"d": 0, "a": 0, "s": 0}

    def add(self, key, n=1):
        self.now[key] = self.now.get(key, 0) + n
        return self.now[key]

    def got(self, key):
        return self.now.get(key, 0)

    def value(self, key, n):
        value = self.before.get(key, 0) + n
        assert value > 0, (key, value)
        if self.lap is not None and self.per.get(key, 0):
            return self.lap * self.per[key] + value
        return value

    def wait(self, key, n):
        self.eng.wait_ge(self.sems[key], self.value(key, n))

    def next(self, key, n=1):
        self.wait(key, self.add(key, n))

    @contextmanager
    def laps(self, laps, per):
        for key, n in self.now.items():
            self.before[key] = self.before.get(key, 0) + n
        self.now, self.per = {}, per
        with self.eng.Fori(0, laps) as lap:
            self.lap = lap
            yield lap
        wrong = {key: n for key, n in self.now.items() if per.get(key) != n}
        assert not wrong, (wrong, self.now)
        for key, n in per.items():
            self.before[key] = self.before.get(key, 0) + laps * n
        self.now, self.lap, self.per = {}, None, {}


def build(nc, dram, out):
    with ExitStack() as ctx:
        def sb(name, shape):
            return ctx.enter_context(nc.sbuf_tensor(name, shape, F32))

        def scratch(name, shape):
            return nc.dram_tensor(name, shape, F32, kind="Internal").ap()

        X = sb("X", [S, B * D])
        XN = sb("XN", [S, B * D])
        XNT = sb("XNT", [P, C, T])
        ctx_now = sb("ctx_now", [CTX, NKP])
        const = sb("const_sb", [P, CONST_N])
        arena = sb("arena", [P, ARENA])
        stats = sb("stats", [S, B, 8])
        rstd = sb("rstd", [S, 2 * B])
        gates = sb("gates", [S, E1, B])
        gate_now = sb("gate_now", [S, B])
        idle = sb("idle", [S, 32])
        small = sb("small", [S, 16, B, E])
        gate_row = sb("gate_row", [S, E + 1])
        cent = sb("cent", [P, C * E])
        bq4 = sb("bq4", [P, 32])
        rbias = sb("rbias", [S, E])
        sums = sb("sums", [S, H])
        rsum = sb("rsum", [S, H])
        ntop = sb("ntop", [S, 16])
        banks = ctx.enter_context(nc.psum_tensor("banks", [P, 8, 512], F32))

        turned = scratch("turned", (B, D * S))
        history = scratch("history", (B, S, G))

        def cut(pack, base, name, *dims):
            at, n = pack[name]
            a = arena[:, base + at:base + at + n]
            if len(dims) == 1:
                a = a.rearrange("p (k n) -> p k n", k=dims[0])
            return a

        def cst(name):
            at, n = CONST[name]
            return const[:, at:at + n]

        ident, ones, ones8 = cst("ident"), cst("ones"), cst("ones8")[0:1, :]

        at = AT_WORK

        def work(n):
            nonlocal at
            a = arena[:, at:at + n]
            at += n
            return a

        xb = work(D)[0:S]
        xn = work(D)[0:S]
        xnT = work(C * S).rearrange("p (k s) -> p k s", k=C)
        qT = work(16 * S).rearrange("p (k s) -> p k s", k=16)
        kT = work(8 * NK).rearrange("p (k s) -> p k s", k=8)
        v = work(KC * 1024).rearrange("p (c n) -> p c n", c=KC)
        o = work(1024)[0:S]
        oT = work(8 * S).rearrange("p (k s) -> p k s", k=8)
        gT = work(S)
        rope_t = work(4 * S).rearrange("p (k s) -> p k s", k=4)
        rope_u = work(4 * S).rearrange("p (k s) -> p k s", k=4)
        assert at <= AT_FW, at
        at = AT_WORK2
        probs_x = work(2 * 2 * NKP)[0:S].rearrange("p (u i k) -> p u i k", u=2, i=2)
        probs_s = work(2 * 2 * 4 * S)[0:S].rearrange("p (u i k) -> p u i k", u=2, i=2)
        pT = work(2 * 4 * S).rearrange("p (i m s) -> p i m s", i=2, m=4)
        assert at <= ARENA, at

        h0T = arena[:, AT_WORK:AT_WORK + 6400].rearrange("p (f t) -> p f t", f=8)
        h1T = arena[:, AT_WORK + 6400:AT_WORK + 12800].rearrange("p (f t) -> p f t", f=8)
        fc = arena[:, AT_FW:AT_FW + 2048].rearrange("p (k f) -> p k f", k=2)
        pj = arena[:, AT_FW + 2048:AT_FW + 4096].rearrange("p (f d) -> p f d", f=8)
        w2 = arena[:, AT_FW + 2048:AT_FW + 4096].rearrange("p (k f) -> p k f", k=2)
        slots = [arena[:, 1024 * i:1024 * (i + 1)].rearrange("p (k o) -> p k o", k=8) for i in range(4)]
        w3 = arena[:, 4096:6144].rearrange("p (f d) -> p f d", f=8)
        w3s = arena[:, 6144:6400]
        s2 = arena[:, 6400:6432].rearrange("p (m f) -> p m f", m=4)
        y2 = arena[:, 6656:6656 + 2 * D].rearrange("p (i d) -> p i d", i=2)
        silu2 = arena[:, AT_WORK2:AT_WORK2 + 800].rearrange("p (r t) -> p r t", r=2)
        gu3 = arena[:, AT_FW:AT_FW + 2048].rearrange("p (u k f) -> p u k f", u=2, k=2)
        dn3 = arena[:, AT_FW + 2048:AT_FW + 3072].rearrange("p (f d) -> p f d", f=4)
        whh = arena[:, 0:24576].rearrange("p (k j n) -> p k j n", k=8, j=4)
        wih = arena[:, 24576:30720].rearrange("p (k j n) -> p k j n", k=2, j=4)
        g0 = 30720

        def gru(n):
            nonlocal g0
            a = arena[:, g0:g0 + n]
            g0 += n
            return a

        h = gru(512).rearrange("p (i n) -> p i n", i=2)
        hT = gru(256).rearrange("p (c q) -> p c q", c=2)
        xt = gru(128).rearrange("p (i k q) -> p i k q", i=2, k=2)
        rz = gru(512)
        omz = gru(256)
        zh = gru(256)
        cand = gru(256)
        t1 = gru(256)
        mean = gru(64).rearrange("p (k q) -> p k q", k=2)
        cb = gru(1024)
        assert g0 <= AT_FW, g0
        cw = arena[:, AT_WORK2:AT_WORK2 + 2048].rearrange("p (k g) -> p k g", k=2)
        ew = arena[:, 0:2048].rearrange("p (k g) -> p k g", k=2)
        R = arena[0:S, 2048:2048 + 2 * G].rearrange("p (i g) -> p i g", i=2)
        ex = arena[0:S, 4096:4096 + G]
        prod = arena[0:S, 5120:5120 + G]
        dots = arena[0:S, 6144:6144 + 3 * B * E].rearrange("p (q b e) -> p q b e", q=3, b=B)
        gram = arena[0:S, 6400:6400 + 512].rearrange("p (b q) -> p b q", b=B)
        gsq = arena[0:S, 6912:6912 + 512].rearrange("p (b q) -> p b q", b=B)
        pen = arena[0:S, 7424:7424 + 16]
        h3 = arena[:, 8192:8192 + 3200].rearrange("p (f t) -> p f t", f=4)
        silu3 = arena[:, 12288:12288 + 800].rearrange("p (r t) -> p r t", r=2)

        names = (
            "d_full", "d_evac", "a_full", "a_evac", "s_full", "s_max", "s_exp",
            "xn", "p_ready", "gelu", "o_ready", "rotated", "root_in", "root_out", "gate_d", "gate_e", "turn", "v_step", "a_step", "silu", "xt_zero", "phase", "raw",
            "rz_full", "n_full", "x_used", "x_slice", "rz_done", "n_in", "n_done", "h_new", "h_turned", "h_back",
            "pen_in", "R_used", "zeroed",
            "l_const", "l_x", "l_ctx", "l_wa", "l_wb", "l_wc", "l_fc", "l_pj", "l_rb", "l_w2", "l_s0", "l_s1",
            "l_s2", "l_s3", "l_w3", "l_gru", "l_cw", "l_h0", "l_h1", "l_gu", "l_dn", "l_ew", "l_R0", "l_R1",
            "o_turn", "l_out")
        sem = {name: ctx.enter_context(nc.semaphore(name)) for name in names}
        block = ctx.enter_context(nc.Block())

        RING = {"d": 4, "a": 6}
        MARK = {}

        def narrow(hh):
            return (hh, [(0, P, hh // 4 + 4 * (hh % 4), hh // 4)])

        SELF = [[[narrow(4 * c + j) for c in range(4)] for j in (2 * u, 2 * u + 1)] for u in range(2)]
        CROSS = [[[narrow(hh)] for hh in (2 * u, 2 * u + 1)] for u in range(8)]
        WIDE = [[[(hh, [(64 * (hh % 2), 64, hh // 2, hh // 2)])] for hh in (2 * u, 2 * u + 1)] for u in range(8)]
        WHOLE = [[[(0, [(0, P, 0, 0), (0, P, 1, 1)])]]]

        def outputs_of(units, g, hh, w):
            if w == 32:
                return 32 * (hh % 4), hh // 4, g == 0, g == len(units) - 1
            if units is SELF:
                return 64 * (hh % 2), hh // 4, True, True
            return 64 * (hh % 2), hh // 2 % 4, g % 4 == 0, g % 4 == 3

        def probs_of(unit_slot, bank, keys):
            return (probs_s if keys == S else probs_x)[:, unit_slot, bank]

        def wa(name, *k):
            return cut(WA, AT_WA, name, *k)

        def wb(name, *k):
            return cut(WB, AT_WB, name, *k)

        def wc(name, *k):
            return cut(WC, AT_WC, name, *k)

        def like(dst, src):
            return src if len(dst.shape) == 2 else src.rearrange("p (a b) -> p a b", a=dst.shape[1])

        def per_column(bias, n, width):
            return bias[:, 0:n].unsqueeze(2).to_broadcast([P, n, width])

        @block.tensor
        def _(pe):
            n = Count(pe, sem)

            def open_unit(ring):
                n.wait(ring + "_evac", n.got(ring + "_evac") - 1)
                bank = RING[ring] + n.parity[ring]
                n.parity[ring] ^= 1
                return banks[:, bank, :], n.add(ring + "_evac")

            def evacuated(ring, unit=None):
                n.wait(ring + "_evac", n.got(ring + "_evac") if unit is None else unit)

            def full(ring, last):
                last.then_inc(sem[ring + "_full"], 1)

            def turn_rows(ring, src, chunks):
                u, k = open_unit(ring)
                for c in range(chunks):
                    last = nc.tensor.transpose(u[:, c * S:(c + 1) * S], src[:, c * P:(c + 1) * P], ident[0:S, 0:S])
                full(ring, last)
                return k

            def features(ring, w, lo, hi):
                u, k = open_unit(ring)
                for i, c in enumerate(range(lo, hi)):
                    for kk in range(C):
                        last = nc.tensor.matmul(u[:, i * S:(i + 1) * S], w[:, kk, c * P:(c + 1) * P], xnT[:, kk, :],
                                                start=kk == 0, stop=kk == C - 1)
                full(ring, last)
                return k

            def tokens(ring, parts, cols, bias=None):
                u, k = open_unit(ring)
                for i, (a, b) in enumerate(parts):
                    last = nc.tensor.matmul(u[0:S, 0:cols], a, b, start=i == 0, stop=bias is None and i == len(parts) - 1)
                if bias is not None:
                    last = nc.tensor.matmul(u[0:S, 0:cols], ones[0:1, 0:S], bias, start=False, stop=True)
                full(ring, last)
                return k

            def project(ring, w, lo, cols, bias=None):
                return tokens(ring, [(xnT[:, kk, :], w[:, kk, lo:lo + cols]) for kk in range(C)], cols, bias)

            def context_keys(w, chunks, rings):
                for c in range(chunks):
                    ring = rings[c % len(rings)]
                    u, _ = open_unit(ring)
                    full(ring, nc.tensor.matmul(u[:, 0:NK], w[:, c * P:(c + 1) * P], ctx_now[:, 0:NK], start=True, stop=True))

            def context_values(w, width, bias, rings):
                cols = min(width, 512)
                pieces = [(c, j) for c in range(KC) for j in range(0, width, cols)]
                per = 512 // cols
                for i in range(0, len(pieces), per):
                    ring = rings[i // per % len(rings)]
                    u, _ = open_unit(ring)
                    for m, (c, j) in enumerate(pieces[i:i + per]):
                        last = nc.tensor.matmul(u[0:KR, m * cols:(m + 1) * cols], ctx_now[:, c * KR:(c + 1) * KR],
                                                w[:, j:j + cols], start=True, stop=bias is None)
                        if bias is not None:
                            last = nc.tensor.matmul(u[0:KR, m * cols:(m + 1) * cols], ones[0:1, 0:KR],
                                                    bias[0:1, j:j + cols], start=False, stop=True)
                    full(ring, last)

            def scores(unit, keys):
                n.wait("s_exp", n.got("s_exp") - 1)
                slot = n.parity["s"]
                n.parity["s"] ^= 1
                for m in range(len(unit[0])):
                    for i, bank in enumerate(unit):
                        parts = bank[m][1]
                        for q, (r, w, cq, ck) in enumerate(parts):
                            last = nc.tensor.matmul(banks[0:S, 2 * slot + i, m * keys:(m + 1) * keys], qT[r:r + w, cq, :],
                                                    kT[r:r + w, ck, 0:keys], start=q == 0, stop=q == len(parts) - 1)
                last.then_inc(sem["s_full"], 1)
                return slot, n.add("s_exp")

            def attention(units, keys, w):
                evacuated("a")
                evacuated("d")
                slots_ = [scores(unit, keys)[0] for unit in units[:2]]
                chunks, step = (1, S) if keys == S else (KC, KR)
                for g in range(len(units) + 1):
                    if g + 2 < len(units):
                        slots_.append(scores(units[g + 2], keys)[0])
                    if g > 0:
                        unit = units[g - 1]
                        _, _, opens, completes = outputs_of(units, g - 1, 0, w)
                        evacuated("a", turned_unit)
                        if opens:
                            ob, _ = open_unit("d")
                        for m in range(len(unit[0])):
                            for c in range(chunks):
                                for i, bank in enumerate(unit):
                                    hh = bank[m][0]
                                    r, col, _, _ = outputs_of(units, g - 1, hh, w)
                                    last = nc.tensor.matmul(ob[r:r + w, col * S:(col + 1) * S], v[0:step, c, hh * w:(hh + 1) * w],
                                                            pT[0:step, i, m * chunks + c, :], start=c == 0, stop=c == chunks - 1,
                                                            skip_group_check=True)
                        if completes:
                            full("d", last)
                    if g < len(units):
                        slot = slots_.pop(0)
                        n.next("p_ready")
                        for i, bank in enumerate(units[g]):
                            u, turned_unit = open_unit("a")
                            for m in range(len(bank) * chunks):
                                last = nc.tensor.transpose(u[0:step, m * S:(m + 1) * S],
                                                           probs_of(slot, i, keys)[:, m * step:(m + 1) * step], ident[0:S, 0:S])
                            full("a", last)
                evacuated("d")

            def attention_whole():
                evacuated("a")
                evacuated("d")
                slot, done = scores(WHOLE[0], NK)
                n.wait("s_exp", done)
                u, k = open_unit("a")
                for c in range(KC):
                    last = nc.tensor.transpose(u[0:KR, c * S:(c + 1) * S], probs_x[:, slot, 0, c * KR:(c + 1) * KR], ident[0:S, 0:S])
                full("a", last)
                evacuated("a", k)
                tokens("d", [(pT[0:KR, 0, c, :], v[0:KR, c, 0:D]) for c in range(KC)], D)
                evacuated("d")

            def out_rows(chunks, w, bias):
                tokens("d", [(oT[:, c, :], w[:, c, :]) for c in range(chunks)], D, bias)

            def stay_warm(bank, count):
                for _ in range(count):
                    nc.tensor.matmul(bank[:, 0:P], ident, ident, start=True, stop=True, skip_group_check=True)

            def free_bank(ring):
                n.wait(ring + "_evac", n.got(ring + "_evac") - 1)
                return banks[:, RING[ring] + n.parity[ring], :]

            def normed(idle_products=14):
                stay_warm(free_bank("a"), idle_products)
                n.next("xn")
                evacuated("a", turn_rows("a", xn, C))

            pe.wait_ge(sem["l_const"], 16)
            pe.wait_ge(sem["l_wa"], 16)
            with n.laps(B, LAP_A) as lap:
                normed()
                features("a", wa("a_pick", C), 0, 4)
                features("d", wa("a_wk", C), 0, 4)
                for j in (0, 512):
                    project("a", wa("a_wv", C), j, 512, wa("r_a_bv")[0:1, j:j + 512])
                attention(SELF, S, 64)
                n.next("gelu")
                out_rows(8, wa("a_wf", 8), wa("r_a_bf")[0:1, :])
                normed()
                features("d", wa("x_wq", C), 0, 2)
                pe.wait_ge(sem["l_ctx"], 16 * lap + 16)
                context_keys(wa("x_wk"), C, "a")
                context_values(wa("x_wv"), D, wa("r_x_bv"), "a")
                attention_whole()
                normed()
                project("d", wa("f_router", C), 0, E, wa("r_router")[0:1, :])
                for j in range(0, 9, 2):
                    project("d", wa("f_w", C), j * D, min(2, 9 - j) * D)
                n.next("gate_d", 2)
                u, k = open_unit("a")
                full("a", nc.tensor.transpose(u[0:9, 0:S], gate_row[:, :], ident[0:S, 0:S]))
                evacuated("a", k)
                tokens("d", [(gT[0:9, :], wa("f_b")[0:9, :])], D)
                normed()
                features("a", wa("s_wqkv", C), 0, 2)
                features("a", wa("s_wqkv", C), 2, 4)
                project("a", wa("s_wqkv", C), 512, D)
                evacuated("a")
                slot, _ = scores(WHOLE[0], S)
                n.next("xn")
                u, k = open_unit("d")
                full("d", nc.tensor.transpose(u[0:S, 0:S], probs_s[:, slot, 0, 0:S], ident[0:S, 0:S]))
                evacuated("d", k)
                u, k = open_unit("a")
                for c in range(C):
                    last = nc.tensor.matmul(u[:, c * S:(c + 1) * S], v[0:S, 0, c * P:(c + 1) * P], pT[0:S, 0, 0, :],
                                            start=True, stop=True)
                full("a", last)
                MARK["turn"] = k
                stay_warm(free_bank("a"), 18)
                pe.wait_ge(sem["turn"], 16 * lap + 16)
                turn_rows("a", o, C)
                evacuated("a")
                tokens("d", [(oT[:, 4 + c, :], wa("s_wo", C)[:, c, :]) for c in range(C)], D, wa("r_s_bo")[0:1, :])
                normed()
                features("d", wa("y_wq", C), 0, 4)
                context_keys(wa("y_wk"), 4, "da")
                context_values(wa("y_wv"), 512, wa("r_y_bv"), "a")
                attention(CROSS, NK, 32)
                out_rows(4, wa("y_wo", 4), wa("r_y_bo")[0:1, :])

            def turn_all():
                n.next("xn")
                for b in range(B):
                    turn_rows("a", XN[:, b * D:], C)
                evacuated("a")

            def all_features(ring, parts, half):
                u, k = open_unit(ring)
                for i, (w, x) in enumerate(parts):
                    last = nc.tensor.matmul(u[:, 0:HALF], w, x[:, half * HALF:(half + 1) * HALF],
                                            start=i == 0, stop=i == len(parts) - 1)
                full(ring, last)
                return k

            def down(hid, w, chunks):
                for b in range(B):
                    tokens("d", [(hid[:, f, b * S:(b + 1) * S], w[:, f, :]) for f in range(chunks)], D)

            def router_rows(w):
                u, _ = open_unit("d")
                for b in range(B):
                    for kk in range(C):
                        last = nc.tensor.matmul(u[0:S, b * E:(b + 1) * E], XNT[:, kk, b * S:(b + 1) * S], w[:, kk, :],
                                                start=kk == 0, stop=kk == C - 1)
                full("d", last)

            turn_all()
            pe.wait_ge(sem["l_rb"], 32)
            router_rows(cent[:, :].rearrange("p (k e) -> p k e", k=C))
            MARK["F1"] = {key: n.value(key, n.got(key)) for key in ("d_evac", "a_evac")}
            with n.laps(E1, LAP_F1) as e:
                pe.wait_ge(sem["l_fc"], 16 * e + 16)
                for f in range(8):
                    for half in range(2):
                        all_features("a", [(fc[:, kk, f * P:(f + 1) * P], XNT[:, kk, :]) for kk in range(C)], half)
                evacuated("a")
                pe.wait_ge(sem["l_pj"], 16 * e + 16)
                down(h0T, pj, 8)

            pe.wait_ge(sem["l_wb"], 16)
            pe.wait_ge(sem["l_wc"], 16)
            with n.laps(B, LAP_B) as lap:
                normed()
                features("d", wb("wq", C), 0, 4)
                features("d", wb("wk", C), 0, 4)
                project("a", wb("wv", C), 0, 512, wb("r_bv")[0:1, :])
                attention(SELF, S, 32)
                out_rows(4, wb("wo", 4), wb("r_bo")[0:1, :])
                normed()
                features("a", wb("x_wq", C), 0, 4)
                features("d", wb("x_wq", C), 4, 8)
                pe.wait_ge(sem["l_ctx"], 16 * lap + 16 * (B + 1))
                context_keys(wb("x_wk"), 8, "da")
                context_values(wb("x_wv"), 1024, None, "adaada")
                attention(WIDE, NK, 64)
                out_rows(8, wb("x_wo", 8), wb("r_x_bo")[0:1, :])

            turn_all()
            pe.wait_ge(sem["l_w2"], 48)
            for f in range(8):
                for half in range(2):
                    all_features("a", [(fc[:, kk, f * P:(f + 1) * P], XNT[:, kk, :]) for kk in range(C)], half)
                    all_features("d", [(w2[:, kk, f * P:(f + 1) * P], XNT[:, kk, :]) for kk in range(C)], half)
            evacuated("d")
            MARK["slots"] = []
            for i in range(16):
                source = h0T if i < 8 else h1T
                if i == 8:
                    evacuated("a")
                pe.wait_ge(sem["l_s%d" % (i % 4)], 16 * (i // 4 + 1))
                for half in range(2):
                    k = all_features("a", [(slots[i % 4][:, kk, :], source[:, kk, :]) for kk in range(8)], half)
                MARK["slots"].append(n.value("a_evac", k))
            evacuated("a")
            pe.wait_ge(sem["l_w3"], 32)
            down(h0T, w3, 8)

            with n.laps(B, LAP_C) as lap:
                normed()
                for name in ("wq", "wqs", "wk", "wks"):
                    features("d", wc(name, C), 0, 4)
                for j in (0, D):
                    project("a", wc("wv", C), j, D)
                n.next("rotated", 2)
                attention(SELF, S, 32)
                out_rows(4, wc("wo", 4), None)
                normed()
                features("a", wc("x_wq", C), 0, 4)
                pe.wait_ge(sem["l_ctx"], 16 * lap + 16 * (2 * B + 1))
                context_keys(wc("x_wk"), 4, "da")
                context_values(wc("x_wv"), 512, None, "a")
                attention(CROSS, NK, 32)
                out_rows(4, wc("x_wo", 4), None)

            turn_all()
            pe.wait_ge(sem["l_cw"], 32)
            pe.wait_ge(sem["zeroed"], 1)
            u, k = open_unit("d")
            for j in range(4):
                for kk in range(C):
                    nc.tensor.matmul(u[32 * j:32 * j + 32, 0:256], mean[:, kk, :], cw[:, kk, 256 * j:256 * j + 256],
                                     start=kk == 0, stop=False, skip_group_check=True)
                last = nc.tensor.matmul(u[32 * j:32 * j + 32, 0:256], ones8, cb[0:1, 256 * j:256 * j + 256],
                                        start=False, stop=True, skip_group_check=True)
            full("d", last)

            def turn_half(i, c):
                nc.tensor.transpose(banks[:, 4 + c, 0:P], h[:, i, c * P:(c + 1) * P], ident[:, :]).then_inc(sem["h_back"], 1)

            def x_gates(i):
                for kk in range(C):
                    for j in range(4):
                        nc.tensor.matmul(banks[32 * j:32 * j + 32, i, :], xt[:, i, kk, :], wih[:, kk, j, 0:512],
                                         start=kk == 0, stop=False, skip_group_check=True)

            def x_candidate(i):
                for kk in range(C):
                    for j in range(4):
                        last = nc.tensor.matmul(banks[32 * j:32 * j + 32, 2 + i, 256:512], xt[:, i, kk, :], wih[:, kk, j, 512:768],
                                                start=kk == 0, stop=False, skip_group_check=True)
                last.then_inc(sem["x_used"], 1)

            pe.wait_ge(sem["l_gru"], 32)
            pe.wait_ge(sem["x_slice"], 1)
            x_gates(0)
            x_candidate(0)
            pe.wait_ge(sem["h_new"], 2)
            for c in range(2):
                turn_half(1, c)
            halves = [kk for c in range(2) for kk in range(c, 8, 2)]
            with pe.Fori(0, S // 2) as t:
                for i in range(2):
                    for kk in halves:
                        if kk < 2:
                            pe.wait_ge(sem["h_turned"], 4 * t + 2 * i + kk + 1)
                        for j in range(4):
                            last = nc.tensor.matmul(banks[32 * j:32 * j + 32, i, :], hT[:, kk % 2, 32 * (kk // 2):32 * (kk // 2) + 32],
                                                    whh[:, kk, j, 0:512], start=False, stop=kk == 7, skip_group_check=True)
                    last.then_inc(sem["rz_full"], 1)
                    for kk in range(8):
                        for j in range(4):
                            last = nc.tensor.matmul(banks[32 * j:32 * j + 32, 2 + i, 0:256], hT[:, kk % 2, 32 * (kk // 2):32 * (kk // 2) + 32],
                                                    whh[:, kk, j, 512:768], start=False, stop=kk == 7, skip_group_check=True)
                    last.then_inc(sem["n_full"], 1)
                    pe.wait_ge(sem["x_slice"], 2 * t + i + 2)
                    x_gates(1 - i)
                    pe.wait_ge(sem["h_new"], 4 * t + 2 * i + 3)
                    turn_half(i, 0)
                    x_candidate(1 - i)
                    pe.wait_ge(sem["h_new"], 4 * t + 2 * i + 4)
                    turn_half(i, 1)

            pe.wait_ge(sem["l_ew"], 16)
            pe.wait_ge(sem["h_turned"], 2 * S + 2)
            for b in range(B):
                for j in range(2):
                    tokens("a", [(XNT[:, kk, b * S:(b + 1) * S], ew[:, kk, 512 * j:512 * j + 512]) for kk in range(C)], 512)
            pe.wait_ge(sem["pen_in"], 1)
            u, k = open_unit("d")
            full("d", nc.tensor.matmul(u[0:S, 0:1], ones[0:S, 0:S], pen[:, 8:9], start=True, stop=True))

            MARK["F3"] = {key: n.value(key, n.got(key)) for key in ("d_evac", "a_evac")}
            with n.laps(E3, LAP_F3) as e:
                pe.wait_ge(sem["l_gu"], 16 * e + 16)
                for f in range(4):
                    for half in range(2):
                        all_features("a", [(gu3[:, 0, kk, f * P:(f + 1) * P], XNT[:, kk, :]) for kk in range(C)], half)
                        all_features("d", [(gu3[:, 1, kk, f * P:(f + 1) * P], XNT[:, kk, :]) for kk in range(C)], half)
                evacuated("d")
                pe.wait_ge(sem["l_dn"], 16 * e + 16)
                down(h3, dn3, 4)

        @block.scalar
        def _(act):
            n = Count(act, sem)

            def take():
                n.next("a_full")
                bank = RING["a"] + n.parity["a"]
                n.parity["a"] ^= 1
                n.add("a_evac")
                return banks[:, bank, :]

            def evac(dst, rows, cols, func=ACT.Copy, scale=1.0):
                nc.scalar.activation(dst, like(dst, take()[0:rows, 0:cols]), func, scale=scale).then_inc(sem["a_evac"], 1)

            def queries(src, mask):
                for j in range(4):
                    last = nc.scalar.activation(flat(qT, 4 * j, 4 * j + 4), src[:, 0:4 * S], ACT.Copy, scale=cst(mask)[:, j:j + 1])
                return last

            def flat(t, lo, hi):
                return t[:, lo:hi, :].rearrange("p k s -> p (k s)")

            def exps(unit, keys, at):
                n.next("s_max")
                slot = n.parity["s"]
                n.parity["s"] ^= 1
                for i, bank in enumerate(unit):
                    for m in range(len(bank)):
                        col = len(bank) * i + m
                        last = nc.scalar.activation(probs_of(slot, i, keys)[:, m * keys:(m + 1) * keys],
                                                    banks[0:S, 2 * slot + i, m * keys:(m + 1) * keys], ACT.Exp,
                                                    bias=ntop[:, 8 * slot + col:8 * slot + col + 1],
                                                    accum_out=sums[:, at + col:at + col + 1])
                last.then_inc(sem["s_exp"], 1)
                n.add("s_exp")

            def attention(units, keys):
                size = sum(len(bank) for bank in units[0])
                for g, unit in enumerate(units[:2]):
                    exps(unit, keys, size * g)
                for g, unit in enumerate(units):
                    for i in range(len(unit)):
                        if keys == S:
                            evac(pT[0:S, i, 0:4, :], S, 4 * S)
                        else:
                            evac(pT[0:KR, i, 0:KC, :], KR, KC * S)
                    if g + 2 < len(units):
                        exps(units[g + 2], keys, size * (g + 2))

            def values(width, rings="a"):
                cols = min(width, 512)
                pieces = [(c, j) for c in range(KC) for j in range(0, width, cols)]
                per = 512 // cols
                for i in range(0, len(pieces), per):
                    if rings[i // per % len(rings)] == "a":
                        c, j = pieces[i]
                        m = len(pieces[i:i + per])
                        evac(v[0:KR, c:c + m, j:j + cols], KR, m * cols)

            act.wait_ge(sem["l_wa"], 16)
            with n.laps(B, LAP_A) as lap:
                evac(flat(xnT, 0, 2), P, 2 * S)
                queries(take(), "m1").then_inc(sem["a_evac"], 1)
                for j in (0, 512):
                    evac(v[0:S, 0, j:j + 512], S, 512)
                attention(SELF, S)
                n.next("o_ready")
                nc.scalar.activation(flat(oT, 0, 8), flat(oT, 0, 8), ACT.Gelu).then_inc(sem["gelu"], 1)
                evac(flat(xnT, 0, 2), P, 2 * S)
                for c in range(C):
                    u = take()
                    nc.scalar.activation(kT[:, c, :], u[:, 0:NK], ACT.Identity, bias=wa("x_bk")[:, c:c + 1]
                                         ).then_inc(sem["a_evac"], 1)
                values(D)
                attention(WHOLE, NK)
                evac(flat(xnT, 0, 2), P, 2 * S)
                n.wait("gate_d", n.add("gate_d"))
                nc.scalar.activation(small[:, 12, 0:1, 0], small[:, 11, 0:1, 0], ACT.Exp).then_inc(sem["gate_e"], 1)
                n.add("gate_d")
                n.add("gate_e")
                evac(gT[0:9, :], 9, S)
                evac(flat(xnT, 0, 2), P, 2 * S)
                evac(flat(qT, 0, 2), P, 2 * S, scale=0.25)
                evac(kT[:, 0:2, 0:S], P, 2 * S)
                evac(v[0:S, 0, 0:D], S, D)
                exps(WHOLE[0], S, 0)
                evac(flat(oT, 0, 2), P, 2 * S)
                evac(flat(oT, 4, 6), P, 2 * S)
                evac(flat(xnT, 0, 2), P, 2 * S)
                for c in (1, 3):
                    u = take()
                    nc.scalar.activation(kT[:, c, :], u[:, 0:NK], ACT.Identity, bias=wa("y_bk")[:, c:c + 1]
                                         ).then_inc(sem["a_evac"], 1)
                values(512)
                attention(CROSS, NK)

            def turned_all():
                for b in range(B):
                    evac(XNT[:, :, b * S:(b + 1) * S], P, 2 * S)

            turned_all()
            act.wait_ge(sem["raw"], 1)
            nc.scalar.activation(small[:, 0:2], small[:, 14:16], ACT.Sigmoid).then_inc(sem["raw"], 1)
            n.wait("gate_d", n.add("gate_d"))
            nc.scalar.activation(small[:, 12, :, 0], small[:, 11, :, 0], ACT.Exp).then_inc(sem["gate_e"], 1)
            n.add("gate_e")
            n.add("d_evac")
            with n.laps(E1, LAP_F1):
                for f in range(8):
                    for half in range(2):
                        evac(h0T[:, f, half * HALF:(half + 1) * HALF], P, HALF, ACT.Gelu)

            with n.laps(B, LAP_B):
                evac(flat(xnT, 0, 2), P, 2 * S)
                evac(v[0:S, 0, 0:512], S, 512)
                attention(SELF, S)
                evac(flat(xnT, 0, 2), P, 2 * S)
                evac(flat(qT, 0, 4), P, 4 * S, scale=0.125)
                for c in (1, 3, 5, 7):
                    evac(kT[:, c, :], P, NK)
                values(1024, "adaada")
                attention(CROSS, NK)

            turned_all()
            act.wait_ge(sem["l_w2"], 48)
            for f in range(8):
                for half in range(2):
                    if 2 * f + half >= 2:
                        n.wait("d_evac", 2 * f + half - 1)
                    u = take()
                    nc.scalar.activation(silu2[:, half, :], u[:, 0:HALF], ACT.Silu, scale=s2[:, 0, f:f + 1]
                                         ).then_inc(sem["a_evac"], 1)
            for i in range(16):
                dst = h1T if i < 8 else h0T
                for half in range(2):
                    u = take()
                    nc.scalar.activation(dst[:, i % 8, half * HALF:(half + 1) * HALF], u[:, 0:HALF], ACT.Gelu,
                                         scale=s2[:, 2 + i // 8, i % 8:i % 8 + 1]).then_inc(sem["a_evac"], 1)
            n.add("d_evac", 16 + 8)

            with n.laps(B, LAP_C):
                evac(flat(xnT, 0, 2), P, 2 * S)
                for j in (0, D):
                    evac(v[0:S, 0, j:j + D], S, D)
                attention(SELF, S)
                evac(flat(xnT, 0, 2), P, 2 * S)
                queries(take(), "m4").then_inc(sem["a_evac"], 1)
                for c in (1, 3):
                    evac(kT[:, c, :], P, NK)
                values(512)
                attention(CROSS, NK)

            turned_all()
            n.add("d_evac")
            with act.Fori(0, S // 2) as t:
                for i in range(2):
                    act.wait_ge(sem["rz_full"], 2 * t + i + 1)
                    act.wait_ge(sem["h_new"], 4 * t + 2 * i + 2)
                    nc.scalar.activation(rz[:, :], banks[:, i, :], ACT.Sigmoid).then_inc(sem["rz_done"], 1)
                    for c in range(2):
                        act.wait_ge(sem["n_in"], 4 * t + 2 * i + c + 1)
                        nc.scalar.activation(cand[:, c * P:(c + 1) * P], t1[:, c * P:(c + 1) * P], ACT.Tanh).then_inc(sem["n_done"], 1)
            for b in range(B):
                if b:
                    act.wait_ge(sem["R_used"], b)
                for j in range(2):
                    evac(ex[:, 512 * j:512 * j + 512], S, 512)
            for i, norms in enumerate((dots[:, 0:2], small[:, 7])):
                act.wait_ge(sem["root_in"], i + 1)
                nc.scalar.activation(norms, norms, ACT.Sqrt).then_inc(sem["root_out"], 1)
            n.wait("gate_d", n.add("gate_d"))
            nc.scalar.activation(small[:, 12, :, 0], small[:, 11, :, 0], ACT.Exp).then_inc(sem["gate_e"], 1)
            n.add("gate_e")
            n.add("d_evac")
            with n.laps(E3, LAP_F3):
                for i in range(8):
                    n.wait("d_evac", i - 1)
                    u = take()
                    nc.scalar.activation(silu3[:, i % 2, :], u[:, 0:HALF], ACT.Silu).then_inc(sem["a_evac"], 1)

        @block.vector
        def _(dve):
            n = Count(dve, sem)
            steps = [0]

            def step(ins):
                steps[0] += 1
                ins.then_inc(sem["v_step"], 1)
                dve.wait_ge(sem["v_step"], steps[0])

            def settle():
                step(nc.vector.memset(idle[:, 0:1], 0.0))

            signals = [1]

            def signal(key, by=1):
                signals[0] += 1
                nc.vector.memset(idle[:, signals[0]:signals[0] + 1], 0.0).then_inc(sem[key], by)

            @contextmanager
            def laps(count, per):
                dve.sem_clear(sem["v_step"])
                steps[0] = 0
                with n.laps(count, per) as lap:
                    yield lap
                    settle()
                    dve.sem_clear(sem["v_step"])
                    steps[0] = 0

            def take():
                n.next("d_full")
                bank = RING["d"] + n.parity["d"]
                n.parity["d"] ^= 1
                n.add("d_evac")
                return banks[:, bank, :]

            def emptied(last):
                last.then_inc(sem["d_evac"], 1)

            def own():
                n.wait("d_evac", n.got("d_evac"))

            def kernel_rows(u, chunks, width=S):
                return u[:, 0:chunks * width].rearrange("p (k s) -> p k s", k=chunks)

            def evac(dst, rows, cols):
                emptied(nc.vector.tensor_copy(dst, like(dst, take()[0:rows, 0:cols])))

            def biased(dst, chunks, bias, scale=1.0):
                u = take()
                emptied(nc.vector.scalar_tensor_tensor(dst, kernel_rows(u, chunks), scale, per_column(bias, chunks, S),
                                                       ALU.mult, ALU.add))

            def inverse_root(y, x, t):
                step(nc.vector.tensor_scalar(x, x, EPS, None, ALU.add))
                step(nc.vector.tensor_scalar(y.bitcast(I32), x.bitcast(I32), 1, None, ALU.arith_shift_right))
                step(nc.vector.tensor_scalar(y.bitcast(I32), y.bitcast(I32), -1.0, float(0x5F3759DF), ALU.mult, ALU.add))
                for _ in range(3):
                    if x.shape[1] == 1:
                        step(nc.vector.scalar_tensor_tensor(t, y, x, y, ALU.mult, ALU.mult))
                    else:
                        step(nc.vector.tensor_tensor(t, y, y, ALU.mult))
                        step(nc.vector.tensor_tensor(t, t, x, ALU.mult))
                    step(nc.vector.tensor_scalar(t, t, -0.5, 1.5, ALU.mult, ALU.add))
                    step(nc.vector.tensor_tensor(y, y, t, ALU.mult))

            def queries(bias, at):
                u = kernel_rows(take(), 4)
                for j in range(4):
                    last = nc.vector.scalar_tensor_tensor(qT[:, 4 * j:4 * j + 4, :], u, cst("m4")[:, j:j + 1],
                                                          per_column(bias[:, at + 4 * j:], 4, S), ALU.mult, ALU.add)
                emptied(last)

            def norm():
                step(nc.vector.bn_stats(stats[:, 0, 0:6], xb))
                step(nc.vector.bn_aggr(stats[:, 0, 6:8], stats[:, 0, 0:6]))
                inverse_root(rstd[:, 0:1], stats[:, 0, 7:8], rstd[:, 1:2])
                nc.vector.tensor_scalar(xn, xb, stats[:, 0, 6:7], rstd[:, 0:1], ALU.subtract, ALU.mult
                                        ).then_inc(sem["xn"], 1)
                n.add("xn")

            def maxima(unit, keys, mask=None):
                n.next("s_full")
                slot = n.parity["s"]
                n.parity["s"] ^= 1
                i, m = len(unit), len(unit[0])
                sc = banks[0:S, 2 * slot:2 * slot + i, 0:m * keys]
                if m > 1:
                    sc = sc.rearrange("p i (m k) -> p i m k", m=m)
                if mask is not None:
                    over = mask[0:S, :].unsqueeze(1).unsqueeze(1).to_broadcast([S, i, m, keys])
                    step(nc.vector.tensor_tensor(sc, sc, over, ALU.add))
                top = ntop[:, 8 * slot:8 * slot + i * m]
                nc.vector.tensor_reduce(top if m == 1 else top.rearrange("p (i m) -> p i m", i=i), sc, AX, ALU.max, negate=True
                                        ).then_inc(sem["s_max"], 1)
                return slot

            def normalize(g, unit, keys, slot):
                i, m = len(unit), len(unit[0])
                at = i * m * g
                n.next("s_exp")
                step(nc.vector.reciprocal(rsum[:, at:at + i * m], sums[:, at:at + i * m]))
                if m > 1:
                    pr = probs_s[:, slot].rearrange("p i (m k) -> p (i m) k", m=m)
                    last = nc.vector.tensor_tensor(pr, pr, rsum[:, at:at + i * m].unsqueeze(2).to_broadcast([S, i * m, keys]), ALU.mult)
                else:
                    for b in range(i):
                        pr = probs_x[:, slot, b, 0:keys]
                        last = nc.vector.tensor_scalar(pr, pr, rsum[:, at + b:at + b + 1], None, ALU.mult)
                last.then_inc(sem["p_ready"], 1)

            def attention(units, keys, w, mask=None):
                slots_ = [maxima(unit, keys, mask) for unit in units[:2]]
                normalize(0, units[0], keys, slots_[0])
                for g in range(len(units) + 1):
                    if g + 2 < len(units):
                        slots_.append(maxima(units[g + 2], keys, mask))
                    if g + 1 < len(units):
                        normalize(g + 1, units[g + 1], keys, slots_[g + 1])
                    if g > 0 and outputs_of(units, g - 1, 0, w)[3]:
                        if w == 32:
                            dst = oT[:, 0:4, :]
                        elif units is SELF:
                            dst = oT.rearrange("p (c u) s -> p u c s", u=2)[:, g - 1]
                        else:
                            dst = oT[:, (g - 1) // 4 * 4:(g - 1) // 4 * 4 + 4, :]
                        evac(dst, P, 4 * S)

            def add_unit():
                u = take()
                emptied(nc.vector.tensor_tensor(xb, xb, u[0:S, 0:D], ALU.add))
                own()

            def top_two(nb, value, score, gate, ready):
                t = lambda i: small[:, i, 0:nb, :]
                col = lambda i: small[:, i, 0:nb, 0:1]
                wide_ = lambda a: a.to_broadcast([S, nb, E])
                rank = cst("rank")[0:S, :].unsqueeze(1).to_broadcast([S, nb, E])
                hot = (8, 9)
                for r in range(2):
                    step(nc.vector.tensor_reduce(col(2), score, AX, ALU.max))
                    step(nc.vector.tensor_tensor(t(3), score, wide_(col(2)), ALU.is_equal))
                    step(nc.vector.tensor_tensor(t(4), t(3), rank, ALU.mult))
                    step(nc.vector.tensor_reduce(col(5), t(4), AX, ALU.max))
                    step(nc.vector.tensor_tensor(t(hot[r]), t(4), wide_(col(5)), ALU.is_equal))
                    step(nc.vector.tensor_tensor(t(6), t(hot[r]), value, ALU.mult))
                    step(nc.vector.tensor_reduce(col(7 if r == 0 else 10), t(6), AX, ALU.add))
                    if r == 0:
                        step(nc.vector.scalar_tensor_tensor(score, t(hot[0]), MASKED, score, ALU.mult, ALU.add))
                nc.vector.tensor_tensor(col(11), col(10), col(7), ALU.subtract).then_inc(sem["gate_d"], 1)
                n.add("gate_d")
                n.next("gate_e")
                step(nc.vector.tensor_scalar(col(2), col(12), 1.0, None, ALU.add))
                step(nc.vector.reciprocal(col(5), col(2)))
                step(nc.vector.tensor_tensor(col(7), col(12), col(5), ALU.mult))
                step(nc.vector.tensor_tensor(t(3), t(8), wide_(col(5)), ALU.mult))
                step(nc.vector.tensor_tensor(t(4), t(9), wide_(col(7)), ALU.mult))
                ready(nc.vector.tensor_tensor(gate, t(3), t(4), ALU.add))

            nc.vector.memset(gate_row[:, :], 1.0).then_inc(sem["d_evac"], 2)
            step(nc.vector.memset(probs_x[:, :, :, :], 0.0))
            nc.vector.memset(small[:, :, :, :], 0.0).then_inc(sem["a_evac"], 2)
            dve.wait_ge(sem["l_x"], 16)
            dve.wait_ge(sem["l_wa"], 16)
            dve.wait_ge(sem["l_const"], 16)
            for j in range(4):
                step(nc.vector.tensor_scalar(bq4[:, 4 * j:4 * j + 4], wa("y_bq"), cst("m4")[:, j:j + 1], None, ALU.mult))
            nc.vector.memset(stats[:, :, :], 0.0).then_inc(sem["s_exp"], 2)
            with laps(B, LAP_A) as lap:
                step(nc.vector.tensor_copy(xb, X[:, bass.ds(lap * D, D)]))
                norm()
                biased(kT[:, 0:4, 0:S], 4, wa("a_bk"))
                attention(SELF, S, 64, cst("causal"))
                own()
                nc.vector.memset(idle[:, 1:2], 0.0).then_inc(sem["o_ready"], 1)
                n.wait("xn", n.got("xn"))
                step(nc.vector.tensor_tensor(xb, xb, xn, ALU.add))
                add_unit()
                norm()
                biased(qT[:, 0:2, :], 2, wa("x_bq"))

                maxima(WHOLE[0], NK)
                n.next("s_exp")
                step(nc.vector.reciprocal(rsum[:, 0:1], sums[:, 0:1]))
                emptied(nc.vector.scalar_tensor_tensor(xb, take()[0:S, 0:D], rsum[:, 0:1], xb, ALU.mult, ALU.add))
                own()
                norm()
                u = take()
                emptied(nc.vector.tensor_copy(small[:, 0, 0, :], u[0:S, 0:E]))
                own()
                step(nc.vector.tensor_copy(small[:, 1, 0, :], small[:, 0, 0, :]))

                def ready(last):
                    last.then_inc(sem["gate_d"], 1)
                    n.next("gate_d")
                top_two(1, small[:, 0, 0:1, :], small[:, 1, 0:1, :], gate_row[:, 0:E].unsqueeze(1), ready)
                for j in range(0, 9, 2):
                    u = take()
                    m = min(2, 9 - j)
                    for i in range(m):
                        last = nc.vector.scalar_tensor_tensor(xb, u[0:S, i * D:(i + 1) * D], gate_row[:, j + i:j + i + 1], xb,
                                                              ALU.mult, ALU.add)
                        if i + 1 < m:
                            step(last)
                    emptied(last)
                    own()
                add_unit()
                norm()
                slot = maxima(WHOLE[0], S)
                n.next("s_exp")
                step(nc.vector.reciprocal(rsum[:, 0:1], sums[:, 0:1]))
                nc.vector.tensor_scalar(probs_s[:, slot, 0, 0:S], probs_s[:, slot, 0, 0:S], rsum[:, 0:1], None, ALU.mult
                                        ).then_inc(sem["xn"], 1)
                n.add("xn")
                evac(pT[0:S, 0, 0, :], S, S)
                add_unit()
                norm()
                queries(bq4, 0)
                for c in (0, 2):
                    emptied(nc.vector.tensor_scalar(kT[:, c, :], take()[:, 0:NK], wa("y_bk")[:, c:c + 1], None, ALU.add))
                attention(CROSS, NK, 32)
                add_unit()
                settle()
                step(nc.vector.tensor_copy(X[:, bass.ds(lap * D, D)], xb))

            def norm_all():
                for b in range(B):
                    last = nc.vector.bn_stats(stats[:, b, 0:6], X[:, b * D:(b + 1) * D])
                step(last)
                for b in range(B):
                    last = nc.vector.bn_aggr(stats[:, b, 6:8], stats[:, b, 0:6])
                step(last)
                inverse_root(rstd[:, 0:B], stats[:, :, 7], rstd[:, B:])
                for b in range(B):
                    last = nc.vector.tensor_scalar(XN[:, b * D:(b + 1) * D], X[:, b * D:(b + 1) * D], stats[:, b, 6:7],
                                                   rstd[:, b:b + 1], ALU.subtract, ALU.mult)
                last.then_inc(sem["xn"], 1)
                n.next("xn")
                n.add("a_evac", B)

            def phase_over():
                signal("phase")

            phase_over()
            norm_all()
            step(nc.vector.tensor_tensor(X[:, :], X[:, :], XN[:, :], ALU.add))
            dve.wait_ge(sem["l_rb"], 32)
            u = take()
            raw = u[0:S, 0:B * E].rearrange("p (b e) -> p b e", b=B)
            step(nc.vector.tensor_copy(small[:, 14], raw))
            emptied(nc.vector.tensor_tensor(small[:, 15], raw, rbias[:, :].unsqueeze(1).to_broadcast([S, B, E]), ALU.add))
            n.wait("d_evac", n.got("d_evac"))
            nc.vector.memset(gates[:, E:E1, :], 1.0).then_inc(sem["raw"], 1)
            dve.wait_ge(sem["raw"], 2)
            top_two(B, small[:, 0], small[:, 1], gates[:, 0:E, :].rearrange("p e b -> p b e"), step)

            def experts(lap_gate):
                step(nc.vector.tensor_copy(gate_now[:, :].unsqueeze(1), gates[:, bass.ds(lap_gate, 1), :]))

            def weighted():
                for b in range(B):
                    xs = X[:, b * D:(b + 1) * D]
                    emptied(nc.vector.scalar_tensor_tensor(xs, take()[0:S, 0:D], gate_now[:, b:b + 1], xs, ALU.mult, ALU.add))

            with laps(E1, LAP_F1) as e:
                experts(e)
                weighted()
                own()

            phase_over()
            dve.wait_ge(sem["l_wb"], 16)
            for j in range(4):
                step(nc.vector.tensor_scalar(bq4[:, 16 + 4 * j:20 + 4 * j], wb("bq"), cst("m4")[:, j:j + 1], None, ALU.mult))
            with laps(B, LAP_B) as lap:
                step(nc.vector.tensor_copy(xb, X[:, bass.ds(lap * D, D)]))
                norm()
                queries(bq4, 16)
                biased(kT[:, 0:4, 0:S], 4, wb("bk"))
                attention(SELF, S, 32, cst("causal"))
                add_unit()
                norm()
                emptied(nc.vector.tensor_scalar(qT[:, 4:8, :], kernel_rows(take(), 4), 0.125, None, ALU.mult))
                for c in (0, 2, 4, 6):
                    evac(kT[:, c, :], P, NK)
                for c, j in ((0, 512), (2, 0)):
                    evac(v[0:KR, c, j:j + 512], KR, 512)
                attention(WIDE, NK, 64)
                add_unit()
                settle()
                step(nc.vector.tensor_copy(X[:, bass.ds(lap * D, D)], xb))

            phase_over()
            norm_all()
            dve.wait_ge(sem["l_w2"], 48)
            for f in range(8):
                for half in range(2):
                    n.next("a_evac")
                    emptied(nc.vector.scalar_tensor_tensor(h0T[:, f, half * HALF:(half + 1) * HALF], take()[:, 0:HALF],
                                                           s2[:, 1, f:f + 1], silu2[:, half, :], ALU.mult, ALU.mult))
            n.add("a_evac", 32)
            dve.wait_ge(sem["l_w3"], 32)
            for b in range(B):
                xs = X[:, b * D:(b + 1) * D]
                emptied(nc.vector.tensor_tensor(y2[0:S, b % 2, :], take()[0:S, 0:D], w3s[0:S, :], ALU.mult))
                own()
                step(nc.vector.tensor_tensor(xs, xs, y2[0:S, b % 2, :], ALU.add))

            def rotated(dst, cos, sin):
                for name, t in ((cos, rope_t), (sin, rope_u)):
                    emptied(nc.vector.tensor_tensor(t, kernel_rows(take(), 4), cst(name).unsqueeze(1).to_broadcast([P, 4, S]),
                                                    ALU.mult))
                own()
                if dst is None:
                    step(nc.vector.tensor_tensor(rope_t, rope_t, rope_u, ALU.add))
                    for j in range(4):
                        last = nc.vector.tensor_scalar(qT[:, 4 * j:4 * j + 4, :], rope_t, cst("m4")[:, j:j + 1], None, ALU.mult)
                else:
                    last = nc.vector.tensor_tensor(dst, rope_t, rope_u, ALU.add)
                last.then_inc(sem["rotated"], 1)
                n.next("rotated")

            with laps(B, LAP_C) as lap:
                step(nc.vector.tensor_copy(xb, X[:, bass.ds(lap * D, D)]))
                norm()
                rotated(None, "cos", "sin")
                rotated(kT[:, 0:4, 0:S], "cos", "sin")
                attention(SELF, S, 32, cst("window"))
                add_unit()
                norm()
                for c in (0, 2):
                    evac(kT[:, c, :], P, NK)
                attention(CROSS, NK, 32)
                add_unit()
                settle()
                step(nc.vector.tensor_copy(X[:, bass.ds(lap * D, D)], xb))

            phase_over()
            norm_all()
            step(nc.vector.memset(mean[:, :, :], 0.0))
            n.wait("a_evac", n.got("a_evac"))
            for kk in range(C):
                last = nc.vector.tensor_reduce(mean[:, kk, 0:B], XNT[:, kk, :].rearrange("p (b s) -> p b s", b=B), AX, ALU.add)
            step(last)
            nc.vector.tensor_scalar(mean[:, :, :], mean[:, :, :], 1.0 / S, None, ALU.mult).then_inc(sem["zeroed"], 1)
            emptied(nc.vector.tensor_copy(h[:, 1, :], take()[:, 0:256]))
            own()
            signal("h_new", 2)
            for i in range(2):
                signal("l_h%d" % i, 64)
            def keep_half(c):
                nc.vector.tensor_copy(hT[:, c, :], banks[:, 4 + c, 0:P]).then_inc(sem["h_turned"], 1)

            for c in range(2):
                dve.wait_ge(sem["h_back"], c + 1)
                keep_half(c)
            dve.sem_clear(sem["v_step"])
            steps[0] = 0
            with dve.Fori(0, S // 2) as t:
                for i in range(2):
                    dve.wait_ge(sem["rz_done"], 2 * t + i + 1)
                    step(nc.vector.tensor_tensor(zh[:, :], rz[:, 256:512], h[:, 1 - i, :], ALU.mult))
                    step(nc.vector.tensor_scalar(omz[:, :], rz[:, 256:512], -1.0, 1.0, ALU.mult, ALU.add))
                    dve.wait_ge(sem["n_full"], 2 * t + i + 1)
                    us = [slice(c * P, (c + 1) * P) for c in range(2)]
                    for c in range(2):
                        step(nc.vector.tensor_tensor(t1[:, us[c]], rz[:, us[c]], banks[:, 2 + i, us[c]], ALU.mult))
                        nc.vector.tensor_tensor(t1[:, us[c]], t1[:, us[c]], banks[:, 2 + i, D + c * P:D + (c + 1) * P], ALU.add
                                                ).then_inc(sem["n_in"], 1)
                    for c in range(2):
                        dve.wait_ge(sem["n_done"], 4 * t + 2 * i + c + 1)
                        step(nc.vector.tensor_tensor(cand[:, us[c]], cand[:, us[c]], omz[:, us[c]], ALU.mult))
                        if c == 0:
                            dve.wait_ge(sem["l_h%d" % i], 64 * t + 64)
                        nc.vector.tensor_tensor(h[:, i, us[c]], cand[:, us[c]], zh[:, us[c]], ALU.add).then_inc(sem["h_new"], 1)
                    for c in range(2):
                        dve.wait_ge(sem["h_back"], 4 * t + 2 * i + c + 3)
                        keep_half(c)
                settle()
                dve.sem_clear(sem["v_step"])
                steps[0] = 0

            eight = lambda a: a.rearrange("p (e d) -> p e d", d=ED)
            dve.wait_ge(sem["h_turned"], 2 * S + 2)
            for b in range(B):
                dve.wait_ge(sem["l_R%d" % (b % 2)], 16 * (b // 2 + 1))
                rb = R[:, b % 2, :]
                step(nc.vector.tensor_tensor(prod, rb, rb, ALU.mult))
                step(nc.vector.tensor_reduce(dots[:, 0, b, :], eight(prod), AX, ALU.add))
                for s_ in range(1, E):
                    m = E - s_
                    step(nc.vector.tensor_tensor(prod[:, 0:m * ED], rb[:, 0:m * ED], rb[:, s_ * ED:], ALU.mult))
                    step(nc.vector.tensor_reduce(gram[:, b, s_:s_ + (m - 1) * (E + 1) + 1:E + 1], eight(prod[:, 0:m * ED]), AX, ALU.add))
                    step(nc.vector.tensor_copy(gram[:, b, E * s_:E * s_ + (m - 1) * (E + 1) + 1:E + 1], gram[:, b, s_:s_ + (m - 1) * (E + 1) + 1:E + 1]))
                n.wait("a_evac", n.add("a_evac", 2))
                step(nc.vector.tensor_tensor(prod, ex, ex, ALU.mult))
                step(nc.vector.tensor_reduce(dots[:, 1, b, :], eight(prod), AX, ALU.add))
                nc.vector.tensor_tensor(prod, ex, rb, ALU.mult).then_inc(sem["R_used"], 1)
                dve.wait_ge(sem["R_used"], b + 1)
                step(nc.vector.tensor_reduce(dots[:, 2, b, :], eight(prod), AX, ALU.add))
            t = lambda i: small[:, i]
            step(nc.vector.tensor_copy(gram[:, :, 0:E * E:E + 1], dots[:, 0]))
            signal("root_in")
            dve.wait_ge(sem["root_out"], 1)
            step(nc.vector.tensor_scalar(t(2), dots[:, 0], 1e-12, None, ALU.max))
            step(nc.vector.reciprocal(t(3), t(2)))
            step(nc.vector.tensor_tensor(t(4), dots[:, 0], t(3), ALU.mult))
            step(nc.vector.tensor_scalar(t(4), t(4), 1e-8, None, ALU.max))
            step(nc.vector.tensor_scalar(t(5), dots[:, 1], 1e-8, None, ALU.max))
            step(nc.vector.tensor_tensor(t(4), t(4), t(5), ALU.mult))
            step(nc.vector.reciprocal(t(5), t(4)))
            step(nc.vector.tensor_tensor(t(6), dots[:, 2], t(3), ALU.mult))
            step(nc.vector.tensor_tensor(t(6), t(6), t(5), ALU.mult))
            step(nc.vector.tensor_scalar(t(6), t(6), -1.0, 1.0, ALU.mult, ALU.add))
            for b in range(B):
                gb = gram[:, b, :].rearrange("p (e f) -> p e f", e=E)
                step(nc.vector.tensor_tensor(gb, gb, t(3)[:, b, :].unsqueeze(2).to_broadcast([S, E, E]), ALU.mult))
                step(nc.vector.tensor_tensor(gb, gb, t(3)[:, b, :].unsqueeze(1).to_broadcast([S, E, E]), ALU.mult))
            step(nc.vector.tensor_scalar(gram[:, :, 0:E * E:E + 1], gram[:, :, 0:E * E:E + 1], -1.0, None, ALU.add))
            step(nc.vector.tensor_tensor(gsq, gram, gram, ALU.mult))
            g3 = gsq.rearrange("p b (e f) -> p (b e) f", e=E)
            t7 = t(7).rearrange("p b e -> p (b e)")
            nc.vector.tensor_reduce(t7, g3, AX, ALU.add).then_inc(sem["root_in"], 1)
            dve.wait_ge(sem["root_out"], 2)
            step(nc.vector.tensor_scalar(t(7), t(7), 1e-12, None, ALU.max))
            step(nc.vector.reciprocal(t(7), t(7)))
            gr = gram.rearrange("p b (e f) -> p (b e) f", e=E)
            step(nc.vector.tensor_tensor(gr, gr, t7.unsqueeze(2).to_broadcast([S, B * E, E]), ALU.mult))
            step(nc.vector.tensor_tensor(gsq, gram, gram, ALU.mult))
            nc.vector.tensor_reduce(pen[:, 8:9], gsq.rearrange("p b q -> p (b q)"), AX, ALU.add).then_inc(sem["pen_in"], 1)
            emptied(nc.vector.tensor_scalar(pen[:, 9:10], take()[0:S, 0:1], 1.0 / T, 1.0, ALU.mult, ALU.add))
            own()
            step(nc.vector.tensor_scalar(t(0), t(6), pen[:, 9:10], None, ALU.mult))
            step(nc.vector.tensor_copy(t(1), t(0)))
            top_two(B, small[:, 0], small[:, 1], gates[:, 0:E, :].rearrange("p e b -> p b e"), step)
            phase_over()
            with laps(E3, LAP_F3) as e:
                experts(e)
                for f in range(4):
                    for half in range(2):
                        n.next("a_evac")
                        emptied(nc.vector.tensor_tensor(h3[:, f, half * HALF:(half + 1) * HALF], take()[:, 0:HALF],
                                                        silu3[:, half, :], ALU.mult))
                weighted()
                own()
            phase_over()

        @block.gpsimd
        def _(pool):
            pool.wait_ge(sem["zeroed"], 1)
            nc.gpsimd.memset(xt[:, :, :, :], 0.0).then_inc(sem["xt_zero"], 1)
            pool.wait_ge(sem["xt_zero"], 1)
            by_s = XNT[:, :, :].rearrange("p k (b s) -> p k b s", b=B)
            nc.gpsimd.tensor_copy(xt[:, 0, :, 0:B], by_s[:, :, :, 0]).then_inc(sem["x_slice"], 1)
            nc.gpsimd.tensor_copy(xt[:, 1, :, 0:B], by_s[:, :, :, 1]).then_inc(sem["x_slice"], 1)
            with pool.Fori(0, S // 2 - 1) as t:
                for i in range(2):
                    pool.wait_ge(sem["x_used"], 2 * t + i + 1)
                    nc.gpsimd.tensor_copy(xt[:, i, :, 0:B], by_s[:, :, :, bass.ds(2 * t + i + 2, 1)].rearrange("p k b s -> p k (b s)")
                                          ).then_inc(sem["x_slice"], 1)
            pool.wait_ge(sem["x_used"], S - 1)
            nc.gpsimd.tensor_copy(xt[:, 0, :, 0:B], by_s[:, :, :, S - 1]).then_inc(sem["x_slice"], 1)

        @block.sync
        def _(sp):
            def load(dst, name, s, n=16):
                sp.dma_start(dst, dram[name]).then_inc(sem[s], n)

            load(const[:, :], "const", "l_const")
            sp.dma_start(X[:, :].rearrange("s (b d) -> s b d", b=B), dram["x"].rearrange("b s d -> s b d")).then_inc(sem["l_x"], 16)
            load(arena[:, AT_WA:AT_WA + WA_N], "WA", "l_wa")
            ctxs = dram["ctxT"].rearrange("(b p) k -> b p k", b=B)
            n = Count(sp, sem)

            def context(lap, first):
                sp.dma_start(ctx_now[:, :], ctxs[bass.ds(lap, 1)].rearrange("o p k -> (o p) k")).then_inc(sem["l_ctx"], 16)

            sp.dma_start(cent[:, :], dram["centroids"]).then_inc(sem["l_rb"], 16)
            sp.dma_start(rbias[:, :], dram["routing_bias"].partition_broadcast(S)).then_inc(sem["l_rb"], 16)
            turned_rows = turned.rearrange("b (c p s) -> b p c s", c=C, p=P)
            turned_back = turned.rearrange("b (s d) -> b s d", s=S)
            with n.laps(B, LAP_A) as lap:
                n.wait("s_exp", 0)
                context(lap, 0)
                n.wait("a_evac", MARK["turn"])
                sp.dma_start(turned_rows[bass.ds(lap, 1)].rearrange("o p c s -> (o p) c s"), oT[:, 0:2, :]).then_inc(sem["o_turn"], 16)
                sp.wait_ge(sem["o_turn"], 16 * lap + 16)
                sp.dma_start(o[:, 0:D], turned_back[bass.ds(lap, 1)].rearrange("o s d -> (o s) d")).then_inc(sem["turn"], 16)
            sp.wait_ge(sem["phase"], 1)
            load(arena[:, AT_WB:AT_WB + WB_N], "WB", "l_wb")
            load(arena[:, AT_WC:AT_WC + WC_N], "WC", "l_wc")
            fcs = dram["fc"].rearrange("(e p) n -> e p n", e=E1)
            pjs = dram["pj"].rearrange("(e p) n -> e p n", e=E1)
            with sp.Fori(0, E1) as e:
                sp.wait_ge(sem["a_evac"], e * LAP_F1["a_evac"] + MARK["F1"]["a_evac"])
                sp.dma_start(arena[:, AT_FW:AT_FW + 2048], fcs[bass.ds(e, 1)].rearrange("o p n -> (o p) n")).then_inc(sem["l_fc"], 16)
                sp.wait_ge(sem["d_evac"], e * LAP_F1["d_evac"] + MARK["F1"]["d_evac"])
                sp.dma_start(arena[:, AT_FW + 2048:AT_FW + 4096], pjs[bass.ds(e, 1)].rearrange("o p n -> (o p) n")).then_inc(sem["l_pj"], 16)
            sp.wait_ge(sem["phase"], 2)
            load(arena[:, AT_FW:AT_FW + 2048], "w1", "l_w2")
            load(arena[:, AT_FW + 2048:AT_FW + 4096], "w2", "l_w2")
            with sp.Fori(0, B) as lap:
                sp.wait_ge(sem["s_exp"], lap * LAP_B["s_exp"] + n.before["s_exp"])
                context(lap, B)
            sp.wait_ge(sem["phase"], 3)
            load(arena[:, 6400:6432], "s2", "l_w2")
            load(arena[:, 4096:6144], "w3", "l_w3")
            sp.dma_start(w3s[0:S, :], dram["w3s"].partition_broadcast(S)).then_inc(sem["l_w3"], 16)
            hh_ = dram["hh"].rearrange("(i p) n -> i p n", i=16)
            for i in range(16):
                if i >= 4:
                    sp.wait_ge(sem["a_evac"], MARK["slots"][i - 4])
                sp.dma_start(arena[:, 1024 * (i % 4):1024 * (i % 4) + 1024], hh_[i]).then_inc(sem["l_s%d" % (i % 4)], 16)
            with sp.Fori(0, B) as lap:
                sp.wait_ge(sem["s_exp"], lap * LAP_C["s_exp"] + n.before["s_exp"] + B * LAP_B["s_exp"])
                context(lap, 2 * B)
            sp.wait_ge(sem["phase"], 4)
            load(arena[:, 0:24576], "whh", "l_gru")
            load(arena[:, 24576:30720], "wih", "l_gru")
            load(arena[:, AT_WORK2:AT_WORK2 + 2048], "ctx_w", "l_cw")
            load(cb[0:1, :], "ctx_b", "l_cw")
            by_group = history.rearrange("b s (j u) -> s j b u", j=4)
            with sp.Fori(0, S // 2) as t:
                for i in range(2):
                    sp.wait_ge(sem["h_new"], 4 * t + 2 * i + 4)
                    for j in range(4):
                        sp.dma_start(by_group[bass.ds(2 * t + i, 1), j].rearrange("o b u -> (o b) u"), h[32 * j:32 * j + B, i, :]
                                     ).then_inc(sem["l_h%d" % i], 16)
            sp.wait_ge(sem["h_turned"], 2 * S + 2)
            load(arena[:, 0:2048], "ew", "l_ew")
            sp.wait_ge(sem["l_h0"], 64 * (S // 2 + 1))
            sp.wait_ge(sem["l_h1"], 64 * (S // 2 + 1))
            for b in range(B):
                if b >= 2:
                    sp.wait_ge(sem["R_used"], b - 1)
                sp.dma_start(R[:, b % 2, :], history[b]).then_inc(sem["l_R%d" % (b % 2)], 16)
            gus = dram["gu"].rearrange("(e p) n -> e p n", e=E3)
            dns = dram["dn"].rearrange("(e p) n -> e p n", e=E3)
            with sp.Fori(0, E3) as e:
                sp.wait_ge(sem["a_evac"], e * LAP_F3["a_evac"] + MARK["F3"]["a_evac"])
                sp.wait_ge(sem["d_evac"], e * LAP_F3["d_evac"] + MARK["F3"]["d_evac"] - 8)
                sp.dma_start(arena[:, AT_FW:AT_FW + 2048], gus[bass.ds(e, 1)].rearrange("o p n -> (o p) n")).then_inc(sem["l_gu"], 16)
                sp.wait_ge(sem["d_evac"], e * LAP_F3["d_evac"] + MARK["F3"]["d_evac"])
                sp.dma_start(arena[:, AT_FW + 2048:AT_FW + 3072], dns[bass.ds(e, 1)].rearrange("o p n -> (o p) n")).then_inc(sem["l_dn"], 16)
            sp.wait_ge(sem["phase"], 6)
            sp.dma_start(out.rearrange("b s d -> s b d"), X[:, :].rearrange("s (b d) -> s b d", b=B)).then_inc(sem["l_out"], 16)
            sp.wait_ge(sem["l_out"], 16)


def rows_first(w):
    k, m = w.shape
    return np.ascontiguousarray(w.reshape(k // P, P, m).transpose(1, 0, 2).reshape(P, -1))


def pad_heads(w):
    w = w.reshape(-1, H, HD)
    out = np.zeros((w.shape[0], H, 32), w.dtype)
    out[:, :, :HD] = w
    return out.reshape(w.shape[0], H * 32)


def columns(bias):
    return np.ascontiguousarray(bias.reshape(-1, P).T)


def pack(where, total, parts):
    out = np.zeros((P, total), np.float32)
    for name, (at, m) in where.items():
        a = parts[name]
        a = a.reshape(1, -1) if a.ndim == 1 else a
        assert a.shape[1] == m, (name, a.shape, m)
        out[:a.shape[0], at:at + m] = a
    return out


def constants():
    i = np.arange(S)
    inv = (1.0 / np.float32(10000.0) ** (np.arange(0, HD, 2, dtype=np.float32) / HD)).astype(np.float32)
    ang = np.arange(S, dtype=np.float32)[:, None] * inv
    cos, sin = np.cos(ang), np.sin(ang)
    rot_c, rot_s = np.zeros((P, S), np.float32), np.zeros((P, S), np.float32)
    for q in range(4):
        for d in range(HD):
            rot_c[32 * q + d] = cos[:, d // 2]
            rot_s[32 * q + d] = (1 if d % 2 else -1) * sin[:, d // 2]
    head_rows = (np.arange(P)[:, None] // 32 == np.arange(4)[None]).astype(np.float32)
    return dict(
        ident=np.eye(P, dtype=np.float32), rank=np.tile(E - np.arange(E, dtype=np.float32), (P, 1)),
        causal=np.where(i[None] <= i[:, None], 0, MASKED).astype(np.float32),
        window=np.where(abs(i[None] - i[:, None]) <= 32, 0, MASKED).astype(np.float32),
        cos=rot_c, sin=rot_s, m1=head_rows, m4=head_rows / 4, ones=np.ones((P, P), np.float32),
        ones8=np.tile((np.arange(32) < B).astype(np.float32), (P, 1)))


def layouts(a):
    L0a, L0x, L0f = (lambda s: a["L0_attn_" + s]), (lambda s: a["L0_xattn_" + s]), (lambda s: a["L0_ffn_" + s])
    y = lambda s: a["L1_xattn_" + s]
    qkv1 = a["L1_attn_w_qkv"].T
    pick = np.eye(D, dtype=np.float32)
    experts0 = np.concatenate([w.T for w in L0f("W_experts")] + [L0f("W_shared").T], 1)
    wa = dict(
        a_pick=rows_first(pad_heads(pick)), a_wk=rows_first(pad_heads(L0a("Wk"))), a_wv=rows_first(L0a("Wv")),
        a_wf=rows_first(L0a("Wf")), a_bk=columns(pad_heads(L0a("bk")[None])[0]),
        x_wq=rows_first(L0x("Wq")), x_wk=L0x("Wk"), x_wv=L0x("Wv"), x_bq=columns(L0x("bq")), x_bk=columns(L0x("bk")),
        f_w=rows_first(experts0), f_router=rows_first(L0f("W_router").T),
        f_b=np.concatenate([L0f("b_experts"), L0f("b_shared")[None]], 0),
        s_wqkv=rows_first(qkv1), s_wo=rows_first(a["L1_attn_w_proj"].T),
        y_wq=rows_first(pad_heads(y("Wq"))), y_wk=pad_heads(y("Wk")), y_wv=pad_heads(y("Wv")), y_wo=rows_first(pad_heads(y("Wo").T).T),
        y_bq=columns(pad_heads(y("bq")[None])[0]), y_bk=columns(pad_heads(y("bk")[None])[0]),
        r_a_bv=L0a("bv"), r_a_bf=L0a("bf"), r_x_bv=L0x("bv"), r_router=L0f("b_router"),
        r_s_bo=a["L1_attn_b_proj"], r_y_bv=pad_heads(y("bv")[None])[0], r_y_bo=y("bo"))
    w, bb = a["L2_attn_w_qkv"], a["L2_attn_b_qkv"]
    z = lambda s: a["L2_xattn_" + s]
    wb = dict(
        wq=rows_first(pad_heads(w[:, :D])), wk=rows_first(pad_heads(w[:, D:2 * D])), wv=rows_first(pad_heads(w[:, 2 * D:])),
        wo=rows_first(pad_heads(a["L2_attn_w_proj"].T).T), bq=columns(pad_heads(bb[None, :D])[0]), bk=columns(pad_heads(bb[None, D:2 * D])[0]),
        x_wq=rows_first(z("Wq")), x_wk=z("Wk"), x_wv=z("Wv"), x_wo=rows_first(z("Wo")),
        r_bv=pad_heads(bb[None, 2 * D:])[0], r_bo=a["L2_attn_b_proj"], r_x_bo=z("bo"))
    swap = np.arange(D).reshape(-1, 2)[:, ::-1].reshape(-1)
    q3 = a["L3_attn_Wq"]
    each = lambda m: np.repeat(m.reshape(D, 4, HD), 4, axis=1).reshape(D, D)
    k3, v3 = each(a["L3_attn_Wk"]), each(a["L3_attn_Wv"])
    kv = a["L3_xattn_Wkv"].T
    wc = dict(
        wq=rows_first(pad_heads(q3)), wqs=rows_first(pad_heads(q3[:, swap])), wk=rows_first(pad_heads(k3)),
        wks=rows_first(pad_heads(k3[:, swap])), wv=rows_first(pad_heads(v3)), wo=rows_first(pad_heads(a["L3_attn_Wo"].T).T),
        x_wq=rows_first(pad_heads(a["L3_xattn_Wq"].T)), x_wk=pad_heads(kv[:, :D]), x_wv=pad_heads(kv[:, D:]),
        x_wo=rows_first(pad_heads(a["L3_xattn_Wo"]).T))
    context = np.zeros((B, CTX, NKP), np.float32)
    context[:, :, :NK] = a["ctx_512"].transpose(0, 2, 1)
    stack = lambda ws: np.concatenate([rows_first(m.T) for m in ws], 0)
    g = lambda m: np.ascontiguousarray(
        m.T.reshape(-1, P, 3, 4, 256).transpose(1, 0, 3, 2, 4).reshape(P, -1))
    f = lambda s: a["L2_ffn_" + s]
    hidden = lambda m: np.concatenate([rows_first(m.T[:, o * P:(o + 1) * P]) for o in range(8)], 0)
    t = lambda s: a["L3_ffn_" + s]
    gate_up = [np.concatenate([rows_first(gw.T), rows_first(uw.T)], 1)
               for gw, uw in list(zip(t("gate_w"), t("up_w"))) + [(t("shared_gate_w"), t("shared_up_w"))]]
    return dict(
        const=pack(CONST, CONST_N, constants()), x=a["x"], ctxT=context.reshape(B * CTX, NKP),
        WA=pack(WA, WA_N, wa), WB=pack(WB, WB_N, wb), WC=pack(WC, WC_N, wc),
        centroids=rows_first(a["L1_ffn_centroids"].T), routing_bias=a["L1_ffn_routing_bias"],
        fc=stack(list(a["L1_ffn_Wfc_r"]) + list(a["L1_ffn_Wfc_sh"])),
        pj=stack(list(a["L1_ffn_Wproj_r"]) + list(a["L1_ffn_Wproj_sh"])),
        w1=rows_first(f("w1_w").T), w2=rows_first(f("w2_w").T), w3=rows_first(f("w3_w").T), w3s=f("w3_s"),
        s2=np.concatenate([columns(f(s)) for s in ("w1_s", "w2_s", "h1_s", "h2_s")], 1),
        hh=np.concatenate([hidden(f("h1_w")), hidden(f("h2_w"))], 0),
        whh=g(t("gru_w_hh")), wih=g(t("gru_w_ih")), ctx_w=rows_first(t("ctx_w").T), ctx_b=t("ctx_b")[None],
        ew=rows_first(t("expr_w").T), gu=np.concatenate(gate_up, 0),
        dn=stack(list(t("down_w")) + [t("shared_down_w")]))


def kernel(**inputs):
    import concourse.bacc as _bacc
    from concourse.bass_utils import run_bass_kernel_spmd as _run

    nc = _bacc.Bacc("TRN2", target_bir_lowering=False, num_devices=1)
    arrays = {name: np.ascontiguousarray(m) for name, m in layouts({k: np.asarray(m) for k, m in inputs.items()}).items()}
    dram = {name: nc.dram_tensor(name, m.shape, F32, kind="ExternalInput").ap() for name, m in arrays.items()}
    out = nc.dram_tensor("out", (B, S, D), F32, kind="ExternalOutput").ap()
    build(nc, dram, out)
    return _run(nc, [arrays], core_ids=[0]).results[0]["out"]
```
